# Optimizing a Trainium2 kernel written in Bass

```python
import numpy as np
import jax
import jax.numpy as jnp

def _softmax(x, axis=-1):
    return jax.nn.softmax(x, axis=axis)

def _gelu(x):
    return jax.nn.gelu(x, approximate=True)

def _silu(x):
    return jax.nn.silu(x)

def _sigmoid(x):
    return jax.nn.sigmoid(x)

def _layernorm(x, axis=-1, eps=1e-05):
    m = jnp.mean(x, axis=axis, keepdims=True)
    v = jnp.var(x, axis=axis, keepdims=True)
    return (x - m) / jnp.sqrt(v + eps)

def _scatter_add(tgt, idx, src, axis=0):
    return tgt.at[idx].add(src)

def _segment_sum(src, seg, n):
    return jax.ops.segment_sum(src, seg, n)
kernel_name = 'mk_perceiver_d1_seqx_r4_f0b60f'

def setup_inputs(seed: int=0):
    np.random.seed(seed)
    _w = jnp.asarray

    def _rec_inputs():
        import jax
        import jax.numpy as jnp
        _rk = jax.random.key(seed)
        x = 7.22e-05 + 1 * jax.random.normal(jax.random.fold_in(_rk, 1), (64, 32, 256), jnp.float32)
        _lenS = 32 - jax.random.randint(jax.random.fold_in(_rk, 7), (64,), 0, max(1, 32 // 4) + 1, jnp.int32)
        _lenS2 = 257 - jax.random.randint(jax.random.fold_in(_rk, 8), (64,), 0, max(1, 257 // 4) + 1, jnp.int32)
        _ctx_768P = jax.random.normal(jax.random.fold_in(_rk, 11), (64, 16, 192), jnp.float32)
        _ctx_768c = jax.random.dirichlet(jax.random.fold_in(_rk, 511), 0.3 * jnp.ones((16,), jnp.float32), (64, 257))
        _ctx_768t = jnp.einsum('bsk,bkd->bsd', _ctx_768c, _ctx_768P)
        _ctx_768t = _ctx_768t * jax.lax.rsqrt(jnp.mean(jnp.square(_ctx_768t)) + 1e-12) * 0.953939
        ctx_768 = -0.000191848 + 0.999787 * (_ctx_768t + 0.3 * jax.random.normal(jax.random.fold_in(_rk, 611), (64, 257, 192), jnp.float32))
        return (x, ctx_768)
    x, ctx_768 = _rec_inputs()

    def _L0_xattn_setup():
        import jax, jax.numpy as jnp
        import numpy as np
        NUM_HEADS = 16
        CLAMP = 10000.0
        key = jax.random.key(seed)
        ks = jax.random.split(key, 8)
        B, Nq, Nkv, Cq, Ckv = (4, 512, 512, 256, 192)
        s_q = 1.0 / np.sqrt(Cq)
        s_kv = 1.0 / np.sqrt(Ckv)
        return {'query': jax.random.normal(ks[0], (B, Nq, Cq), jnp.float32), 'key_value': jax.random.normal(ks[1], (B, Nkv, Ckv), jnp.float32), 'Wq': jax.random.normal(ks[2], (Cq, Cq), jnp.float32) * s_q, 'bq': jnp.zeros((Cq,), jnp.float32), 'Wk': jax.random.normal(ks[3], (Ckv, Cq), jnp.float32) * s_kv, 'bk': jnp.zeros((Cq,), jnp.float32), 'Wv': jax.random.normal(ks[4], (Ckv, Cq), jnp.float32) * s_kv, 'bv': jnp.zeros((Cq,), jnp.float32), 'Wo': jax.random.normal(ks[5], (Cq, Cq), jnp.float32) * s_q, 'bo': jnp.zeros((Cq,), jnp.float32)}
    _L0_xattn_all = _L0_xattn_setup()
    _L0_xattn_in = {k: v for k, v in _L0_xattn_all.items() if k in ('Wq', 'bq', 'Wk', 'bk', 'Wv', 'bv', 'Wo', 'bo')}
    del _L0_xattn_all

    def _L0_attn_setup():
        import jax, jax.numpy as jnp
        import numpy as np
        B, L, D, H, E, F, STEPS, TOPK = (2, 256, 256, 16, 8, 512, 3, 2)
        HD = D // H

        def layernorm(x, g, b, eps=1e-05):
            m = jnp.mean(x, -1, keepdims=True)
            v = jnp.var(x, -1, keepdims=True)
            return (x - m) * jax.lax.rsqrt(v + eps) * g + b

        def gated_attention(x, Wqkv, Wout, Wgate):
            b, l, d = x.shape
            qkv = (x @ Wqkv).reshape(b, l, 3, H, HD)
            q, k, v = [jnp.moveaxis(qkv[:, :, i], 1, 2) for i in range(3)]
            attn = jax.nn.softmax(jnp.einsum('bhqd,bhkd->bhqk', q, k) * HD ** (-0.5), axis=-1)
            out = jnp.einsum('bhqk,bhkd->bhqd', attn, v)
            out = jnp.moveaxis(out, 1, 2).reshape(b, l, d)
            return out @ Wout * jax.nn.sigmoid(x @ Wgate)

        def ssm(x, Win, cw, cb, Wout):
            xz = x @ Win
            xs, z = jnp.split(xz, 2, axis=-1)
            xt = jnp.swapaxes(xs, 1, 2)
            y = jax.lax.conv_general_dilated(xt, cw, window_strides=(1,), padding=[(3, 0)], dimension_numbers=('NCH', 'OIH', 'NCH'), feature_group_count=D) + cb[None, :, None]
            xc = jax.nn.silu(jnp.swapaxes(y, 1, 2))
            return xc * jax.nn.sigmoid(z) @ Wout

        def moe(x, Wg, W1, W2, W3):
            b, l, d = x.shape
            flat = x.reshape(-1, d)
            probs = jax.nn.softmax(flat @ Wg, axis=-1)
            topp, topi = jax.lax.top_k(probs, TOPK)
            topp = topp / (jnp.sum(topp, -1, keepdims=True) + 1e-08)
            T = flat.shape[0]
            cw = jnp.zeros((T, E), flat.dtype).at[jnp.arange(T)[:, None], topi].add(topp)
            out = jnp.zeros_like(flat)
            for e in range(E):
                h = jax.nn.silu(flat @ W1[e]) * (flat @ W3[e])
                out = out + cw[:, e:e + 1] * (h @ W2[e])
            return out.reshape(b, l, d)
        key = jax.random.key(seed)
        ks = jax.random.split(key, 16)

        def n(k, shape, scale=0.02):
            return jax.random.normal(k, shape, jnp.float32) * scale
        return dict(x=jax.random.normal(ks[0], (B, L, D), jnp.float32), Wr=n(ks[1], (D, 2)), br=jnp.zeros((2,), jnp.float32), step_bias=jnp.zeros((STEPS,), jnp.float32), ln1_g=jnp.ones((D,), jnp.float32), ln1_b=jnp.zeros((D,), jnp.float32), ln2_g=jnp.ones((D,), jnp.float32), ln2_b=jnp.zeros((D,), jnp.float32), ls1=jnp.full((D,), 1e-05, jnp.float32), ls2=jnp.full((D,), 1e-05, jnp.float32), Wqkv=n(ks[2], (D, 3 * D)), Wout=n(ks[3], (D, D)), Wgate=n(ks[4], (D, D)), Win_ssm=n(ks[5], (D, 2 * D)), conv_w=n(ks[6], (D, 1, 4)), conv_b=jnp.zeros((D,), jnp.float32), Wout_ssm=n(ks[7], (D, D)), Wg=n(ks[8], (D, E)), W1=n(ks[9], (E, D, F)), W2=n(ks[10], (E, F, D)), W3=n(ks[11], (E, D, F)))
    _L0_attn_all = _L0_attn_setup()
    _L0_attn_in = {k: v for k, v in _L0_attn_all.items() if k in ('Wr', 'br', 'step_bias', 'ln1_g', 'ln1_b', 'ln2_g', 'ln2_b', 'ls1', 'ls2', 'Wqkv', 'Wout', 'Wgate', 'Win_ssm', 'conv_w', 'conv_b', 'Wout_ssm', 'Wg', 'W1', 'W2', 'W3')}
    del _L0_attn_all

    def _L0_ffn_setup():
        import jax, jax.numpy as jnp
        import numpy as np
        E = 8
        K = 2
        CAP_FACTOR = 1.0
        key = jax.random.key(seed)
        ks = jax.random.split(key, 5)
        B, T, C, H = (4, 512, 256, 1024)
        x = jax.random.normal(ks[0], (B, T, C), dtype=jnp.float32)
        Wr = jax.random.normal(ks[1], (C, E), dtype=jnp.float32) * 0.02
        br = jnp.zeros((E,), jnp.float32)
        W1 = jax.random.normal(ks[2], (E, C, H), dtype=jnp.float32) * 0.02
        b1 = jnp.zeros((E, H), jnp.float32)
        W2 = jax.random.normal(ks[3], (E, H, C), dtype=jnp.float32) * 0.02
        b2 = jnp.zeros((E, C), jnp.float32)
        return {'x': x, 'Wr': Wr, 'br': br, 'W1': W1, 'b1': b1, 'W2': W2, 'b2': b2}
    _L0_ffn_all = _L0_ffn_setup()
    _L0_ffn_in = {k: v for k, v in _L0_ffn_all.items() if k in ('Wr', 'br', 'W1', 'b1', 'W2', 'b2')}
    del _L0_ffn_all
    return {'x': x, 'ctx_768': ctx_768, 'L0_xattn_Wq': _L0_xattn_in['Wq'], 'L0_xattn_bq': _L0_xattn_in['bq'], 'L0_xattn_Wk': _L0_xattn_in['Wk'], 'L0_xattn_bk': _L0_xattn_in['bk'], 'L0_xattn_Wv': _L0_xattn_in['Wv'], 'L0_xattn_bv': _L0_xattn_in['bv'], 'L0_xattn_Wo': _L0_xattn_in['Wo'], 'L0_xattn_bo': _L0_xattn_in['bo'], 'L0_attn_Wr': _L0_attn_in['Wr'], 'L0_attn_br': _L0_attn_in['br'], 'L0_attn_step_bias': _L0_attn_in['step_bias'], 'L0_attn_ln1_g': _L0_attn_in['ln1_g'], 'L0_attn_ln1_b': _L0_attn_in['ln1_b'], 'L0_attn_ln2_g': _L0_attn_in['ln2_g'], 'L0_attn_ln2_b': _L0_attn_in['ln2_b'], 'L0_attn_ls1': _L0_attn_in['ls1'], 'L0_attn_ls2': _L0_attn_in['ls2'], 'L0_attn_Wqkv': _L0_attn_in['Wqkv'], 'L0_attn_Wout': _L0_attn_in['Wout'], 'L0_attn_Wgate': _L0_attn_in['Wgate'], 'L0_attn_Win_ssm': _L0_attn_in['Win_ssm'], 'L0_attn_conv_w': _L0_attn_in['conv_w'], 'L0_attn_conv_b': _L0_attn_in['conv_b'], 'L0_attn_Wout_ssm': _L0_attn_in['Wout_ssm'], 'L0_attn_Wg': _L0_attn_in['Wg'], 'L0_attn_W1': _L0_attn_in['W1'], 'L0_attn_W2': _L0_attn_in['W2'], 'L0_attn_W3': _L0_attn_in['W3'], 'L0_ffn_Wr': _L0_ffn_in['Wr'], 'L0_ffn_br': _L0_ffn_in['br'], 'L0_ffn_W1': _L0_ffn_in['W1'], 'L0_ffn_b1': _L0_ffn_in['b1'], 'L0_ffn_W2': _L0_ffn_in['W2'], 'L0_ffn_b2': _L0_ffn_in['b2']}

def reference(x, ctx_768, L0_xattn_Wq, L0_xattn_bq, L0_xattn_Wk, L0_xattn_bk, L0_xattn_Wv, L0_xattn_bv, L0_xattn_Wo, L0_xattn_bo, L0_attn_Wr, L0_attn_br, L0_attn_step_bias, L0_attn_ln1_g, L0_attn_ln1_b, L0_attn_ln2_g, L0_attn_ln2_b, L0_attn_ls1, L0_attn_ls2, L0_attn_Wqkv, L0_attn_Wout, L0_attn_Wgate, L0_attn_Win_ssm, L0_attn_conv_w, L0_attn_conv_b, L0_attn_Wout_ssm, L0_attn_Wg, L0_attn_W1, L0_attn_W2, L0_attn_W3, L0_ffn_Wr, L0_ffn_br, L0_ffn_W1, L0_ffn_b1, L0_ffn_W2, L0_ffn_b2):
    import jax
    import jax.numpy as jnp

    def _L0_xattn_ref(query, key_value, Wq, bq, Wk, bk, Wv, bv, Wo, bo):
        import jax, jax.numpy as jnp
        import numpy as np
        NUM_HEADS = 16
        CLAMP = 10000.0
        B, Nq, Cq = query.shape
        Nkv = key_value.shape[1]
        H = NUM_HEADS
        D = Cq // H
        scale = D ** (-0.5)
        q = (query @ Wq + bq).reshape(B, Nq, H, D).transpose(0, 2, 1, 3)
        k = (key_value @ Wk + bk).reshape(B, Nkv, H, D).transpose(0, 2, 1, 3)
        v = (key_value @ Wv + bv).reshape(B, Nkv, H, D).transpose(0, 2, 1, 3)
        attn = jnp.einsum('bhqd,bhkd->bhqk', q, k) * scale
        attn = jnp.clip(attn, -CLAMP, CLAMP)
        attn = jax.nn.softmax(attn, axis=-1)
        attn = jnp.where(jnp.any(jnp.isnan(attn)), jnp.asarray(1.0 / Nkv, attn.dtype), attn)
        x = jnp.einsum('bhqk,bhkd->bqhd', attn, v).reshape(B, Nq, Cq)
        return x @ Wo + bo

    def _L0_attn_ref(x, Wr, br, step_bias, ln1_g, ln1_b, ln2_g, ln2_b, ls1, ls2, Wqkv, Wout, Wgate, Win_ssm, conv_w, conv_b, Wout_ssm, Wg, W1, W2, W3):
        import jax, jax.numpy as jnp
        import numpy as np
        B, L, D, H, E, F, STEPS, TOPK = (2, 256, 256, 16, 8, 512, 3, 2)
        HD = D // H

        def layernorm(x, g, b, eps=1e-05):
            m = jnp.mean(x, -1, keepdims=True)
            v = jnp.var(x, -1, keepdims=True)
            return (x - m) * jax.lax.rsqrt(v + eps) * g + b

        def gated_attention(x, Wqkv, Wout, Wgate):
            b, l, d = x.shape
            qkv = (x @ Wqkv).reshape(b, l, 3, H, HD)
            q, k, v = [jnp.moveaxis(qkv[:, :, i], 1, 2) for i in range(3)]
            attn = jax.nn.softmax(jnp.einsum('bhqd,bhkd->bhqk', q, k) * HD ** (-0.5), axis=-1)
            out = jnp.einsum('bhqk,bhkd->bhqd', attn, v)
            out = jnp.moveaxis(out, 1, 2).reshape(b, l, d)
            return out @ Wout * jax.nn.sigmoid(x @ Wgate)

        def ssm(x, Win, cw, cb, Wout):
            xz = x @ Win
            xs, z = jnp.split(xz, 2, axis=-1)
            xt = jnp.swapaxes(xs, 1, 2)
            y = jax.lax.conv_general_dilated(xt, cw, window_strides=(1,), padding=[(3, 0)], dimension_numbers=('NCH', 'OIH', 'NCH'), feature_group_count=D) + cb[None, :, None]
            xc = jax.nn.silu(jnp.swapaxes(y, 1, 2))
            return xc * jax.nn.sigmoid(z) @ Wout

        def moe(x, Wg, W1, W2, W3):
            b, l, d = x.shape
            flat = x.reshape(-1, d)
            probs = jax.nn.softmax(flat @ Wg, axis=-1)
            topp, topi = jax.lax.top_k(probs, TOPK)
            topp = topp / (jnp.sum(topp, -1, keepdims=True) + 1e-08)
            T = flat.shape[0]
            cw = jnp.zeros((T, E), flat.dtype).at[jnp.arange(T)[:, None], topi].add(topp)
            out = jnp.zeros_like(flat)
            for e in range(E):
                h = jax.nn.silu(flat @ W1[e]) * (flat @ W3[e])
                out = out + cw[:, e:e + 1] * (h @ W2[e])
            return out.reshape(b, l, d)
        accumulated = jnp.zeros_like(x)
        remainder = jnp.ones(x.shape[:2] + (1,), x.dtype)
        for step in range(STEPS):
            normed = layernorm(x, ln1_g, ln1_b)
            r = normed @ Wr + br
            alpha = jax.nn.sigmoid(r[..., 0:1])
            halt = jax.nn.sigmoid(r[..., 1:2] + step_bias[step])
            ssm_out = ssm(normed, Win_ssm, conv_w, conv_b, Wout_ssm)
            attn_out = gated_attention(normed, Wqkv, Wout, Wgate)
            blended = ls1 * ((1 - alpha) * ssm_out + alpha * attn_out)
            moe_out = moe(layernorm(x + blended, ln2_g, ln2_b), Wg, W1, W2, W3)
            step_output = x + blended + ls2 * moe_out
            weight = remainder if step == STEPS - 1 else halt * remainder
            accumulated = accumulated + weight * step_output
            remainder = jnp.clip(remainder - weight, 0.0, None)
        return accumulated + x

    def _L0_ffn_ref(x, Wr, br, W1, b1, W2, b2):
        import jax, jax.numpy as jnp
        import numpy as np
        E = 8
        K = 2
        CAP_FACTOR = 1.0
        B, T, C = x.shape
        N = B * T
        xf = x.reshape(N, C)
        logits = xf @ Wr + br
        topv, topi = jax.lax.top_k(logits, K)
        gates = jax.nn.softmax(topv, axis=-1)
        rw = jnp.zeros((N, E), xf.dtype).at[jnp.arange(N)[:, None], topi].set(gates)
        cap = int(N * K / E * CAP_FACTOR)
        sel = jax.nn.one_hot(topi, E, dtype=jnp.int32).sum(1)
        rank = jnp.cumsum(sel, axis=0) - sel
        keep = (sel > 0) & (rank < cap)
        tok = jnp.broadcast_to(jnp.arange(N, dtype=jnp.int32)[:, None], (N, E))
        eid = jnp.broadcast_to(jnp.arange(E, dtype=jnp.int32)[None, :], (N, E))
        rank_c = jnp.where(keep, rank, cap)
        buf = jnp.full((E, cap), N, dtype=jnp.int32)
        buf = buf.at[eid, rank_c].set(tok, mode='drop')
        xpad = jnp.concatenate([xf, jnp.zeros((1, C), xf.dtype)], axis=0)
        xg = xpad[buf]
        h = jax.nn.gelu(jnp.einsum('ecd,edh->ech', xg, W1) + b1[:, None, :], approximate=False)
        out = jnp.einsum('ech,ehd->ecd', h, W2) + b2[:, None, :]
        rw_pad = jnp.concatenate([rw, jnp.zeros((1, E), rw.dtype)], axis=0)
        w = rw_pad[buf, jnp.arange(E, dtype=jnp.int32)[:, None]]
        weighted = out * w[..., None]
        final = jnp.zeros((N + 1, C), xf.dtype).at[buf.reshape(-1)].add(weighted.reshape(-1, C))
        return final[:N].reshape(B, T, C)
    x = x + _L0_xattn_ref(_layernorm(x, axis=-1), ctx_768, L0_xattn_Wq, L0_xattn_bq, L0_xattn_Wk, L0_xattn_bk, L0_xattn_Wv, L0_xattn_bv, L0_xattn_Wo, L0_xattn_bo)
    x = x + _L0_attn_ref(_layernorm(x, axis=-1), L0_attn_Wr, L0_attn_br, L0_attn_step_bias, L0_attn_ln1_g, L0_attn_ln1_b, L0_attn_ln2_g, L0_attn_ln2_b, L0_attn_ls1, L0_attn_ls2, L0_attn_Wqkv, L0_attn_Wout, L0_attn_Wgate, L0_attn_Win_ssm, L0_attn_conv_w, L0_attn_conv_b, L0_attn_Wout_ssm, L0_attn_Wg, L0_attn_W1, L0_attn_W2, L0_attn_W3)
    x = x + _L0_ffn_ref(_layernorm(x, axis=-1), L0_ffn_Wr, L0_ffn_br, L0_ffn_W1, L0_ffn_b1, L0_ffn_W2, L0_ffn_b2)
    return x

_drawn_inputs = setup_inputs


def setup_inputs(seed=0):
    import zlib

    import numpy as np

    out = dict(_drawn_inputs(seed))
    spreads = {'L0_xattn_bq': (0.0, 0.393),
     'L0_xattn_bk': (0.0, 2.0),
     'L0_xattn_bv': (0.0, 0.1),
     'L0_xattn_bo': (0.0, 0.1),
     'L0_attn_br': (0.0, 2.0),
     'L0_attn_step_bias': (0.0, 2.0),
     'L0_attn_ln1_g': (1.0, 0.6),
     'L0_attn_ln1_b': (0.0, 2.0),
     'L0_attn_ln2_g': (1.0, 0.6),
     'L0_attn_ln2_b': (0.0, 2.0),
     'L0_attn_ls1': (9.999999747378752e-06, 0.6),
     'L0_attn_ls2': (9.999999747378752e-06, 0.6),
     'L0_attn_conv_b': (0.0, 2.0),
     'L0_ffn_br': (0.0, 0.319),
     'L0_ffn_b1': (0.0, 0.8),
     'L0_ffn_b2': (0.0, 0.42)}
    factors = {'L0_attn_Wr': 200.0,
     'L0_attn_Wqkv': 200.0,
     'L0_attn_Wout': 200.0,
     'L0_attn_Wgate': 200.0,
     'L0_attn_Win_ssm': 200.0,
     'L0_attn_conv_w': 200.0,
     'L0_attn_Wout_ssm': 176.793,
     'L0_attn_Wg': 64.0,
     'L0_attn_W1': 64.0,
     'L0_attn_W2': 64.0,
     'L0_attn_W3': 64.0,
     'L0_ffn_W1': 2.7}
    for name, (base, spread) in spreads.items():
        noise = np.random.default_rng([zlib.crc32(name.encode()), seed]).standard_normal(out[name].shape)
        drawn = base * np.exp(spread * noise) if base else spread * noise
        out[name] = jnp.asarray(drawn.astype(out[name].dtype))
    for name, factor in factors.items():
        out[name] = (out[name] * factor).astype(out[name].dtype)
    return out
```

```python
from contextlib import ExitStack

import numpy as np
import concourse.bass as bass
from concourse import mybir

F32 = mybir.dt.float32
I32 = mybir.dt.int32
U32 = mybir.dt.uint32
ALU = mybir.AluOpType
ACT = mybir.ActivationFunctionType
AXX = mybir.AxisListType.X

P = 128
B, L, D = 64, 32, 256
S, DC = 257, 192
H, HD = 16, 16
N = B * L
T = N // P
SM = 2 * P
G = 4
CLAMP = 10000.0
SCALE = HD ** -0.5
EPS = 1e-5


class Mem:

    def __init__(self, nc, st, clear=False):
        self.nc, self.st, self.sems = nc, st, []
        if clear:
            st.callback(self.clear)

    def clear(self):
        self.nc.clear_and_free_semaphores(self.sems)
        self.nc.all_engine_barrier()

    def sb(self, name, shape, dt=F32):
        return self.st.enter_context(self.nc.sbuf_tensor(name, shape, dt))

    def ps(self, name, shape, dt=F32):
        return self.st.enter_context(self.nc.psum_tensor(name, shape, dt))

    def sem(self, name):
        self.sems.append(self.nc.alloc_semaphore(name))
        return self.sems[-1]


def rsqrt_refined(dve, act_var, rt, r, t, sem, n0, var):
    dve.reciprocal(r, rt).then_inc(sem, 1)
    dve.wait_ge(sem, n0 + 1)
    dve.tensor_tensor(t, r, r, ALU.mult).then_inc(sem, 1)
    dve.wait_ge(sem, n0 + 2)
    dve.tensor_tensor(t, t, var, ALU.mult).then_inc(sem, 1)
    dve.wait_ge(sem, n0 + 3)
    dve.tensor_scalar(t, t, -0.5, 1.5, ALU.mult, ALU.add).then_inc(sem, 1)
    dve.wait_ge(sem, n0 + 4)
    dve.tensor_tensor(r, r, t, ALU.mult).then_inc(sem, 1)
    dve.wait_ge(sem, n0 + 5)


def query_phase(nc, io, m, xs, qT):
    with ExitStack() as st:
        p = Mem(nc, st)
        ident = p.sb("qa_ident", [P, P])
        wq = p.sb("qa_wq", [P, 2, D])
        bq = p.sb("qa_bq", [P, 2])
        stats = p.sb("qa_stats", [P, T, 6])
        mv = p.sb("qa_mv", [P, T, 2])
        ve = p.sb("qa_ve", [P, T])
        rt = p.sb("qa_rt", [P, T])
        rs = p.sb("qa_rs", [P, T])
        tmp = p.sb("qa_tmp", [P, T])
        xn = p.sb("qa_xn", [P, 4, D])
        xnT = p.sb("qa_xnT", [P, 2, 4 * P])
        tp = p.ps("qa_tp", [P, 2, 4 * P])
        qp = p.ps("qa_qp", [P, 2, 4 * P])
        x_loaded = p.sem("qa_x_loaded")
        w_loaded = p.sem("qa_w_loaded")
        step = p.sem("qa_step")
        var_ready = p.sem("qa_var_ready")
        sqrt_ready = p.sem("qa_sqrt_ready")
        xn_ready = p.sem("qa_xn_ready")
        tp_ready = p.sem("qa_tp_ready")
        xnT_ready = p.sem("qa_xnT_ready")
        qp_ready = p.sem("qa_qp_ready")
        q_stored = p.sem("qa_q_stored")
        block = st.enter_context(nc.Block())

        @block.sync
        def _(sp):
            for c in range(4):
                sp.dma_start(xs[:, 4 * c:4 * c + 4, :],
                             io["x"].rearrange("(t p) d -> p t d", p=P)[:, 4 * c:4 * c + 4, :]).then_inc(x_loaded, 16)
            sp.dma_start(wq[:], io["Wq"].rearrange("(k p) m -> p k m", p=P)).then_inc(w_loaded, 16)
            sp.dma_start(bq[:], io["bq"]).then_inc(w_loaded, 16)
            sp.dma_start(ident[:], io["c_ident"]).then_inc(w_loaded, 16)

        @block.vector
        def _(dve):
            dve.wait_ge(x_loaded, 64)
            for t in range(T):
                dve.bn_stats(stats[:, t, :], xs[:, t, :]).then_inc(step, 1)
            for t in range(T):
                dve.wait_ge(step, t + 1)
                dve.bn_aggr(mv[:, t, :], stats[:, t, :]).then_inc(step, 1)
            dve.wait_ge(step, 2 * T)
            dve.tensor_scalar(ve[:], mv[:, :, 1], EPS, None, ALU.add).then_inc(var_ready, 1)
            dve.wait_ge(sqrt_ready, 1)
            rsqrt_refined(dve, None, rt[:], rs[:], tmp[:], step, 2 * T, ve[:])
            for c in range(4):
                for j in range(4):
                    t = 4 * c + j
                    if c:
                        dve.wait_ge(tp_ready, 2 * c)
                    dve.tensor_scalar(xn[:, j, :], xs[:, t, :], mv[:, t, 0:1], rs[:, t:t + 1],
                                      ALU.subtract, ALU.mult).then_inc(xn_ready, 1)
                if c:
                    dve.wait_ge(qp_ready, 2 * c)
                for k in range(2):
                    dve.wait_ge(tp_ready, 2 * c + k + 1)
                    dve.tensor_copy(xnT[:, k, :], tp[:, k, :]).then_inc(xnT_ready, 1)

        @block.scalar
        def _(act):
            act.wait_ge(var_ready, 1)
            act.activation(rt[:], ve[:], ACT.Sqrt).then_inc(sqrt_ready, 1)
            act.wait_ge(w_loaded, 48)
            for c in range(4):
                for h in range(2):
                    act.wait_ge(qp_ready, 2 * c + h + 1)
                    act.activation(qT[:, h, 512 * c:512 * c + 512], qp[:, h, :], ACT.Identity,
                                   bias=bq[:, h:h + 1]).then_inc(q_stored, 1)

        @block.tensor
        def _(pe):
            pe.wait_ge(w_loaded, 48)
            for c in range(4):
                if c:
                    pe.wait_ge(xnT_ready, 2 * c)
                pe.wait_ge(xn_ready, 4 * c + 4)
                for k in range(2):
                    for j in range(4):
                        mm = pe.transpose(tp[:, k, P * j:P * j + P], xn[:, j, P * k:P * k + P], ident[:])
                    mm.then_inc(tp_ready, 1)
                pe.wait_ge(xnT_ready, 2 * c + 2)
                if c:
                    pe.wait_ge(q_stored, 2 * c)
                for h in range(2):
                    for k in range(2):
                        mm = pe.matmul(qp[:, h, :], wq[:, k, P * h:P * h + P], xnT[:, k, :],
                                       start=(k == 0), stop=(k == 1))
                    mm.then_inc(qp_ready, 1)


def cross_attention_phase(nc, io, m, qT, oT, rawsum, csum, zero_slots, zeroed):
    with ExitStack() as st:
        p = Mem(nc, st, clear=True)
        ident = p.sb("xa_ident", [P, P])
        zero = p.sb("xa_zero", [P, 1, D])
        istack = p.sb("xa_istack", [P, L])
        mask8 = p.sb("xa_mask8", [P, 8])
        mask64 = p.sb("xa_mask64", [P, 64])
        wk = p.sb("xa_wk", [P, 2, D])
        wv = p.sb("xa_wv", [P, 2, D])
        bk = p.sb("xa_bk", [P, 2])
        floor = p.sb("xa_floor", [P, 1])
        cl = p.sb("xa_cl", [P, 2, B])
        vl = p.sb("xa_vl", [B, D])
        vlast = p.sb("xa_vlast", [G, B, G * 65])
        ctx = p.sb("xa_ctx", [P, 2, 2, 2, S])
        kT = p.sb("xa_kT", [P, 2, 2, S])
        v = p.sb("xa_v", [P, 2, 2, G, 65])
        qbd = p.sb("xa_qbd", [P, 2, G, P])
        mx = p.sb("xa_mx", [P, 2, G])
        nm = p.sb("xa_nm", [P, 2, G])
        low = p.sb("xa_low", [P, 2, G])
        pr = p.sb("xa_pr", [P, 2, G, S])
        pT = p.sb("xa_pT", [P, 2, G, 2, P])
        pTl = p.sb("xa_pTl", [G, 2, P])
        unused = p.sb("xa_unused", [P, 2, S])
        rinv = p.sb("xa_rinv", [P, 2, G])
        om = p.sb("xa_om", [P, 2, D])
        on = p.sb("xa_on", [P, 2, D])
        kvp = p.ps("xa_kvp", [P, 2, 512])
        sc = p.ps("xa_sc", [P, G, 512])
        ptp = p.ps("xa_ptp", [P, 512])
        ob = p.ps("xa_ob", [P, 512])
        OT, PL = 260, 324

        w_loaded = p.sem("xa_w_loaded")
        cl_loaded = p.sem("xa_cl_loaded")
        zero_set = p.sem("xa_zero_set")
        ctx_loaded = [p.sem(f"xa_ctx_loaded{i}") for i in range(2)]
        vlp_ready = p.sem("xa_vlp_ready")
        vl_ready = p.sem("xa_vl_ready")
        vlast_loaded = p.sem("xa_vlast_loaded")
        vlast_ready = p.sem("xa_vlast_ready")
        ones_ready = p.sem("xa_ones_ready")
        floor_ready = p.sem("xa_floor_ready")
        kp_ready = p.sem("xa_kp_ready")
        k_ready = p.sem("xa_k_ready")
        vp_ready = p.sem("xa_vp_ready")
        v_ready = p.sem("xa_v_ready")
        q_ready = p.sem("xa_q_ready")
        s_ready = p.sem("xa_s_ready")
        mx_step = p.sem("xa_mx_step")
        nm_ready = p.sem("xa_nm_ready")
        exp_ready = p.sem("xa_exp_ready")
        low_ready = p.sem("xa_low_ready")
        pr_ready = p.sem("xa_pr_ready")
        ptp_ready = p.sem("xa_ptp_ready")
        plp_ready = p.sem("xa_plp_ready")
        pT_ready = p.sem("xa_pT_ready")
        pTl_ready = p.sem("xa_pTl_ready")
        o_ready = p.sem("xa_o_ready")
        rinv_ready = p.sem("xa_rinv_ready")
        om_ready = p.sem("xa_om_ready")
        on_ready = p.sem("xa_on_ready")
        oTp_ready = p.sem("xa_oTp_ready")
        oT_stored = p.sem("xa_oT_stored")
        csum_ready = p.sem("xa_csum_ready")
        block = st.enter_context(nc.Block())

        def run_steps(eng, step, first, last):
            for b in range(first, 4):
                step(b, b % 2, b // 2)
            with eng.Fori(1, B // 4 - 1) as i:
                for j in range(4):
                    step(i * 4 + j, j % 2, j // 2)
            for b in range(B - 4, last):
                step(b, b % 2, b // 2 % 2)

        @block.sync
        def _(sp):
            for dst, name in ((wk, "Wk"), (wv, "Wv")):
                sp.dma_start(dst[:, 0, :], io[name][0:P, :]).then_inc(w_loaded, 16)
                sp.dma_start(dst[0:64, 1, :], io[name][P:DC, :]).then_inc(w_loaded, 16)
            sp.dma_start(bk[:], io["bk"]).then_inc(w_loaded, 16)
            sp.dma_start(ident[:], io["c_ident"]).then_inc(w_loaded, 16)
            sp.dma_start(istack[:], io["c_istack"]).then_inc(w_loaded, 16)
            sp.dma_start(mask8[:], io["c_mask8s"]).then_inc(w_loaded, 16)
            sp.dma_start(mask64[:], io["c_mask64"]).then_inc(w_loaded, 16)
            sp.dma_start(cl[:, 0, :], io["ctx_last"][0:P, :]).then_inc(cl_loaded, 16)
            sp.dma_start(cl[0:64, 1, :], io["ctx_last"][P:DC, :]).then_inc(cl_loaded, 16)

            def load(i, slot):
                sp.dma_start(ctx[:, slot, 0, :, :], io["ctxT"][0:P, bass.ds(i * 2, 2), :]).then_inc(ctx_loaded[slot], 16)
                sp.dma_start(ctx[0:64, slot, 1, :, :],
                             io["ctxT"][P:DC, bass.ds(i * 2, 2), :]).then_inc(ctx_loaded[slot], 16)

            load(0, 0)
            load(1, 1)
            sp.dma_start(vlast[:], io["c_vlast"]).then_inc(vlast_loaded, 16)
            sp.wait_ge(vl_ready, 1)
            sp.wait_ge(vlast_loaded, 16)
            for g in range(G):
                sp.dma_start(vlast[g:g + 1, :, 65 * g:65 * g + 64],
                             vl[:, 64 * g:64 * g + 64]).then_inc(vlast_ready, 16)
            sp.wait_ge(zero_set, 1)
            zero_slots(sp, zero)
            with sp.Fori(1, B // 4) as i:
                for j in range(2):
                    sp.wait_ge(vp_ready, i * 4 + (2 * j - 2))
                    sp.wait_ge(csum_ready, i * 8 + (4 * j - 4))
                    load(i * 2 + j, j)
            sp.wait_ge(*zeroed)

        @block.tensor
        def _(pe):
            pe.wait_ge(w_loaded, 16 * 9)
            pe.wait_ge(cl_loaded, 32)
            pe.matmul(ptp[0:B, 0:D], cl[:, 0, :], wv[:, 0, :], start=True, stop=False)
            pe.matmul(ptp[0:B, 0:D], cl[0:64, 1, :], wv[0:64, 1, :], start=False, stop=True).then_inc(vlp_ready, 1)

            def project_k(b, par, slot):
                for h in range(2):
                    if h == 0:
                        pe.wait_ge(k_ready, b * 2)
                    else:
                        pe.wait_ge(v_ready, b)
                    for k, rows in ((0, P), (1, 64)):
                        mm = pe.matmul(kvp[:, (par + h) % 2, 0:S], wk[0:rows, k, P * h:P * h + P],
                                       ctx[0:rows, slot, k, par, :], start=(k == 0), stop=(k == 1))
                    mm.then_inc(kp_ready, 1)

            def project_v(b, par, slot, tiles):
                pe.wait_ge(k_ready, b * 2 + 1)
                for t in tiles:
                    for k, rows in ((0, P), (1, 64)):
                        mm = pe.matmul(kvp[:, par, D * t:D * t + D], ctx[0:rows, slot, k, par, P * t:P * t + P],
                                       wv[0:rows, k, :], start=(k == 0), stop=(k == 1))
                if t == 1:
                    mm.then_inc(vp_ready, 1)

            def scores(b, par):
                pe.wait_ge(q_ready, b + 1)
                for h in range(2):
                    pe.wait_ge(k_ready, b * 2 + h + 1)
                    if not (isinstance(b, int) and b == 0):
                        pe.wait_ge(exp_ready, b * 4 + (2 * h - 2))
                    for g in (2 * h, 2 * h + 1):
                        mm = pe.matmul(sc[:, g, 0:S], qbd[:, par, g, :], kT[:, par, h, :], start=True, stop=True)
                    mm.then_inc(s_ready, 1)

            def turn(b, par, h):
                pe.wait_ge(pr_ready, b * 4 + (2 * h + 2))
                if h == 1:
                    if not (isinstance(b, int) and b == 0):
                        pe.wait_ge(om_ready, b)
                    pe.transpose(ob[0:G, PL:PL + P], pr[:, par, :, S - 1], ident[:]).then_inc(plp_ready, 1)
                pe.wait_ge(pT_ready, b * 2 + h)
                for g in (2 * h, 2 * h + 1):
                    for t in range(2):
                        c = (2 * (g % 2) + t) * P
                        mm = pe.transpose(ptp[:, c:c + P], pr[:, par, g, P * t:P * t + P], ident[:])
                mm.then_inc(ptp_ready, 1)

            def values(b, par):
                pe.wait_ge(pTl_ready, b + 1)
                pe.wait_ge(v_ready, b + 1)
                if not (isinstance(b, int) and b == 0):
                    pe.wait_ge(oT_stored, b)
                pe.matmul(ob[:, 0:G * 65], pTl[:, par, :], vlast[:, b, :], start=True, stop=False, skip_group_check=True)
                pe.wait_ge(pT_ready, b * 2 + 2)
                for g in range(G):
                    for t in range(2):
                        mm = pe.matmul(ob[:, 65 * g:65 * g + 65], pT[:, par, g, t, :], v[:, par, t, g, :],
                                       start=False, stop=(g == G - 1 and t == 1), skip_group_check=True)
                mm.then_inc(o_ready, 1)

            def turn_output(b, par):
                pe.wait_ge(on_ready, b + 1)
                if not (isinstance(b, int) and b == B - 1):
                    pe.wait_ge(pTl_ready, b + 2)
                for h in range(2):
                    mm = pe.matmul(ob[:, OT + L * h:OT + L * h + L], on[:, par, P * h:P * h + P], istack[:],
                                   start=True, stop=True, skip_group_check=True)
                mm.then_inc(oTp_ready, 1)

            def step(b, par, slot):
                static = isinstance(b, int)
                scores(b, par)
                if not static or b >= 1:
                    turn(b - 1, 1 - par, 0)
                if not static or b < B - 1:
                    nslot = slot if par == 0 else 1 - slot
                    if par == 1:
                        loaded(b + 1, nslot)
                    project_k(b + 1, 1 - par, nslot)
                if not static or b >= 1:
                    turn(b - 1, 1 - par, 1)
                if not static or b < B - 1:
                    project_v(b + 1, 1 - par, nslot, (0,))
                if not static or b >= 2:
                    turn_output(b - 2, par)
                if not static or b < B - 1:
                    project_v(b + 1, 1 - par, nslot, (1,))
                if not static or b >= 1:
                    values(b - 1, 1 - par)

            def loaded(b, slot):
                if isinstance(b, int):
                    pe.wait_ge(ctx_loaded[slot], 32 * (b // 4 + 1))
                else:
                    pe.wait_ge(ctx_loaded[slot], b * 8 + (32 if slot == 0 else 16))

            loaded(0, 0)
            project_k(0, 0, 0)
            pe.wait_ge(vlast_ready, 64)
            project_v(0, 0, 0, (0, 1))
            for b in range(4):
                step(b, b % 2, b // 2 % 2)
            with pe.Fori(1, B // 4 - 1) as i:
                for j in range(4):
                    step(i * 4 + j, j % 2, j // 2)
            for b in range(B - 4, B):
                step(b, b % 2, b // 2 % 2)
            turn(B - 1, 1, 0)
            turn(B - 1, 1, 1)
            turn_output(B - 2, 0)
            values(B - 1, 1)
            turn_output(B - 1, 1)

        @block.gpsimd
        def _(pool):
            pool.memset(floor[:], -CLAMP).then_inc(floor_ready, 1)
            pool.memset(zero[:], 0.0).then_inc(zero_set, 1)
            for par in range(2):
                pool.memset(v[:, par, :, :, 64], 1.0).then_inc(ones_ready, 1)
            pool.wait_ge(w_loaded, 16 * 9)

            def queries(b, par):
                if not (isinstance(b, int) and b < 2):
                    pool.wait_ge(s_ready, b * 2 - 2)
                src = qT[:, :, bass.ds(b * L, L)].unsqueeze(2).to_broadcast([P, 2, 8, L])
                msk = mask8[:].unsqueeze(1).unsqueeze(3).to_broadcast([P, 2, 8, L])
                dst = qbd[:, par].rearrange("p (h j) (e q) -> p h (j e) q", h=2, q=L)
                pool.tensor_tensor(dst, src, msk, ALU.mult).then_inc(q_ready, 1)

            def normalise(b, par):
                pool.wait_ge(rinv_ready, b + 1)
                pool.wait_ge(om_ready, b + 1)
                if not (isinstance(b, int) and b < 2):
                    pool.wait_ge(oTp_ready, b - 1)
                pool.tensor_tensor(on[:, par, :].rearrange("p (g c) -> p g c", g=G),
                                   om[:, par, :].rearrange("p (g c) -> p g c", g=G),
                                   rinv[:, par, :].unsqueeze(2).to_broadcast([P, G, 64]),
                                   ALU.mult).then_inc(on_ready, 1)

            def step(b, par, slot):
                static = isinstance(b, int)
                if not static or b < B - 1:
                    queries(b + 1, 1 - par)
                if not static or b >= 2:
                    normalise(b - 2, par)

            queries(0, 0)
            run_steps(pool, step, 0, B)
            normalise(B - 2, 0)
            normalise(B - 1, 1)

        @block.scalar
        def _(act):
            act.wait_ge(w_loaded, 16 * 9)
            act.wait_ge(floor_ready, 1)

            def store_k(b, par, h):
                if not (isinstance(b, int) and b < 2):
                    act.wait_ge(s_ready, b * 2 - 2)
                act.wait_ge(kp_ready, b * 2 + h + 1)
                act.activation(kT[:, par, h, :], kvp[:, (par + h) % 2, 0:S], ACT.Identity,
                               bias=bk[:, h:h + 1]).then_inc(k_ready, 1)

            def sum_context(b, par, slot):
                for k, rows in ((0, P), (1, 64)):
                    act.activation(unused[0:rows, k, :], ctx[0:rows, slot, k, par, :], ACT.Copy,
                                   accum_out=csum[0:rows, k, bass.ds(b, 1)]).then_inc(csum_ready, 1)

            def exponentials(b, par, h):
                act.wait_ge(nm_ready, b * 2 + h + 1)
                if h == 0 and not (isinstance(b, int) and b < 2):
                    act.wait_ge(plp_ready, b - 1)
                    act.wait_ge(pr_ready, b * 4 - 4)
                act.activation(low[:, par, 2 * h:2 * h + 2], nm[:, par, 2 * h:2 * h + 2], ACT.Exp,
                               bias=floor[:]).then_inc(low_ready, 1)
                for g in (2 * h, 2 * h + 1):
                    act.activation(pr[:, par, g, :], sc[:, g, 0:S], ACT.Exp, bias=nm[:, par, g:g + 1],
                                   scale=-1.0, accum_out=rawsum[:, bass.ds(b * G + g, 1)]).then_inc(exp_ready, 1)

            def step(b, par, slot):
                static = isinstance(b, int)
                for h in range(2):
                    exponentials(b, par, h)
                    if not static or b < B - 1:
                        store_k(b + 1, 1 - par, h)
                if not (static and b == 0):
                    act.wait_ge(csum_ready, b * 2)
                sum_context(b, par, slot)

            store_k(0, 0, 0)
            store_k(0, 0, 1)
            run_steps(act, step, 0, B)

        @block.vector
        def _(dve):
            dve.wait_ge(w_loaded, 16 * 9)
            dve.wait_ge(ones_ready, 2)
            dve.wait_ge(vlp_ready, 1)
            dve.tensor_copy(vl[:], ptp[0:B, 0:D]).then_inc(vl_ready, 1)

            def store_v(b, par):
                dve.wait_ge(vp_ready, b + 1)
                if not (isinstance(b, int) and b < 2):
                    dve.wait_ge(o_ready, b - 1)
                dve.tensor_copy(v[:, par, :, :, 0:64], kvp[:, par, :].rearrange("p (t g c) -> p t g c", t=2, g=G)
                                ).then_inc(v_ready, 1)

            def maxima(b, par, h):
                g = slice(2 * h, 2 * h + 2)
                dve.wait_ge(s_ready, b * 2 + h + 1)
                dve.tensor_reduce(mx[:, par, g], sc[:, g, 0:S], AXX, ALU.min).then_inc(mx_step, 1)
                dve.wait_ge(mx_step, b * 2 + h + 1)
                if not (isinstance(b, int) and b < 2):
                    dve.wait_ge(low_ready, b * 2 + (h - 3))
                dve.tensor_scalar(nm[:, par, g], mx[:, par, g], -CLAMP, CLAMP, ALU.max, ALU.min).then_inc(nm_ready, 1)

            def store_probabilities(b, par, h):
                if h == 1:
                    dve.wait_ge(plp_ready, b + 1)
                    dve.tensor_copy(pTl[:, par, :], ob[0:G, PL:PL + P]).then_inc(pTl_ready, 1)
                dve.wait_ge(ptp_ready, b * 2 + h + 1)
                dve.tensor_copy(pT[:, par, 2 * h:2 * h + 2].rearrange("p g t c -> p (g t c)"),
                                ptp[:]).then_inc(pT_ready, 1)

            def clamp(b, par):
                dve.wait_ge(low_ready, b * 2 + 2)
                for g in range(G):
                    dve.wait_ge(exp_ready, b * 4 + (g + 1))
                    dve.tensor_scalar(pr[:, par, g, :], pr[:, par, g, :], 1.0, low[:, par, g:g + 1],
                                       ALU.min, ALU.max).then_inc(pr_ready, 1)

            def mask_output(b, par):
                dve.wait_ge(o_ready, b + 1)
                if not (isinstance(b, int) and b < 2):
                    dve.wait_ge(on_ready, b - 1)
                o = ob[:, 0:G * 65].rearrange("p (g c) -> p g c", g=G)
                dve.reciprocal(rinv[:, par, :], o[:, :, 64]).then_inc(rinv_ready, 1)
                dve.tensor_tensor(om[:, par, :].rearrange("p (g c) -> p g c", g=G), o[:, :, 0:64],
                                  mask64[:].unsqueeze(1).to_broadcast([P, G, 64]), ALU.mult).then_inc(om_ready, 1)

            def store_output(b):
                dve.wait_ge(oTp_ready, b + 1)
                dve.tensor_copy(oT[:, :, bass.ds(b * L, L)],
                                ob[:, OT:OT + 2 * L].rearrange("p (h q) -> p h q", h=2)).then_inc(oT_stored, 1)

            def step(b, par, slot):
                static = isinstance(b, int)
                store_v(b, par)
                if not static or b >= 2:
                    mask_output(b - 2, par)
                maxima(b, par, 0)
                maxima(b, par, 1)
                if not static or b >= 1:
                    store_probabilities(b - 1, 1 - par, 0)
                if not static or b >= 1:
                    store_probabilities(b - 1, 1 - par, 1)
                if not static or b >= 2:
                    store_output(b - 2)
                clamp(b, par)

            run_steps(dve, step, 0, B)
            mask_output(B - 2, 0)
            store_probabilities(B - 1, 1, 0)
            store_probabilities(B - 1, 1, 1)
            store_output(B - 2)
            mask_output(B - 1, 1)
            store_output(B - 1)


def constants():
    p = np.arange(P)
    vl = np.zeros((G, B, G * 65), np.float32)
    for g in range(G):
        vl[g, :, 65 * g + 64] = 1.0
    return {
        "c_ident": np.eye(P, dtype=np.float32),
        "c_istack": (p[:, None] % L == np.arange(L)).astype(np.float32),
        "c_mask8": (p[:, None] // HD == np.arange(8)).astype(np.float32),
        "c_mask8s": -SCALE * (p[:, None] // HD == np.arange(8)).astype(np.float32),
        "c_mask64": (p[:, None] // L == np.arange(64) // HD).astype(np.float32),
        "c_mask4": (p[:, None] // L == np.arange(4)).astype(np.float32),
        "c_onesr": np.ones((1, P), np.float32),
        "c_tri": (p[:, None] < p).astype(np.float32),
        "c_ones": np.ones((P, P), np.float32),
        "c_reset": np.tile((p % T != 0).astype(np.float32), (P, 1)),
        "c_iota": np.tile(np.arange(8, dtype=np.float32), (P, 1)),
        "c_steps": np.tile(P * np.arange(T, dtype=np.float32), (P, 1)),
        "c_tiles": np.tile(np.arange(40, dtype=np.float32), (P, 1)),
        "c_first": np.tile(512 * np.arange(8, dtype=np.float32), (P, 1)),
        "one2": np.ones((P, 2), np.float32),
        "zero2": np.zeros((P, 2), np.float32),
        "zero8": np.zeros((8,), np.float32),
        "c_vlast": vl,
    }



V2 = 2 * P
NS = N // V2
BS = V2 // L


class Link:

    def __init__(self, eng, sem, base=0):
        self.eng, self.sem, self.base, self.n = eng, sem, base, 0

    def __call__(self, ins):
        self.n += 1
        ins.then_inc(self.sem, 1)
        self.eng.wait_ge(self.sem, self.base + self.n)


def refine(dve, link, ve, rt, rs, tmp):
    link(dve.reciprocal(rs, rt))
    link(dve.tensor_tensor(tmp, rs, rs, ALU.mult))
    link(dve.tensor_tensor(tmp, tmp, ve, ALU.mult))
    link(dve.tensor_scalar(tmp, tmp, -0.5, 1.5, ALU.mult, ALU.add))
    link(dve.tensor_tensor(rs, rs, tmp, ALU.mult))


def merge_phase(nc, io, m, oT, rawsum, csum, xs, xin, nT):
    with ExitStack() as st:
        p = Mem(nc, st)
        ident = p.sb("mg_ident", [P, P])
        onesr = p.sb("mg_onesr", [1, P])
        wv = p.sb("mg_wv", [P, 2, D])
        wo = p.sb("mg_wo", [P, 2, D])
        bv = p.sb("mg_bv", [P, 2])
        bo = p.sb("mg_bo", [P, D])
        g1 = p.sb("mg_g1", [P, 2])
        b1 = p.sb("mg_b1", [P, 2])
        same = p.sb("mg_same", [P, B * G])
        ok = p.sb("mg_ok", [P, 1])
        ok1 = p.sb("mg_ok1", [1, 1])
        bad = p.sb("mg_bad", [P, 1], U32)
        mean = p.sb("mg_mean", [P, 2, B])
        ost = p.sb("mg_ost", [P, 2, 2, V2])
        stats = p.sb("mg_stats", [P, T, 6])
        mv = p.sb("mg_mv", [P, T, 2])
        ve = p.sb("mg_ve", [P, T])
        rt = p.sb("mg_rt", [P, T])
        rs = p.sb("mg_rs", [P, T])
        tmp = p.sb("mg_tmp", [P, T])
        xh = p.sb("mg_xh", [P, 2, 2, D])
        fp = p.ps("mg_fp", [P, 512])
        xo = p.ps("mg_xo", [P, 2, 2, D])
        tp = p.ps("mg_tp", [P, 2, 2, V2])
        loaded = p.sem("mg_loaded")
        xb_ready = p.sem("mg_xb_ready")
        okT_ready = p.sem("mg_okT_ready")
        mean_ready = p.sem("mg_mean_ready")
        ok_ready = p.sem("mg_ok_ready")
        okb_ready = p.sem("mg_okb_ready")
        ost_ready = p.sem("mg_ost_ready")
        xo_ready = p.sem("mg_xo_ready")
        xo_free = p.sem("mg_xo_free")
        var_ready = p.sem("mg_var_ready")
        sqrt_ready = p.sem("mg_sqrt_ready")
        xh_ready = p.sem("mg_xh_ready")
        tp_ready = p.sem("mg_tp_ready")
        nT_stored = p.sem("mg_nT_stored")
        step = p.sem("mg_step")
        block = st.enter_context(nc.Block())
        NLOAD = 9

        @block.sync
        def _(sp):
            for dst, src in ((ident[:], io["c_ident"]), (onesr[:], io["c_onesr"]), (wv[:, 0, :], io["Wv"][0:P, :]),
                             (wv[0:64, 1, :], io["Wv"][P:DC, :]), (wo[:], io["Wo"].rearrange("(k p) m -> p k m", p=P)),
                             (bv[:], io["bv"]), (bo[:], io["bo"].partition_broadcast(P)), (g1[:], io["g1"]), (b1[:], io["b1"])):
                sp.dma_start(dst, src).then_inc(loaded, 16)

        @block.gpsimd
        def _(pool):
            pool.wait_ge(loaded, 16 * NLOAD)
            for i in range(4):
                pool.tensor_tensor(xs[:, 4 * i:4 * i + 4, :], xs[:, 4 * i:4 * i + 4, :],
                                   bo[:].unsqueeze(1).to_broadcast([P, 4, D]), ALU.add).then_inc(xb_ready, 1)

        @block.tensor
        def _(pe):
            pe.wait_ge(loaded, 16 * NLOAD)
            for h in range(2):
                for k, rows in ((0, P), (1, 64)):
                    mm = pe.matmul(fp[:, B * h:B * h + B], wv[0:rows, k, P * h:P * h + P], csum[0:rows, k, :],
                                   start=(k == 0), stop=(k == 1))
            mm.then_inc(mean_ready, 1)
            pe.wait_ge(ok_ready, 2)
            pe.transpose(fp[0:1, 0:P], ok[:], ident[:]).then_inc(okT_ready, 1)
            pe.wait_ge(ok_ready, 3)
            pe.matmul(fp[:, 256:257], onesr[:], ok1[:], start=True, stop=True).then_inc(okb_ready, 1)
            with pe.Fori(0, NS // 2) as i:
                for j in range(2):
                    s = i * 2 + j
                    pe.wait_ge(ost_ready, s * 2 + 2)
                    pe.wait_ge(xo_free, s + 1)
                    for t in range(2):
                        for k in range(2):
                            mm = pe.matmul(xo[:, j, t, :], ost[:, j, k, P * t:P * t + P], wo[:, k, :],
                                           start=(k == 0), stop=(k == 1))
                    mm.then_inc(xo_ready, 1)
            with pe.Fori(0, NS // 2) as i:
                for j in range(2):
                    s = i * 2 + j
                    pe.wait_ge(xh_ready, s * 2 + 2)
                    pe.wait_ge(nT_stored, s * 2 + 2)
                    for k in range(2):
                        for t in range(2):
                            mm = pe.transpose(tp[:, j, k, P * t:P * t + P], xh[:, j, t, P * k:P * k + P], ident[:])
                    mm.then_inc(tp_ready, 1)

        @block.vector
        def _(dve):
            link = Link(dve, step)
            dve.wait_ge(loaded, 16 * NLOAD)
            link(dve.tensor_tensor(same[:], rawsum[:], rawsum[:], ALU.is_equal))
            dve.wait_ge(mean_ready, 1)
            dve.tensor_scalar(mean[:].rearrange("p h b -> p (h b)"), fp[:, 0:2 * B], 1.0 / S, None, ALU.mult).then_inc(ok_ready, 1)
            dve.tensor_reduce(ok[:], same[:], AXX, ALU.min).then_inc(ok_ready, 1)
            dve.wait_ge(okT_ready, 1)
            dve.tensor_reduce(ok1[:], fp[0:1, 0:P], AXX, ALU.min).then_inc(ok_ready, 1)
            dve.wait_ge(okb_ready, 1)
            link(dve.tensor_scalar(bad[:], fp[:, 256:257], 0.0, None, ALU.is_equal))
            for h in range(2):
                link(dve.copy_predicated(oT[:, h, :].rearrange("p (b q) -> p b q", q=L),
                                         bad[:].unsqueeze(2).to_broadcast([P, B, L]),
                                         mean[:, h, :].unsqueeze(2).to_broadcast([P, B, L])))
            dve.sem_inc(xo_free, 2)
            with dve.Fori(0, NS // 2) as i:
                for j in range(2):
                    s = i * 2 + j
                    for k in range(2):
                        dve.tensor_scalar(ost[:, j, k, :], oT[:, k, bass.ds(s * V2, V2)], bv[:, k:k + 1], None,
                                          ALU.add).then_inc(ost_ready, 1)
                    dve.wait_ge(xo_ready, s + 1)
                    dve.wait_ge(xb_ready, 4)
                    x1 = xs[:, bass.ds(s * 2, 2), :]
                    dve.tensor_tensor(x1, xo[:, j], x1, ALU.add).then_inc(xo_free, 1)
                    dve.wait_ge(xo_free, s + 3)
                    for t in range(2):
                        dve.bn_stats(stats[:, bass.ds(s * 2 + t, 1), :].rearrange("p t c -> p (t c)"),
                                     xs[:, bass.ds(s * 2 + t, 1), :].rearrange("p t c -> p (t c)")).then_inc(step, 1)
            base = link.n + T
            link = Link(dve, step, base)
            dve.wait_ge(step, base)

            def aggregate(n):
                for t in range(T):
                    ins = dve.bn_aggr(mv[:, t, :], stats[:, t, :])
                    if t < T - 1:
                        link.n += 1
                        ins.then_inc(step, 1)
                link(ins)
                link(dve.tensor_scalar(ve[:], mv[:, :, 1], EPS, None, ALU.add))
                dve.sem_inc(var_ready, 1)
                dve.wait_ge(sqrt_ready, n)
                refine(dve, link, ve[:], rt[:], rs[:], tmp[:])

            aggregate(1)
            for t in range(T):
                dve.tensor_scalar(xin[:, t, :], xs[:, t, :], mv[:, t, 0:1], rs[:, t:t + 1],
                                  ALU.subtract, ALU.mult).then_inc(step, 1)
                link.n += 1
                dve.wait_ge(step, link.base + link.n)
                dve.bn_stats(stats[:, t, :], xin[:, t, :]).then_inc(step, 1)
                link.n += 1
            dve.wait_ge(step, link.base + link.n)
            aggregate(2)
            for s in range(NS):
                for t in range(2):
                    if s >= 2:
                        dve.wait_ge(tp_ready, s - 1)
                    dve.tensor_scalar(xh[:, s % 2, t, :], xin[:, 2 * s + t, :], mv[:, 2 * s + t, 0:1],
                                      rs[:, 2 * s + t:2 * s + t + 1], ALU.subtract, ALU.mult).then_inc(xh_ready, 1)

        @block.scalar
        def _(act):
            for n in range(2):
                act.wait_ge(var_ready, n + 1)
                act.activation(rt[:], ve[:], ACT.Sqrt).then_inc(sqrt_ready, 1)
            act.wait_ge(loaded, 16 * NLOAD)
            act.sem_inc(nT_stored, 4)
            with act.Fori(0, NS // 2) as i:
                for j in range(2):
                    s = i * 2 + j
                    act.wait_ge(tp_ready, s + 1)
                    for k in range(2):
                        act.activation(nT[:, k, bass.ds(s * V2, V2)], tp[:, j, k, :], ACT.Identity,
                                       bias=b1[:, k:k + 1], scale=g1[:, k:k + 1]).then_inc(nT_stored, 1)


def state_space_phase(nc, io, m, nT, ssm, sg, r_all, load_experts):
    with ExitStack() as st:
        p = Mem(nc, st)
        wzx = p.sb("ss_wzx", [P, 2, 2 * D])
        wg = p.sb("ss_wg", [P, 2, D])
        wr = p.sb("ss_wr", [P, 2, 2])
        wos = p.sb("ss_wos", [P, 2, D])
        cw = p.sb("ss_cw", [P, 2, 4])
        cb = p.sb("ss_cb", [P, 2])
        br = p.sb("ss_br", [P, 2])
        nS = p.sb("ss_nS", [P, 2, 2, V2])
        sz = p.sb("ss_sz", [P, 2, V2])
        xp = p.sb("ss_xp", [P, 2, BS, L + 3])
        y = p.sb("ss_y", [P, 2, V2])
        sy = p.sb("ss_sy", [P, 2, V2])
        yz = p.sb("ss_yz", [P, 2, V2])
        gT = p.sb("ss_gT", [P, 2, 2, V2])
        zb = p.ps("ss_zb", [P, 2, V2])
        xb = p.ps("ss_xb", [P, 2, V2])
        gb = p.ps("ss_gb", [P, 2, D])
        rb = p.ps("ss_rb", [P, 2, 2])
        ob = p.ps("ss_ob", [P, 2, D])
        loaded = p.sem("ss_loaded")
        pad_ready = p.sem("ss_pad_ready")
        nS_ready = p.sem("ss_nS_ready")
        z_ready = p.sem("ss_z_ready")
        x_ready = p.sem("ss_x_ready")
        g_ready = p.sem("ss_g_ready")
        o_ready = p.sem("ss_o_ready")
        z_stored = p.sem("ss_z_stored")
        x_stored = p.sem("ss_x_stored")
        g_stored = p.sem("ss_g_stored")
        r_stored = p.sem("ss_r_stored")
        o_stored = p.sem("ss_o_stored")
        conv = p.sem("ss_conv")
        sy_ready = p.sem("ss_sy_ready")
        yz_ready = p.sem("ss_yz_ready")
        gT_ready = p.sem("ss_gT_ready")
        block = st.enter_context(nc.Block())
        loads = [(cw[:], io["cw"]), (cb[:], io["cb"]), (br[:], io["br"].partition_broadcast(P))]
        loads += [(dst[:], io[name].rearrange("(k p) m -> p k m", p=P))
                  for dst, name in ((wzx, "Wzx"), (wg, "Wgate"), (wr, "Wr"), (wos, "Wos"))]
        NLOAD = 16 * len(loads)

        def steps(eng, step):
            for s in range(2):
                step(s, s)
            with eng.Fori(1, NS // 2) as i:
                for j in range(2):
                    step(i * 2 + j, j)

        @block.sync
        def _(sp):
            for dst, src in loads:
                sp.dma_start(dst, src).then_inc(loaded, 16)
            load_experts(sp)

        @block.tensor
        def _(pe):
            pe.wait_ge(loaded, NLOAD)

            def output(s, par):
                pe.wait_ge(gT_ready, s + 1)
                pe.wait_ge(o_stored, s)
                for t in range(2):
                    for k in range(2):
                        mm = pe.matmul(ob[:, t, :], gT[:, par, k, P * t:P * t + P], wos[:, k, :],
                                       start=(k == 0), stop=(k == 1))
                mm.then_inc(o_ready, 1)

            def step(s, par):
                src = [nT[:, k, bass.ds(s * V2, V2)] for k in range(2)]
                for bank, o, ready, stored in ((xb, 0, x_ready, x_stored), (zb, D, z_ready, z_stored)):
                    pe.wait_ge(stored, s)
                    for h in range(2):
                        for k in range(2):
                            mm = pe.matmul(bank[:, h, :], wzx[:, k, o + P * h:o + P * h + P], src[k],
                                           start=(k == 0), stop=(k == 1))
                    mm.then_inc(ready, 1)
                pe.wait_ge(nS_ready, s + 1)
                pe.wait_ge(g_stored, s)
                pe.wait_ge(r_stored, s)
                for t in range(2):
                    for k in range(2):
                        lhs = nS[:, par, k, P * t:P * t + P]
                        pe.matmul(gb[:, t, :], lhs, wg[:, k, :], start=(k == 0), stop=(k == 1))
                    for k in range(2):
                        lhs = nS[:, par, k, P * t:P * t + P]
                        mm = pe.matmul(rb[:, t, :], lhs, wr[:, k, :], start=(k == 0), stop=(k == 1))
                mm.then_inc(g_ready, 1)
                if not isinstance(s, int) or s >= 1:
                    output(s - 1, 1 - par)

            steps(pe, step)
            output(NS - 1, 1)

        @block.gpsimd
        def _(pool):
            def step(s, par):
                if not isinstance(s, int) or s >= 2:
                    pool.wait_ge(g_ready, s - 1)
                pool.tensor_copy(nS[:, par], nT[:, :, bass.ds(s * V2, V2)]).then_inc(nS_ready, 1)
                pool.wait_ge(sy_ready, s + 1)
                pool.wait_ge(z_stored, s + 1)
                pool.wait_ge(gT_ready, s)
                pool.tensor_tensor(yz[:], y[:], sz[:], ALU.mult).then_inc(yz_ready, 1)
                pool.wait_ge(yz_ready, s + 1)
                if not isinstance(s, int) or s >= 2:
                    pool.wait_ge(o_ready, s - 1)
                pool.tensor_tensor(gT[:, par], yz[:], sy[:], ALU.mult).then_inc(gT_ready, 1)

            pool.memset(xp[:, :, :, 0:3], 0.0).then_inc(pad_ready, 1)
            steps(pool, step)

        @block.scalar
        def _(act):
            act.wait_ge(loaded, NLOAD)

            def step(s, par):
                act.wait_ge(x_ready, s + 1)
                act.wait_ge(conv, s * 8)
                act.activation(xp[:, :, :, 3:], xb[:].rearrange("p h (b q) -> p h b q", q=L), ACT.Copy).then_inc(x_stored, 1)
                act.wait_ge(z_ready, s + 1)
                act.wait_ge(gT_ready, s)
                act.activation(sz[:], zb[:], ACT.Sigmoid).then_inc(z_stored, 1)
                act.wait_ge(conv, s * 8 + 8)
                act.activation(sy[:], y[:], ACT.Sigmoid).then_inc(sy_ready, 1)
                act.wait_ge(g_ready, s + 1)
                act.activation(sg[:, bass.ds(s * 2, 2), :], gb[:], ACT.Sigmoid).then_inc(g_stored, 1)

            steps(act, step)

        @block.vector
        def _(dve):
            dve.wait_ge(loaded, NLOAD)
            dve.wait_ge(pad_ready, 1)

            def output(s):
                dve.wait_ge(o_ready, s + 1)
                dve.tensor_copy(ssm[:, bass.ds(s * 2, 2), :], ob[:]).then_inc(o_stored, 1)

            def step(s, par):
                dve.wait_ge(x_stored, s + 1)
                dve.wait_ge(gT_ready, s)
                yv = y[:].rearrange("p h (b q) -> p h b q", q=L)
                for n in range(4):
                    for h in range(2):
                        src, w = xp[:, h, :, 3 - n:3 - n + L], cw[:, h, 3 - n:4 - n]
                        if n == 0:
                            ins = dve.tensor_scalar(yv[:, h], src, w, cb[:, h:h + 1], ALU.mult, ALU.add)
                        else:
                            dve.wait_ge(conv, s * 8 + (2 * n - 1 + h))
                            ins = dve.scalar_tensor_tensor(out=yv[:, h], in0=src, scalar=w, in1=yv[:, h],
                                                           op0=ALU.mult, op1=ALU.add)
                        ins.then_inc(conv, 1)
                dve.wait_ge(g_ready, s + 1)
                dve.tensor_tensor(r_all[:, bass.ds(s * 2, 2), :], rb[:], br[:].unsqueeze(1).to_broadcast([P, 2, 2]),
                                  ALU.add).then_inc(r_stored, 1)
                if not isinstance(s, int) or s >= 1:
                    output(s - 1)

            steps(dve, step)
            output(NS - 1)


def self_attention_phase(nc, io, m, nT, ssm, sg, r_all, alpha, xb):
    with ExitStack() as st:
        p = Mem(nc, st, clear=True)
        ident = p.sb("sa_ident", [P, P])
        istack = p.sb("sa_istack", [P, L])
        mask8 = p.sb("sa_mask8", [P, 8])
        mask64 = p.sb("sa_mask64", [P, 64])
        mask4 = p.sb("sa_mask4", [P, 4])
        wqk = p.sb("sa_wqk", [P, 2, 2 * D])
        wv = p.sb("sa_wv", [P, 2, D])
        wout = p.sb("sa_wout", [P, 2, D])
        ls1 = p.sb("sa_ls1", [P, D])
        nS = p.sb("sa_nS", [P, 2, P])
        qkT = p.sb("sa_qkT", [P, 2, 4, P])
        qbd = p.sb("sa_qbd", [P, 2, 4, G, P])
        vbd = p.sb("sa_vbd", [P, G, 4, 64])
        mx = p.sb("sa_mx", [P, G * 4])
        es = p.sb("sa_es", [P, G * 4, L])
        sm = p.sb("sa_sm", [P, G * 4])
        ri = p.sb("sa_ri", [P, G * 4])
        pT = p.sb("sa_pT", [P, G, P])
        om = p.sb("sa_om", [P, 4, G, 64])
        oT = p.sb("sa_oT", [P, 2, P])
        a1 = p.sb("sa_a1", [P, D])
        a3 = p.sb("sa_a3", [P, D])
        qkb = p.ps("sa_qkb", [P, 4, P])
        vb = p.ps("sa_vb", [P, 512])
        sb_ = p.ps("sa_sb", [P, G * 4 * L])
        pb = p.ps("sa_pb", [P, G, P])
        pv = p.ps("sa_pv", [P, G, 4, 64])
        otb = p.ps("sa_otb", [P, 4, P])
        outb = p.ps("sa_outb", [P, 512])
        names = ("loaded nS_ready qk_ready v_ready s_ready pt_ready pv_ready ot_ready out_ready qk_stored q_ready "
                 "v_stored mx_ready es_ready exp_ready sm_ready ri_ready p_ready pT_stored om_ready oT_stored "
                 "a1_ready a2_ready a3_ready a4_ready xb_ready alpha_ready")
        S_ = {n: p.sem("sa_" + n) for n in names.split()}
        (loaded, nS_ready, qk_ready, v_ready, s_ready, pt_ready, pv_ready, ot_ready, out_ready, qk_stored, q_ready,
         v_stored, mx_ready, es_ready, exp_ready, sm_ready, ri_ready, p_ready, pT_stored, om_ready, oT_stored,
         a1_ready, a2_ready, a3_ready, a4_ready, xb_ready, alpha_ready) = S_.values()
        block = st.enter_context(nc.Block())
        loads = [(ident[:], io["c_ident"]), (istack[:], io["c_istack"]), (mask8[:], io["c_mask8"]),
                 (mask64[:], io["c_mask64"]), (mask4[:], io["c_mask4"]), (ls1[:], io["ls1"].partition_broadcast(P))]
        loads += [(dst[:], io[name].rearrange("(k p) m -> p k m", p=P))
                  for dst, name in ((wqk, "Wqk2"), (wv, "Wv2"), (wout, "Wout2"))]
        NLOAD = 16 * len(loads)

        def tiles(eng, step):
            for t in range(-1, 3):
                step(t, t % 2)
            with eng.Fori(1, T // 2 - 1) as i:
                for j in (1, 2):
                    step(i * 2 + j, j % 2)
            for t in range(T - 1, T + 2):
                step(t, t % 2)

        def there(t, back):
            return not isinstance(t, int) or 0 <= t - back < T

        @block.sync
        def _(sp):
            for dst, src in loads:
                sp.dma_start(dst, src).then_inc(loaded, 16)

        @block.tensor
        def _(pe):
            pe.wait_ge(loaded, NLOAD)

            def step(t, par):
                if there(t, -1):
                    if there(t, 0):
                        pe.wait_ge(qk_stored, t + 1)
                    for c in range(4):
                        for k in range(2):
                            mm = pe.matmul(qkb[:, c, :], wqk[:, k, P * c:P * c + P],
                                           nT[:, k, bass.ds((t + 1) * P, P)], start=(k == 0), stop=(k == 1))
                    mm.then_inc(qk_ready, 1)
                if there(t, 1):
                    pe.wait_ge(p_ready, t)
                    pe.wait_ge(pT_stored, t - 1)
                    for g in range(G):
                        mm = pe.transpose(pb[:, g, :], es[:, 4 * g:4 * g + 4, :].rearrange("p b k -> p (b k)"), ident[:])
                    mm.then_inc(pt_ready, 1)
                if there(t, 0):
                    pe.wait_ge(es_ready, t)
                    pe.wait_ge(q_ready, t * 4 + 4)
                    for g in range(G):
                        for b in range(4):
                            n = L if b == 3 else 2 * L
                            mm = pe.matmul(sb_[:, L * (4 * g + b):L * (4 * g + b) + n], qbd[:, par, b, g, :],
                                           qkT[:, par, 2 + g // 2, L * b:L * b + n], start=True, stop=True)
                    mm.then_inc(s_ready, 1)
                if there(t, 2):
                    pe.wait_ge(om_ready, t - 1)
                    pe.wait_ge(oT_stored, t - 2)
                    for b in range(4):
                        for h in range(2):
                            mm = pe.matmul(otb[:, h, L * b:L * b + L],
                                           om[:, b, 2 * h:2 * h + 2, :].rearrange("p g c -> p (g c)"), istack[:],
                                           start=True, stop=True)
                    mm.then_inc(ot_ready, 1)
                if there(t, 1):
                    pe.wait_ge(pT_stored, t)
                    pe.wait_ge(v_stored, t)
                    pe.wait_ge(om_ready, t - 1)
                    for g in range(G):
                        mm = pe.matmul(pv[:, g, :, :].rearrange("p b c -> p (b c)"), pT[:, g, :],
                                       vbd[:, g, :, :].rearrange("p b c -> p (b c)"), start=True, stop=True)
                    mm.then_inc(pv_ready, 1)
                if there(t, 2):
                    pe.wait_ge(oT_stored, t - 1)
                    pe.wait_ge(a1_ready, t - 2)
                    for k in range(2):
                        mm = pe.matmul(outb[:, 0:D], oT[:, k, :], wout[:, k, :], start=(k == 0), stop=(k == 1))
                    mm.then_inc(out_ready, 1)
                if there(t, 0):
                    pe.wait_ge(nS_ready, t + 1)
                    pe.wait_ge(v_stored, t)
                    for k in range(2):
                        mm = pe.matmul(vb[:, 0:D], nS[:, k, :], wv[:, k, :], start=(k == 0), stop=(k == 1))
                    mm.then_inc(v_ready, 1)

            tiles(pe, step)

        @block.gpsimd
        def _(pool):
            pool.wait_ge(loaded, NLOAD)

            def step(t, par):
                if there(t, -1):
                    pool.wait_ge(qk_stored, t + 2)
                    if there(t, 0):
                        pool.wait_ge(s_ready, t)
                    for b in range(4):
                        src = qkT[:, 1 - par, 0:2, L * b:L * b + L].unsqueeze(2).to_broadcast([P, 2, 8, L])
                        msk = mask8[:].unsqueeze(1).unsqueeze(3).to_broadcast([P, 2, 8, L])
                        pool.tensor_tensor(qbd[:, 1 - par, b].rearrange("p (h j) (e q) -> p h (j e) q", h=2, q=L),
                                           src, msk, ALU.mult).then_inc(q_ready, 1)
                if there(t, 0):
                    pool.wait_ge(ri_ready, t + 1)
                    pool.tensor_tensor(es[:], es[:], ri[:].unsqueeze(2).to_broadcast([P, G * 4, L]),
                                       ALU.mult).then_inc(p_ready, 1)
                if there(t, 2):
                    c = t - 2
                    pool.wait_ge(a3_ready, c + 1)
                    pool.tensor_tensor(a3[:], a3[:], ls1[:], ALU.mult).then_inc(a4_ready, 1)
                    pool.wait_ge(a4_ready, c + 1)
                    x = xb[:, bass.ds(c, 1), :].rearrange("p t c -> p (t c)")
                    pool.tensor_tensor(x, a3[:], x, ALU.add).then_inc(xb_ready, 1)

            tiles(pool, step)

        @block.scalar
        def _(act):
            act.activation(alpha[:], r_all[:, :, 0], ACT.Sigmoid).then_inc(alpha_ready, 1)
            act.wait_ge(alpha_ready, 1)

            def step(t, par):
                if there(t, 0):
                    act.wait_ge(v_ready, t)
                    act.activation(nS[:], nT[:, :, bass.ds(t * P, P)], ACT.Copy).then_inc(nS_ready, 1)
                if there(t, -1):
                    act.wait_ge(qk_ready, t + 2)
                    if there(t, 0):
                        act.wait_ge(s_ready, t)
                    act.activation(qkT[:, 1 - par], qkb[:], ACT.Copy).then_inc(qk_stored, 1)
                if there(t, 1):
                    act.wait_ge(pt_ready, t)
                    act.wait_ge(pv_ready, t - 1)
                    act.activation(pT[:], pb[:], ACT.Copy).then_inc(pT_stored, 1)
                if there(t, 0):
                    act.wait_ge(es_ready, t + 1)
                    act.activation(es[:], es[:], ACT.Exp, scale=SCALE).then_inc(exp_ready, 1)

            tiles(act, step)

        @block.vector
        def _(dve):
            dve.wait_ge(loaded, NLOAD)
            dve.wait_ge(alpha_ready, 1)

            def step(t, par):
                if there(t, 0):
                    dve.wait_ge(s_ready, t + 1)
                    scores = sb_[:].rearrange("p (g k) -> p g k", k=L)
                    dve.tensor_reduce(mx[:], scores, AXX, ALU.max).then_inc(mx_ready, 1)
                    dve.wait_ge(mx_ready, t + 1)
                    dve.wait_ge(pt_ready, t)
                    dve.tensor_tensor(es[:], scores, mx[:].unsqueeze(2).to_broadcast([P, G * 4, L]),
                                      ALU.subtract).then_inc(es_ready, 1)
                if there(t, 2):
                    dve.wait_ge(ot_ready, t - 1)
                    dve.wait_ge(out_ready, t - 2)
                    dve.tensor_copy(oT[:], otb[:, 0:2, :]).then_inc(oT_stored, 1)
                if there(t, 0):
                    dve.wait_ge(exp_ready, t + 1)
                    dve.tensor_reduce(sm[:], es[:], AXX, ALU.add).then_inc(sm_ready, 1)
                    dve.wait_ge(sm_ready, t + 1)
                    dve.wait_ge(p_ready, t)
                    dve.reciprocal(ri[:], sm[:]).then_inc(ri_ready, 1)
                if there(t, 1):
                    dve.wait_ge(pv_ready, t)
                    dve.wait_ge(ot_ready, t - 1)
                    dve.tensor_tensor(om[:].rearrange("p b g c -> p g b c"), pv[:],
                                      mask64[:].unsqueeze(1).unsqueeze(1).to_broadcast([P, G, 4, 64]),
                                      ALU.mult).then_inc(om_ready, 1)
                if there(t, 2):
                    c = t - 2
                    row = [a[:, bass.ds(c, 1), :].rearrange("p t c -> p (t c)") for a in (sg, ssm)]
                    dve.wait_ge(out_ready, c + 1)
                    dve.wait_ge(a3_ready, c)
                    dve.tensor_tensor(a1[:], outb[:, 0:D], row[0], ALU.mult).then_inc(a1_ready, 1)
                    dve.wait_ge(a1_ready, c + 1)
                    dve.tensor_tensor(a1[:], a1[:], row[1], ALU.subtract).then_inc(a2_ready, 1)
                    dve.wait_ge(a2_ready, c + 1)
                    dve.wait_ge(xb_ready, c)
                    dve.scalar_tensor_tensor(out=a3[:], in0=a1[:], scalar=alpha[:, bass.ds(c, 1)], in1=row[1],
                                             op0=ALU.mult, op1=ALU.add).then_inc(a3_ready, 1)
                if there(t, 0):
                    dve.wait_ge(v_ready, t + 1)
                    dve.wait_ge(pv_ready, t)
                    dve.tensor_tensor(vbd[:], vb[:, 0:D].rearrange("p (g c) -> p g c", g=G).unsqueeze(2).to_broadcast([P, G, 4, 64]),
                                      mask4[:].unsqueeze(1).unsqueeze(3).to_broadcast([P, G, 4, 64]),
                                      ALU.mult).then_inc(v_stored, 1)

            tiles(dve, step)



E = 8
F1 = 512
F2 = 1024
CAP = 2 * N // E
J1 = 40
GA = 4


def normed_router_phase(nc, io, pre, src, dst, lg, wr, gain, bias, b_router):
    with ExitStack() as st:
        p = Mem(nc, st)
        ident = p.sb(pre + "ident", [P, P])
        w = p.sb(pre + "w", [P, 2, E])
        gb = p.sb(pre + "gb", [P, 2, 2])
        brt = p.sb(pre + "brt", [P, E])
        stats = p.sb(pre + "stats", [P, T, 6])
        mv = p.sb(pre + "mv", [P, T, 2])
        ve = p.sb(pre + "ve", [P, T])
        rt = p.sb(pre + "rt", [P, T])
        rs = p.sb(pre + "rs", [P, T])
        tmp = p.sb(pre + "tmp", [P, T])
        xh = p.sb(pre + "xh", [P, 2, 2, D])
        xT = p.sb(pre + "xT", [P, 2, 2, V2])
        tp = p.ps(pre + "tp", [P, 2, 2, V2])
        lp = p.ps(pre + "lp", [P, 2, 512])
        loaded = p.sem(pre + "loaded")
        step = p.sem(pre + "step")
        var_ready = p.sem(pre + "var_ready")
        sqrt_ready = p.sem(pre + "sqrt_ready")
        xh_ready = p.sem(pre + "xh_ready")
        xh_copied = p.sem(pre + "xh_copied")
        tp_ready = p.sem(pre + "tp_ready")
        xT_ready = p.sem(pre + "xT_ready")
        lp_ready = p.sem(pre + "lp_ready")
        lg_ready = p.sem(pre + "lg_ready")
        block = st.enter_context(nc.Block())
        loads = [(ident[:], io["c_ident"]), (w[:], io[wr].rearrange("(k p) m -> p k m", p=P)),
                 (brt[:], io[b_router].partition_broadcast(P)), (gb[:, 0, :], io[gain]), (gb[:, 1, :], io[bias])]
        NLOAD = 16 * len(loads)

        @block.sync
        def _(sp):
            for d, s in loads:
                sp.dma_start(d, s).then_inc(loaded, 16)

        @block.vector
        def _(dve):
            for t in range(T):
                dve.bn_stats(stats[:, t, :], src[:, t, :]).then_inc(step, 1)
            dve.wait_ge(step, T)
            for t in range(T):
                dve.bn_aggr(mv[:, t, :], stats[:, t, :]).then_inc(step, 1)
            dve.wait_ge(step, 2 * T)
            dve.tensor_scalar(ve[:], mv[:, :, 1], EPS, None, ALU.add).then_inc(var_ready, 1)
            dve.wait_ge(sqrt_ready, 1)
            link = Link(dve, step, 2 * T)
            refine(dve, link, ve[:], rt[:], rs[:], tmp[:])
            dve.wait_ge(loaded, NLOAD)

            def logits(s):
                dve.wait_ge(lp_ready, s + 1)
                dve.tensor_tensor(lg[:, 2 * s:2 * s + 2, :], lp[:, s % 2, 0:2 * E].rearrange("p (t e) -> p t e", t=2),
                                  brt[:].unsqueeze(1).to_broadcast([P, 2, E]), ALU.add).then_inc(lg_ready, 1)

            for s in range(NS):
                if s >= 2:
                    dve.wait_ge(tp_ready, s - 1)
                    dve.wait_ge(xh_copied, s - 1)
                for t in range(2):
                    dve.tensor_scalar(xh[:, s % 2, t, :], src[:, 2 * s + t, :], mv[:, 2 * s + t, 0:1],
                                      rs[:, 2 * s + t:2 * s + t + 1], ALU.subtract, ALU.mult).then_inc(xh_ready, 1)
                if s >= 2:
                    logits(s - 2)
            logits(NS - 2)
            logits(NS - 1)

        @block.gpsimd
        def _(pool):
            for s in range(NS):
                pool.wait_ge(xh_ready, 2 * s + 2)
                pool.tensor_copy(dst[:, 2 * s:2 * s + 2, :], xh[:, s % 2]).then_inc(xh_copied, 1)

        @block.scalar
        def _(act):
            act.wait_ge(var_ready, 1)
            act.activation(rt[:], ve[:], ACT.Sqrt).then_inc(sqrt_ready, 1)
            act.wait_ge(loaded, NLOAD)
            for s in range(NS):
                act.wait_ge(tp_ready, s + 1)
                if s >= 2:
                    act.wait_ge(lp_ready, s - 1)
                for k in range(2):
                    act.activation(xT[:, s % 2, k, :], tp[:, s % 2, k, :], ACT.Identity,
                                   bias=gb[:, 1, k:k + 1], scale=gb[:, 0, k:k + 1]).then_inc(xT_ready, 1)

        @block.tensor
        def _(pe):
            pe.wait_ge(loaded, NLOAD)

            def products(s):
                pe.wait_ge(xT_ready, 2 * s + 2)
                if s >= 2:
                    pe.wait_ge(lg_ready, s - 1)
                for t in range(2):
                    for k in range(2):
                        mm = pe.matmul(lp[:, s % 2, E * t:E * t + E], xT[:, s % 2, k, P * t:P * t + P], w[:, k, :],
                                       start=(k == 0), stop=(k == 1))
                mm.then_inc(lp_ready, 1)

            for s in range(NS):
                pe.wait_ge(xh_ready, 2 * s + 2)
                if s >= 2:
                    pe.wait_ge(xT_ready, 2 * s - 2)
                for k in range(2):
                    for t in range(2):
                        mm = pe.transpose(tp[:, s % 2, k, P * t:P * t + P], xh[:, s % 2, t, P * k:P * k + P], ident[:])
                mm.then_inc(tp_ready, 1)
                if s >= 1:
                    products(s - 1)
            products(NS - 1)


def route_phase(nc, io, pre, lg, slot, weight, te, capped):
    with ExitStack() as st:
        p = Mem(nc, st)

        def sb(name, shape, dt=F32):
            return p.sb(pre + name, shape, dt)

        tri, ones, reset = sb("tri", [P, P]), sb("ones", [P, P]), sb("reset", [P, P])
        iota = sb("iota", [P, E])
        steps = sb("steps", [P, T])
        tiles = sb("tiles", [P, J1])
        first = sb("first", [P, E])
        mx, z, rz = sb("mx", [P, T]), sb("z", [P, T]), sb("rz", [P, T])
        v = sb("v", [P, T, E])
        top = sb("top", [P, T, 8])
        ix = sb("ix", [P, T, 8], U32)
        ixf = sb("ixf", [P, T, 8])
        sel = sb("sel", [P, 3, T, E])
        tot, incl, rank = sb("tot", [P, E, T]), sb("incl", [P, E, T]), sb("rank", [P, E, T])
        keep = sb("keep", [P, E, T])
        nt, tb, tx = sb("nt", [P, E]), sb("tb", [P, E]), sb("tx", [P, E])
        ge = sb("ge", [1, J1, E])
        tef = sb("tef", [1, J1])
        sf = sb("sf", [P, 2, T])
        t1, t2 = sb("t1", [P, T]), sb("t2", [P, T])
        pb = p.ps(pre + "pb", [P, 2, P])
        loaded = p.sem(pre + "loaded")
        step = p.sem(pre + "step")
        exp_in = p.sem(pre + "exp_in")
        exp_out = p.sem(pre + "exp_out")
        sel_ready = p.sem(pre + "sel_ready")
        rank_ready = p.sem(pre + "rank_ready")
        block = st.enter_context(nc.Block())
        loads = [(tri, "c_tri"), (ones, "c_ones"), (reset, "c_reset"), (iota, "c_iota"), (steps, "c_steps"),
                 (tiles, "c_tiles"), (first, "c_first")]
        NLOAD = 16 * len(loads)

        @block.sync
        def _(sp):
            for d, name in loads:
                sp.dma_start(d[:], io[name]).then_inc(loaded, 16)

        @block.scalar
        def _(act):
            act.wait_ge(exp_in, 1)
            if capped:
                act.activation(z[:], z[:], ACT.Exp).then_inc(exp_out, 1)
            else:
                act.activation(v[:], v[:], ACT.Exp).then_inc(exp_out, 1)

        @block.tensor
        def _(pe):
            pe.wait_ge(loaded, NLOAD)
            pe.wait_ge(sel_ready, 1)
            both = sel[:, 2].rearrange("p t e -> p e t")
            pe.matmul(pb[:, 0, :], tri[:], both, start=True, stop=True)
            pe.matmul(pb[:, 1, :], ones[:], both, start=True, stop=True).then_inc(rank_ready, 1)

        @block.vector
        def _(dve):
            link = Link(dve, step)
            dve.wait_ge(loaded, NLOAD)

            def along(a):
                return a.unsqueeze(2).to_broadcast([P, T, E])

            src = lg
            if not capped:
                link(dve.tensor_reduce(mx[:], lg[:], AXX, ALU.max))
                dve.tensor_tensor(v[:], lg[:], along(mx[:]), ALU.subtract).then_inc(exp_in, 1)
                dve.wait_ge(exp_out, 1)
                link(dve.tensor_reduce(z[:], v[:], AXX, ALU.add))
                link(dve.reciprocal(rz[:], z[:]))
                link(dve.tensor_tensor(v[:], v[:], along(rz[:]), ALU.mult))
                src = v
            for t in range(T):
                dve.max(top[:, t, :], src[:, t, :]).then_inc(step, 1)
                link.n += 1
            dve.wait_ge(step, link.n)
            for t in range(T):
                dve.max_index(ix[:, t, :], top[:, t, :], src[:, t, :]).then_inc(step, 1)
                link.n += 1
            dve.wait_ge(step, link.n)
            link(dve.tensor_copy(ixf[:], ix[:]))
            for c in range(2):
                link(dve.tensor_tensor(sel[:, c], iota[:].unsqueeze(1).to_broadcast([P, T, E]), along(ixf[:, :, c]),
                                       ALU.is_equal))
            dve.tensor_tensor(sel[:, 2], sel[:, 0], sel[:, 1], ALU.add).then_inc(sel_ready, 1)
            if capped:
                dve.tensor_tensor(z[:], top[:, :, 1], top[:, :, 0], ALU.subtract).then_inc(exp_in, 1)
                dve.wait_ge(exp_out, 1)
                link(dve.tensor_scalar(t1[:], z[:], 1.0, None, ALU.add))
                link(dve.reciprocal(weight[:, 0, :], t1[:]))
                link(dve.tensor_tensor(weight[:, 1, :], z[:], weight[:, 0, :], ALU.mult))
            else:
                link(dve.tensor_tensor(t1[:], top[:, :, 0], top[:, :, 1], ALU.add))
                link(dve.tensor_scalar(t2[:], t1[:], 1e-8, None, ALU.add))
                link(dve.reciprocal(t1[:], t2[:]))
                for c in range(2):
                    link(dve.tensor_tensor(weight[:, c, :], top[:, :, c], t1[:], ALU.mult))
            dve.wait_ge(rank_ready, 1)
            link(dve.tensor_copy(tot[:].rearrange("p e t -> p (e t)"), pb[:, 1, :]))
            link(dve.tensor_tensor_scan(out=incl[:].rearrange("p e t -> p (e t)"), data0=reset[:],
                                        data1=tot[:].rearrange("p e t -> p (e t)"), initial=0.0,
                                        op0=ALU.mult, op1=ALU.add))
            link(dve.tensor_tensor(rank[:], incl[:], tot[:], ALU.subtract))
            link(dve.tensor_tensor(rank[:].rearrange("p e t -> p (e t)"), pb[:, 0, :],
                                   rank[:].rearrange("p e t -> p (e t)"), ALU.add))
            base = first
            if capped:
                link(dve.tensor_scalar(keep[:], rank[:], float(CAP), None, ALU.is_lt))
            else:
                link(dve.tensor_tensor(keep[:], incl[:, :, T - 1:T].to_broadcast([P, E, T]),
                                       steps[:].unsqueeze(1).to_broadcast([P, E, T]), ALU.is_gt))
                link(dve.tensor_reduce(nt[:], keep[:], AXX, ALU.add))
                link(dve.tensor_tensor_scan(out=tb[:], data0=ones[:, 0:E], data1=nt[:], initial=0.0,
                                            op0=ALU.mult, op1=ALU.add))
                link(dve.tensor_tensor(tx[:], tb[:], nt[:], ALU.subtract))
                link(dve.tensor_scalar(tx[:], tx[:], float(P), None, ALU.mult))
                base = tx
                link(dve.tensor_tensor(ge[:], tiles[0:1, :].unsqueeze(2).to_broadcast([1, J1, E]),
                                       tb[0:1, :].unsqueeze(1).to_broadcast([1, J1, E]), ALU.is_ge))
                link(dve.tensor_reduce(tef[:], ge[:], AXX, ALU.add))
                link(dve.tensor_scalar(te[:], tef[:], float(E - 1), None, ALU.min))
            link(dve.tensor_tensor(rank[:], rank[:], base[:].unsqueeze(2).to_broadcast([P, E, T]), ALU.add))
            if capped:
                link(dve.tensor_scalar(rank[:], rank[:], -2.0 * N, None, ALU.add))
                link(dve.tensor_tensor(rank[:], rank[:], keep[:], ALU.mult))
                link(dve.tensor_scalar(rank[:], rank[:], 2.0 * N, None, ALU.add))
            for c in range(2):
                link(dve.tensor_tensor(v[:], sel[:, c], rank[:].rearrange("p e t -> p t e"), ALU.mult))
                link(dve.tensor_reduce(sf[:, c, :], v[:], AXX, ALU.add))
                link(dve.tensor_copy(slot[:, c, :], sf[:, c, :]))


def scatter_phase(nc, pre, rows, slot, buf, n_slots, zeroed):
    with ExitStack() as st:
        scattered = Mem(nc, st).sem(pre + "scattered")
        block = st.enter_context(nc.Block())

        @block.gpsimd
        def _(pool):
            pool.wait_ge(*zeroed)
            for t in range(T):
                for c in range(2):
                    pool.indirect_dma_start(out=buf, out_offset=bass.IndirectOffsetOnAxis(ap=slot[:, c, t:t + 1], axis=0),
                                            in_=rows[:, t, :], in_offset=None, bounds_check=n_slots - 1,
                                            oob_is_err=False).then_inc(scattered, 16)
            pool.wait_ge(scattered, 16 * 2 * T)


def first_experts_phase(nc, io, xg, yg, te, w13, w2, w_loaded):
    with ExitStack() as st:
        p = Mem(nc, st)
        ident = p.sb("e1_ident", [P, P])
        gb = p.sb("e1_gb", [P, 2, 2])
        x = p.sb("e1_x", [P, 2, D])
        xT = p.sb("e1_xT", [P, 2, 2, P])
        s = p.sb("e1_s", [P, F1])
        h = p.sb("e1_h", [P, F1])
        hT = p.sb("e1_hT", [P, 4, P])
        y = p.sb("e1_y", [P, 2, D])
        tb = p.ps("e1_tb", [P, 2, P])
        ab = p.ps("e1_ab", [P, F1])
        bb = p.ps("e1_bb", [P, F1])
        hb = p.ps("e1_hb", [P, 4, P])
        yb = p.ps("e1_yb", [P, D])
        loaded = p.sem("e1_loaded")
        x_loaded = [p.sem(f"e1_x_loaded{i}") for i in range(2)]
        y_written = [p.sem(f"e1_y_written{i}") for i in range(2)]
        t_ready = p.sem("e1_t_ready")
        xT_ready = p.sem("e1_xT_ready")
        a_ready = p.sem("e1_a_ready")
        b_ready = p.sem("e1_b_ready")
        s_ready = p.sem("e1_s_ready")
        h_ready = p.sem("e1_h_ready")
        hb_ready = p.sem("e1_hb_ready")
        hT_ready = p.sem("e1_hT_ready")
        yb_ready = p.sem("e1_yb_ready")
        y_ready = p.sem("e1_y_ready")
        block = st.enter_context(nc.Block())

        def tiles(eng, step, lag=0):
            for j in range(4):
                step(j, j % 2)
            with eng.Fori(2, J1 // 2 - 1) as i:
                for j in range(2):
                    step(i * 2 + j, j)
            for j in range(J1 - 2, J1 + lag):
                step(j, j % 2)

        def there(j, back):
            return not isinstance(j, int) or 0 <= j - back < J1

        @block.sync
        def _(sp):
            sp.dma_start(ident[:], io["c_ident"]).then_inc(loaded, 16)
            sp.dma_start(gb[:, 0, :], io["g2"]).then_inc(loaded, 16)
            sp.dma_start(gb[:, 1, :], io["b2"]).then_inc(loaded, 16)
            for j in range(2):
                sp.dma_start(x[:, j, :], xg[P * j:P * j + P, :]).then_inc(x_loaded[j], 16)

            def step(j, par):
                if there(j, -2):
                    sp.wait_ge(t_ready, j + 1)
                    sp.dma_start(x[:, par, :], xg[bass.ds(j * P + 2 * P, P), :]).then_inc(x_loaded[par], 16)
                if there(j, 1):
                    sp.wait_ge(y_ready, j)
                    sp.dma_start(yg[bass.ds(j * P - P, P), :], y[:, 1 - par, :]).then_inc(y_written[1 - par], 16)

            tiles(sp, step, 1)
            for c in range(2):
                sp.wait_ge(y_written[c], 16 * J1 // 2)

        @block.tensor
        def _(pe):
            pe.wait_ge(loaded, 48)
            pe.wait_ge(*w_loaded)

            def loads_of(j, par):
                return 16 * (j // 2 + 1) if isinstance(j, int) else j * 8 + (16 if par == 0 else 8)

            def turn_x(j, par):
                pe.wait_ge(x_loaded[par], loads_of(j, par))
                pe.wait_ge(xT_ready, j * 2)
                for k in range(2):
                    mm = pe.transpose(tb[:, k, :], x[:, par, P * k:P * k + P], ident[:])
                mm.then_inc(t_ready, 1)

            def step(j, par):
                if there(j, 0):
                    e = pe.value_load(te[0:1, bass.ds(j, 1)], min_val=0, max_val=E - 1)
                    pe.wait_ge(xT_ready, j * 2 + 2)
                    pe.wait_ge(s_ready, j)
                    for k in range(2):
                        mm = pe.matmul(ab[:], xT[:, par, k, :], w13[:, bass.ds(e * 4 + k, 1), :].rearrange("p a f -> p (a f)"),
                                       start=(k == 0), stop=(k == 1))
                    mm.then_inc(a_ready, 1)
                if there(j, 1):
                    pe.wait_ge(h_ready, j)
                    pe.wait_ge(hT_ready, j - 1)
                    for f in range(4):
                        mm = pe.transpose(hb[:, f, :], h[:, P * f:P * f + P], ident[:])
                    mm.then_inc(hb_ready, 1)
                if there(j, 0):
                    pe.wait_ge(h_ready, j)
                    for k in range(2):
                        mm = pe.matmul(bb[:], xT[:, par, k, :], w13[:, bass.ds(e * 4 + (2 + k), 1), :].rearrange("p a f -> p (a f)"),
                                       start=(k == 0), stop=(k == 1))
                    mm.then_inc(b_ready, 1)
                if there(j, -1):
                    turn_x(j + 1, 1 - par)
                if there(j, 1):
                    d = pe.value_load(te[0:1, bass.ds(j - 1, 1)], min_val=0, max_val=E - 1)
                    pe.wait_ge(hT_ready, j)
                    pe.wait_ge(y_ready, j - 1)
                    for f in range(4):
                        mm = pe.matmul(yb[:], hT[:, f, :], w2[:, bass.ds(d * 4 + f, 1), :].rearrange("p a c -> p (a c)"),
                                       start=(f == 0), stop=(f == 3))
                    mm.then_inc(yb_ready, 1)

            turn_x(0, 0)
            tiles(pe, step, 1)

        @block.scalar
        def _(act):
            act.wait_ge(loaded, 48)

            def turn_x(j, par):
                act.wait_ge(t_ready, j + 1)
                if not isinstance(j, int) or j >= 2:
                    act.wait_ge(b_ready, j - 1)
                for k in range(2):
                    act.activation(xT[:, par, k, :], tb[:, k, :], ACT.Identity,
                                   bias=gb[:, 1, k:k + 1], scale=gb[:, 0, k:k + 1]).then_inc(xT_ready, 1)

            def step(j, par):
                if there(j, 0):
                    act.wait_ge(a_ready, j + 1)
                    act.wait_ge(h_ready, j)
                    act.activation(s[:], ab[:], ACT.Silu).then_inc(s_ready, 1)
                if there(j, -1):
                    turn_x(j + 1, 1 - par)
                if there(j, 1):
                    act.wait_ge(yb_ready, j)
                    if not isinstance(j, int) or j >= 3:
                        act.wait_ge(y_written[1 - par], (j - 1) // 2 * 16 if isinstance(j, int) else j * 8 - (16 if par == 0 else 8))
                    act.activation(y[:, 1 - par, :], yb[:], ACT.Copy).then_inc(y_ready, 1)

            turn_x(0, 0)
            tiles(act, step, 1)

        @block.vector
        def _(dve):
            def step(j, par):
                if there(j, 1):
                    dve.wait_ge(hb_ready, j)
                    dve.wait_ge(yb_ready, j - 1)
                    dve.tensor_copy(hT[:], hb[:]).then_inc(hT_ready, 1)
                if there(j, 0):
                    dve.wait_ge(s_ready, j + 1)
                    dve.wait_ge(b_ready, j + 1)
                    dve.wait_ge(hb_ready, j)
                    dve.tensor_tensor(h[:], bb[:], s[:], ALU.mult).then_inc(h_ready, 1)

            tiles(dve, step, 1)


def first_combine_phase(nc, io, yg, slot, weight, r_all, xb, base, x2):
    with ExitStack() as st:
        p = Mem(nc, st)
        ls2 = p.sb("c1_ls2", [P, D])
        sb_ = p.sb("c1_sb", [P, 3])
        y = p.sb("c1_y", [P, GA, 2, D])
        bs = p.sb("c1_bs", [P, GA, D])
        c1 = p.sb("c1_c1", [P, 2, D])
        c2 = p.sb("c1_c2", [P, 2, D])
        c3 = p.sb("c1_c3", [P, 2, D])
        c4 = p.sb("c1_c4", [P, 2, D])
        halt = p.sb("c1_halt", [P, 2, T])
        rem = p.sb("c1_rem", [P, 2, T])
        w1 = p.sb("c1_w1", [P, T])
        ws = p.sb("c1_ws", [P, 2, T])
        loaded = p.sem("c1_loaded")
        halt_ready = p.sem("c1_halt_ready")
        y_gathered = [p.sem(f"c1_y_gathered{i}") for i in range(GA)]
        bs_loaded = [p.sem(f"c1_bs_loaded{i}") for i in range(GA)]
        c1_ready = p.sem("c1_c1_ready")
        c2_ready = p.sem("c1_c2_ready")
        c3_ready = p.sem("c1_c3_ready")
        c4_ready = p.sem("c1_c4_ready")
        x2_ready = p.sem("c1_x2_ready")
        step = p.sem("c1_step")
        block = st.enter_context(nc.Block())

        @block.sync
        def _(sp):
            sp.dma_start(ls2[:], io["ls2"].partition_broadcast(P)).then_inc(loaded, 16)
            sp.dma_start(sb_[:], io["step_bias"].partition_broadcast(P)).then_inc(loaded, 16)
            for t in range(T):
                if t >= GA:
                    sp.wait_ge(x2_ready, t - GA + 1)
                sp.dma_start(bs[:, t % GA, :], base[:, t, :]).then_inc(bs_loaded[t % GA], 16)

        @block.gpsimd
        def _(pool):
            def gather(t):
                if t >= GA:
                    pool.wait_ge(c2_ready, t - GA + 1)
                for c in range(2):
                    pool.indirect_dma_start(out=y[:, t % GA, c, :], out_offset=None, in_=yg,
                                            in_offset=bass.IndirectOffsetOnAxis(ap=slot[:, c, t:t + 1], axis=0),
                                            ).then_inc(y_gathered[t % GA], 16)

            pool.wait_ge(loaded, 32)
            for t in range(2):
                gather(t)
            for t in range(T):
                if t + 2 < T:
                    gather(t + 2)
                j = t % 2
                pool.wait_ge(c2_ready, t + 1)
                if t >= 2:
                    pool.wait_ge(c4_ready, t - 1)
                pool.tensor_tensor(c3[:, j, :], c2[:, j, :], ls2[:], ALU.mult).then_inc(c3_ready, 1)
                pool.wait_ge(c3_ready, t + 1)
                if t >= 2:
                    pool.wait_ge(x2_ready, t - 1)
                pool.tensor_tensor(c4[:, j, :], c3[:, j, :], xb[:, t, :], ALU.add).then_inc(c4_ready, 1)

        @block.scalar
        def _(act):
            act.wait_ge(loaded, 32)
            for s in range(2):
                act.activation(halt[:, s, :], r_all[:, :, 1], ACT.Sigmoid, bias=sb_[:, s:s + 1]).then_inc(halt_ready, 1)
            for t in range(T):
                act.wait_ge(y_gathered[t % GA], 32 * (t // GA + 1))
                if t >= 2:
                    act.wait_ge(c2_ready, t - 1)
                act.activation(c1[:, t % 2, :], y[:, t % GA, 0, :], ACT.Copy, scale=weight[:, 0, t:t + 1]).then_inc(c1_ready, 1)

        @block.vector
        def _(dve):
            link = Link(dve, step)
            dve.wait_ge(halt_ready, 2)
            link(dve.tensor_scalar(rem[:, 0, :], halt[:, 0, :], -1.0, 1.0, ALU.mult, ALU.add))
            link(dve.tensor_scalar(rem[:, 0, :], rem[:, 0, :], 0.0, None, ALU.max))
            link(dve.tensor_tensor(w1[:], halt[:, 1, :], rem[:, 0, :], ALU.mult))
            link(dve.tensor_tensor(rem[:, 1, :], rem[:, 0, :], w1[:], ALU.subtract))
            link(dve.tensor_scalar(rem[:, 1, :], rem[:, 1, :], 0.0, None, ALU.max))
            link(dve.tensor_tensor(ws[:, 0, :], halt[:, 0, :], w1[:], ALU.add))
            link(dve.tensor_tensor(ws[:, 1, :], ws[:, 0, :], rem[:, 1, :], ALU.add))

            def finish(t):
                dve.wait_ge(c4_ready, t + 1)
                dve.wait_ge(bs_loaded[t % GA], 16 * (t // GA + 1))
                dve.scalar_tensor_tensor(out=x2[:, t, :], in0=c4[:, t % 2, :], scalar=ws[:, 1, t:t + 1],
                                         in1=bs[:, t % GA, :], op0=ALU.mult, op1=ALU.add).then_inc(x2_ready, 1)

            for t in range(T):
                dve.wait_ge(c1_ready, t + 1)
                if t >= 2:
                    dve.wait_ge(c3_ready, t - 1)
                dve.scalar_tensor_tensor(out=c2[:, t % 2, :], in0=y[:, t % GA, 1, :], scalar=weight[:, 1, t:t + 1],
                                         in1=c1[:, t % 2, :], op0=ALU.mult, op1=ALU.add).then_inc(c2_ready, 1)
                if t >= 1:
                    finish(t - 1)
            finish(T - 1)


def second_experts_phase(nc, io, xg, yg):
    ST = CAP // P
    M = F2 // P
    with ExitStack() as st:
        p = Mem(nc, st)
        ident = p.sb("e2_ident", [P, P])
        b1 = p.sb("e2_b1", [P, E, M])
        b2 = p.sb("e2_b2", [P, 2, D])
        w1 = p.sb("e2_w1", [P, 2, 2, F2])
        w2 = p.sb("e2_w2", [P, 2, M, D])
        x = p.sb("e2_x", [P, 2, ST, D])
        xT = p.sb("e2_xT", [P, 2, 2, CAP])
        hT = p.sb("e2_hT", [P, 2, M, CAP])
        y = p.sb("e2_y", [P, 2, ST, D])
        tb = p.ps("e2_tb", [P, 2, CAP])
        hb = p.ps("e2_hb", [P, 2, CAP])
        yb = p.ps("e2_yb", [P, 2, 512])
        loaded = p.sem("e2_loaded")
        w_loaded = [p.sem(f"e2_w_loaded{i}") for i in range(2)]
        x_loaded = [p.sem(f"e2_x_loaded{i}") for i in range(2)]
        y_written = [p.sem(f"e2_y_written{i}") for i in range(2)]
        t_ready = p.sem("e2_t_ready")
        xT_ready = p.sem("e2_xT_ready")
        hb_ready = p.sem("e2_hb_ready")
        hT_ready = p.sem("e2_hT_ready")
        yb_ready = p.sem("e2_yb_ready")
        y_ready = p.sem("e2_y_ready")
        block = st.enter_context(nc.Block())

        def experts(eng, step):
            for e in range(2):
                step(e, e)
            with eng.Fori(1, E // 2 - 1) as i:
                for j in range(2):
                    step(i * 2 + j, j)
            for e in range(E - 2, E):
                step(e, e % 2)

        def static(e):
            return isinstance(e, int)

        def uses(e, par, each):
            return each * (e // 2 + 1) if static(e) else e * (each // 2) + (each if par == 0 else each // 2)

        @block.sync
        def _(sp):
            sp.dma_start(ident[:], io["c_ident"]).then_inc(loaded, 16)
            sp.dma_start(b1[:], io["F_b1"]).then_inc(loaded, 16)

            def load(e, par):
                sp.dma_start(w1[:, par], io["F_W1"][bass.ds(e, 1), :, :].rearrange("a (k p) f -> p (a k) f", p=P)).then_inc(w_loaded[par], 16)
                sp.dma_start(w2[:, par], io["F_W2"][bass.ds(e, 1), :, :].rearrange("a (k p) d -> p (a k) d", p=P)).then_inc(w_loaded[par], 16)
                sp.dma_start(b2[:, par, :], io["F_b2"][bass.ds(e, 1), :].partition_broadcast(P).rearrange("p a d -> p (a d)")).then_inc(w_loaded[par], 16)
                sp.dma_start(x[:, par], xg[bass.ds(e * CAP, CAP), :].rearrange("(s p) d -> p s d", p=P)).then_inc(x_loaded[par], 16)

            for e in range(2):
                load(e, e)

            def step(e, par):
                sp.wait_ge(y_ready, e * ST + ST)
                sp.dma_start(yg[bass.ds(e * CAP, CAP), :].rearrange("(s p) d -> p s d", p=P), y[:, par]).then_inc(y_written[par], 16)
                if not static(e) or e + 2 < E:
                    load(e + 2, par)

            experts(sp, step)
            for c in range(2):
                sp.wait_ge(y_written[c], 16 * E // 2)

        @block.tensor
        def _(pe):
            pe.wait_ge(loaded, 32)

            def turn_x(e, par):
                pe.wait_ge(x_loaded[par], uses(e, par, 16))
                pe.wait_ge(xT_ready, e * 2)
                for k in range(2):
                    for s in range(ST):
                        mm = pe.transpose(tb[:, k, P * s:P * s + P], x[:, par, s, P * k:P * k + P], ident[:])
                    mm.then_inc(t_ready, 1)

            def step(e, par):
                pe.wait_ge(w_loaded[par], uses(e, par, 48))
                pe.wait_ge(xT_ready, e * 2 + 2)
                for f in range(M):
                    if f < 2:
                        pe.wait_ge(hT_ready, e * M)
                    else:
                        pe.wait_ge(hT_ready, e * M + (f - 1))
                    for k in range(2):
                        mm = pe.matmul(hb[:, f % 2, :], w1[:, par, k, P * f:P * f + P], xT[:, par, k, :],
                                       start=(k == 0), stop=(k == 1))
                    mm.then_inc(hb_ready, 1)
                if not static(e) or e + 1 < E:
                    turn_x(e + 1, 1 - par)
                for s in range(ST):
                    pe.wait_ge(hT_ready, e * M + M)
                    if not (static(e) and e == 0 and s < 2):
                        pe.wait_ge(y_ready, e * ST + (s - 1))
                    for f in range(M):
                        mm = pe.matmul(yb[:, s % 2, 0:D], hT[:, par, f, P * s:P * s + P], w2[:, par, f, :],
                                       start=(f == 0), stop=(f == M - 1))
                    mm.then_inc(yb_ready, 1)

            turn_x(0, 0)
            experts(pe, step)

        @block.scalar
        def _(act):
            act.wait_ge(loaded, 32)

            def step(e, par):
                for f in range(M):
                    act.wait_ge(hb_ready, e * M + (f + 1))
                    if f == 0 and not (static(e) and e < 2):
                        act.wait_ge(yb_ready, e * ST - ST)
                    act.activation(hT[:, par, f, :], hb[:, f % 2, :], ACT.Gelu,
                                   bias=b1[:, bass.ds(e, 1), f:f + 1].rearrange("p a b -> p (a b)")).then_inc(hT_ready, 1)

            experts(act, step)

        @block.vector
        def _(dve):
            def turn_x(e, par):
                for k in range(2):
                    dve.wait_ge(t_ready, e * 2 + k + 1)
                    if k == 0 and not (static(e) and e < 2):
                        dve.wait_ge(hb_ready, e * M - M)
                    dve.tensor_copy(xT[:, par, k, :], tb[:, k, :]).then_inc(xT_ready, 1)

            def step(e, par):
                if not static(e) or e + 1 < E:
                    turn_x(e + 1, 1 - par)
                dve.wait_ge(w_loaded[par], uses(e, par, 48))
                if not (static(e) and e < 2):
                    dve.wait_ge(y_written[par], uses(e, par, 16) - 16)
                for s in range(ST):
                    dve.wait_ge(yb_ready, e * ST + (s + 1))
                    dve.tensor_tensor(y[:, par, s, :], yb[:, s % 2, 0:D], b2[:, par, :], ALU.add).then_inc(y_ready, 1)

            turn_x(0, 0)
            experts(dve, step)


def output_phase(nc, io, yg, slot, weight, x2):
    with ExitStack() as st:
        p = Mem(nc, st)
        y = p.sb("o_y", [P, GA, 2, D])
        c1 = p.sb("o_c1", [P, GA, D])
        res = p.sb("o_res", [P, GA, D])
        gathered = [p.sem(f"o_gathered{i}") for i in range(GA)]
        written = [p.sem(f"o_written{i}") for i in range(GA)]
        c1_ready = p.sem("o_c1_ready")
        res_ready = p.sem("o_res_ready")
        block = st.enter_context(nc.Block())
        out = io["out"].rearrange("(t p) d -> p t d", p=P)

        @block.gpsimd
        def _(pool):
            for t in range(T):
                if t >= GA:
                    pool.wait_ge(res_ready, t - GA + 1)
                for c in range(2):
                    pool.indirect_dma_start(out=y[:, t % GA, c, :], out_offset=None, in_=yg,
                                            in_offset=bass.IndirectOffsetOnAxis(ap=slot[:, c, t:t + 1], axis=0),
                                            ).then_inc(gathered[t % GA], 16)

        @block.vector
        def _(dve):
            for t in range(T):
                g = t % GA
                dve.wait_ge(gathered[g], 32 * (t // GA + 1))
                dve.scalar_tensor_tensor(out=c1[:, g, :], in0=y[:, g, 0, :], scalar=weight[:, 0, t:t + 1],
                                         in1=x2[:, t, :], op0=ALU.mult, op1=ALU.add).then_inc(c1_ready, 1)
                dve.wait_ge(c1_ready, t + 1)
                if t >= GA:
                    dve.wait_ge(written[g], 16 * (t // GA))
                dve.scalar_tensor_tensor(out=res[:, g, :], in0=y[:, g, 1, :], scalar=weight[:, 1, t:t + 1],
                                         in1=c1[:, g, :], op0=ALU.mult, op1=ALU.add).then_inc(res_ready, 1)

        @block.sync
        def _(sp):
            for t in range(T):
                sp.wait_ge(res_ready, t + 1)
                sp.dma_start(out[:, t, :], res[:, t % GA, :]).then_inc(written[t % GA], 16)
            for g in range(GA):
                sp.wait_ge(written[g], 16 * (T // GA))


def build_program(nc, io):
    with ExitStack() as st:
        m = Mem(nc, st)
        xg1 = nc.dram_tensor("xg1", (J1 * P, D), F32, kind="Internal").ap()
        yg1 = nc.dram_tensor("yg1", (J1 * P, D), F32, kind="Internal").ap()
        xg2 = nc.dram_tensor("xg2", (2 * N, D), F32, kind="Internal").ap()
        yg2 = nc.dram_tensor("yg2", (2 * N + P, D), F32, kind="Internal").ap()
        base = nc.dram_tensor("base", (P, T, D), F32, kind="Internal").ap()
        zeroed = m.sem("zeroed")
        w_loaded = m.sem("w_loaded")
        base_written = m.sem("base_written")
        xb = m.sb("xb", [P, T, D])
        slot1 = m.sb("slot1", [P, 2, T], I32)
        slot2 = m.sb("slot2", [P, 2, T], I32)
        weight1 = m.sb("weight1", [P, 2, T])
        weight2 = m.sb("weight2", [P, 2, T])
        te = m.sb("te", [1, J1], I32)
        r_all = m.sb("r_all", [P, T, 2])
        alpha = m.sb("alpha", [P, T])
        lg = m.sb("lg", [P, T, E])

        def zero_slots(sp, zero):
            z8 = zero[:].to_broadcast([P, 8, D])
            for buf, tiles in ((xg1, J1), (xg2, 2 * N // P)):
                for i in range(tiles // 8):
                    sp.dma_start(buf[8 * P * i:8 * P * i + 8 * P, :].rearrange("(t p) d -> p t d", p=P),
                                 z8).then_inc(zeroed, 16)
            sp.dma_start(yg2[2 * N:2 * N + P, :], zero[:, 0, :]).then_inc(zeroed, 16)

        NZ = 16 * (J1 // 8 + 2 * N // P // 8 + 1)
        with ExitStack() as s0:
            m0 = Mem(nc, s0)
            nT = m0.sb("nT", [P, 2, N])
            with ExitStack() as s1:
                m1 = Mem(nc, s1)
                xs = m1.sb("xs", [P, T, D])
                oT = m1.sb("oT", [P, 2, N])
                rawsum = m1.sb("rawsum", [P, B * G])
                csum = m1.sb("csum", [P, 2, B])
                qT = m1.sb("qT", [P, 2, N])
                query_phase(nc, io, m1, xs, qT)
                cross_attention_phase(nc, io, m1, qT, oT, rawsum, csum, zero_slots, (zeroed, NZ))
                merge_phase(nc, io, m1, oT, rawsum, csum, xs, xb, nT)
                base_ready = m.sem("base_ready")
                with nc.Block() as block:
                    @block.gpsimd
                    def _(pool):
                        for i in range(4):
                            pool.tensor_tensor(xs[:, 4 * i:4 * i + 4, :], xs[:, 4 * i:4 * i + 4, :],
                                               xb[:, 4 * i:4 * i + 4, :], ALU.add).then_inc(base_ready, 1)

                    @block.sync
                    def _(sp):
                        for i in range(4):
                            sp.wait_ge(base_ready, i + 1)
                            sp.dma_start(base[:, 4 * i:4 * i + 4, :], xs[:, 4 * i:4 * i + 4, :]).then_inc(base_written, 16)
                        sp.wait_ge(base_written, 64)
            w13 = m0.sb("w13", [P, E * 4, F1])
            w2 = m0.sb("w2", [P, E * 4, D])

            def load_experts(sp):
                for e in range(E):
                    for c, name in enumerate(("W1", "W3")):
                        sp.dma_start(w13[:, 4 * e + 2 * c:4 * e + 2 * c + 2, :],
                                     io[name][e].rearrange("(k p) f -> p k f", p=P)).then_inc(w_loaded, 16)
                    sp.dma_start(w2[:, 4 * e:4 * e + 4, :],
                                 io["W2"][e].rearrange("(k p) d -> p k d", p=P)).then_inc(w_loaded, 16)

            with ExitStack() as s2:
                m2 = Mem(nc, s2)
                ssm = m2.sb("ssm", [P, T, D])
                sg = m2.sb("sg", [P, T, D])
                state_space_phase(nc, io, m2, nT, ssm, sg, r_all, load_experts)
                self_attention_phase(nc, io, m2, nT, ssm, sg, r_all, alpha, xb)
            rows = m0.sb("rows1", [P, T, D])
            normed_router_phase(nc, io, "n1_", xb, rows, lg, "Wg", "g2", "b2", "zero8")
            route_phase(nc, io, "r1_", lg, slot1, weight1, te, False)
            scatter_phase(nc, "s1_", rows, slot1, xg1, J1 * P, (zeroed, NZ))
            first_experts_phase(nc, io, xg1, yg1, te, w13, w2, (w_loaded, 16 * 3 * E))
        x2 = m.sb("x2", [P, T, D])
        first_combine_phase(nc, io, yg1, slot1, weight1, r_all, xb, base, x2)
        with ExitStack() as s3:
            m3 = Mem(nc, s3)
            rows = m3.sb("rows2", [P, T, D])
            normed_router_phase(nc, io, "n2_", x2, rows, lg, "F_Wr", "one2", "zero2", "F_br")
            route_phase(nc, io, "r2_", lg, slot2, weight2, None, True)
            scatter_phase(nc, "s2_", rows, slot2, xg2, 2 * N, (zeroed, NZ))
        second_experts_phase(nc, io, xg2, yg2)
        output_phase(nc, io, yg2, slot2, weight2, x2)


def kernel(**inputs):
    import concourse.bacc as bacc
    from concourse.bass_utils import run_bass_kernel_spmd

    a = {k: np.ascontiguousarray(v) for k, v in inputs.items()}
    X, A, Fn = "L0_xattn_", "L0_attn_", "L0_ffn_"

    def by_partition(v):
        return np.ascontiguousarray(v.reshape(2, P).T)

    ctxT = np.ascontiguousarray(a["ctx_768"].transpose(2, 0, 1))
    arrays = {"x": a["x"].reshape(N, D), "ctxT": ctxT, "ctx_last": np.ascontiguousarray(ctxT[:, :, -1])}
    for k in ("Wq", "Wk", "Wv", "Wo", "bo"):
        arrays[k] = a[X + k]
    for k in ("bq", "bk", "bv"):
        arrays[k] = by_partition(a[X + k])
    for k, name in (("g1", "ln1_g"), ("b1", "ln1_b"), ("g2", "ln2_g"), ("b2", "ln2_b"), ("cb", "conv_b")):
        arrays[k] = by_partition(a[A + name])
    for k, name in (("Wzx", "Win_ssm"), ("Wgate", "Wgate"), ("Wr", "Wr"), ("br", "br"), ("Wos", "Wout_ssm"),
                    ("Wout2", "Wout"), ("ls1", "ls1"), ("ls2", "ls2"), ("step_bias", "step_bias"), ("Wg", "Wg"),
                    ("W1", "W1"), ("W2", "W2"), ("W3", "W3")):
        arrays[k] = a[A + name]
    arrays["cw"] = np.ascontiguousarray(a[A + "conv_w"].reshape(2, P, 4).transpose(1, 0, 2))
    arrays["Wqk2"] = np.ascontiguousarray(a[A + "Wqkv"][:, :2 * D])
    arrays["Wv2"] = np.ascontiguousarray(a[A + "Wqkv"][:, 2 * D:])
    for k, name in (("F_Wr", "Wr"), ("F_br", "br"), ("F_W1", "W1"), ("F_W2", "W2"), ("F_b2", "b2")):
        arrays[k] = a[Fn + name]
    arrays["F_b1"] = np.ascontiguousarray(a[Fn + "b1"].reshape(E, F2 // P, P).transpose(2, 0, 1))
    arrays.update(constants())

    nc = bacc.Bacc("TRN2", target_bir_lowering=False, num_devices=1)
    io = {}
    ins = {}
    for name, v in arrays.items():
        ins["in_" + name] = v
        io[name] = nc.dram_tensor("in_" + name, v.shape, mybir.dt.from_np(v.dtype), kind="ExternalInput").ap()
    io["out"] = nc.dram_tensor("out_x", (N, D), F32, kind="ExternalOutput").ap()
    build_program(nc, io)
    r = run_bass_kernel_spmd(nc, [ins], core_ids=[0])
    return r.results[0]["out_x"].reshape(B, L, D)
```

```python
from contextlib import ExitStack

import numpy as np
import concourse.bass as bass
from concourse import mybir

F32 = mybir.dt.float32
I32 = mybir.dt.int32
U32 = mybir.dt.uint32
F32R = mybir.dt.float32r
ALU = mybir.AluOpType
ACT = mybir.ActivationFunctionType
AXX = mybir.AxisListType.X

P = 128
B, L, D = 64, 32, 256
S, DC = 257, 192
H, HD = 16, 16
N = B * L
T = N // P
SE = S + 1
SM = 2 * P
G = 4
CLAMP = 10000.0
SCALE = HD ** -0.5
EPS = 1e-5


class Mem:

    def __init__(self, nc, st, clear=False):
        self.nc, self.st, self.sems = nc, st, []
        if clear:
            st.callback(self.clear)

    def clear(self):
        self.nc.clear_and_free_semaphores(self.sems)
        self.nc.all_engine_barrier()

    def sb(self, name, shape, dt=F32):
        return self.st.enter_context(self.nc.sbuf_tensor(name, shape, dt))

    def ps(self, name, shape, dt=F32):
        return self.st.enter_context(self.nc.psum_tensor(name, shape, dt))

    def sem(self, name):
        self.sems.append(self.nc.alloc_semaphore(name))
        return self.sems[-1]


def rsqrt_refined(dve, rt, r, t, sem, n0, var):
    dve.reciprocal(r, rt).then_inc(sem, 1)
    dve.wait_ge(sem, n0 + 1)
    dve.tensor_tensor(t, r, r, ALU.mult).then_inc(sem, 1)
    dve.wait_ge(sem, n0 + 2)
    dve.tensor_tensor(t, t, var, ALU.mult).then_inc(sem, 1)
    dve.wait_ge(sem, n0 + 3)
    dve.tensor_scalar(t, t, -0.5, 1.5, ALU.mult, ALU.add).then_inc(sem, 1)
    dve.wait_ge(sem, n0 + 4)
    dve.tensor_tensor(r, r, t, ALU.mult).then_inc(sem, 1)
    dve.wait_ge(sem, n0 + 5)


def query_phase(nc, io, m, xs, qs):
    with ExitStack() as st:
        p = Mem(nc, st)
        ident = p.sb("qa_ident", [P, P])
        wq = p.sb("qa_wq", [P, 2, D])
        bq = p.sb("qa_bq", [P, 2])
        stats = p.sb("qa_stats", [P, T, 6])
        mv = p.sb("qa_mv", [P, T, 2])
        ve = p.sb("qa_ve", [P, T])
        rt = p.sb("qa_rt", [P, T])
        rs = p.sb("qa_rs", [P, T])
        tmp = p.sb("qa_tmp", [P, T])
        xn = p.sb("qa_xn", [P, 4, D])
        xnT = p.sb("qa_xnT", [P, 2, 4 * P])
        tp = p.ps("qa_tp", [P, 2, 4 * P])
        qp = p.ps("qa_qp", [P, 2, 4 * P])
        x_loaded = p.sem("qa_x_loaded")
        w_loaded = p.sem("qa_w_loaded")
        step = p.sem("qa_step")
        var_ready = p.sem("qa_var_ready")
        sqrt_ready = p.sem("qa_sqrt_ready")
        xn_ready = p.sem("qa_xn_ready")
        tp_ready = p.sem("qa_tp_ready")
        xnT_ready = p.sem("qa_xnT_ready")
        qp_ready = p.sem("qa_qp_ready")
        q_stored = p.sem("qa_q_stored")
        rest_stored = p.sem("qa_rest_stored")
        block = st.enter_context(nc.Block())

        @block.sync
        def _(sp):
            for c in range(4):
                sp.dma_start(xs[:, 4 * c:4 * c + 4, :],
                             io["x"].rearrange("(t p) d -> p t d", p=P)[:, 4 * c:4 * c + 4, :]).then_inc(x_loaded, 16)
            sp.dma_start(wq[:], io["Wq"].rearrange("(k p) m -> p k m", p=P)).then_inc(w_loaded, 16)
            sp.dma_start(bq[:], io["bq"]).then_inc(w_loaded, 16)
            sp.dma_start(ident[:], io["c_ident"]).then_inc(w_loaded, 16)

        @block.vector
        def _(dve):
            dve.wait_ge(x_loaded, 64)
            for t in range(T):
                dve.bn_stats(stats[:, t, :], xs[:, t, :]).then_inc(step, 1)
            for t in range(T):
                dve.wait_ge(step, t + 1)
                dve.bn_aggr(mv[:, t, :], stats[:, t, :]).then_inc(step, 1)
            dve.wait_ge(step, 2 * T)
            dve.tensor_scalar(ve[:], mv[:, :, 1], EPS, None, ALU.add).then_inc(var_ready, 1)
            dve.wait_ge(sqrt_ready, 1)
            rsqrt_refined(dve, rt[:], rs[:], tmp[:], step, 2 * T, ve[:])

            def rest(c):
                for h in range(2):
                    dve.wait_ge(q_stored, 2 * c + h + 1)
                    part = [qs[:, a, h, 512 * c:512 * c + 512] for a in range(2)]
                    dve.scalar_tensor_tensor(out=part[1], in0=qp[:, h, :], scalar=bq[:, h:h + 1], in1=part[0],
                                             op0=ALU.add, op1=ALU.subtract).then_inc(rest_stored, 1)

            for c in range(4):
                for j in range(4):
                    t = 4 * c + j
                    if c:
                        dve.wait_ge(tp_ready, 2 * c)
                    dve.tensor_scalar(xn[:, j, :], xs[:, t, :], mv[:, t, 0:1], rs[:, t:t + 1],
                                      ALU.subtract, ALU.mult).then_inc(xn_ready, 1)
                if c:
                    dve.wait_ge(qp_ready, 2 * c)
                for k in range(2):
                    dve.wait_ge(tp_ready, 2 * c + k + 1)
                    dve.tensor_copy(xnT[:, k, :], tp[:, k, :]).then_inc(xnT_ready, 1)
                if c:
                    rest(c - 1)
            rest(3)

        @block.scalar
        def _(act):
            act.wait_ge(var_ready, 1)
            act.activation(rt[:], ve[:], ACT.Sqrt).then_inc(sqrt_ready, 1)
            act.wait_ge(w_loaded, 48)
            for c in range(4):
                for h in range(2):
                    act.wait_ge(qp_ready, 2 * c + h + 1)
                    act.activation(qs[:, 0, h, 512 * c:512 * c + 512], qp[:, h, :], ACT.Identity,
                                   bias=bq[:, h:h + 1]).then_inc(q_stored, 1)

        @block.tensor
        def _(pe):
            pe.wait_ge(w_loaded, 48)
            for c in range(4):
                if c:
                    pe.wait_ge(xnT_ready, 2 * c)
                pe.wait_ge(xn_ready, 4 * c + 4)
                for k in range(2):
                    for j in range(4):
                        mm = pe.transpose(tp[:, k, P * j:P * j + P], xn[:, j, P * k:P * k + P], ident[:])
                    mm.then_inc(tp_ready, 1)
                pe.wait_ge(xnT_ready, 2 * c + 2)
                if c:
                    pe.wait_ge(q_stored, 2 * c)
                    pe.wait_ge(rest_stored, 2 * c)
                for h in range(2):
                    for k in range(2):
                        mm = pe.matmul(qp[:, h, :], wq[:, k, P * h:P * h + P], xnT[:, k, :],
                                       start=(k == 0), stop=(k == 1))
                    mm.then_inc(qp_ready, 1)


def cross_attention_phase(nc, io, m, xs, qs, oT, rawsum, csum, zero_slots, zeroed):
    with ExitStack() as st:
        p = Mem(nc, st, clear=True)
        ident = p.sb("xa_ident", [P, P])
        zero = p.sb("xa_zero", [P, 1, D])
        istack = p.sb("xa_istack", [P, L])
        mask8 = p.sb("xa_mask8", [P, 8])
        mask64 = p.sb("xa_mask64", [P, 64])
        wk = p.sb("xa_wk", [P, 2, D])
        wv = p.sb("xa_wv", [P, 2, D])
        wks = p.sb("xa_wks", [P, 3, D], F32R)
        wvs = p.sb("xa_wvs", [P, 3, D], F32R)
        bk = p.sb("xa_bk", [P, 2])
        bo = p.sb("xa_bo", [P, D])
        pad = p.sb("xa_pad", [P, 8])
        floor = p.sb("xa_floor", [P, 1])
        cl = p.sb("xa_cl", [P, 2, B])
        vl = p.sb("xa_vl", [B, D])
        vlast = p.sb("xa_vlast", [G, B, G * 65])
        ctx = p.sb("xa_ctx", [P, 2, 2, 2, S])
        cs = p.sb("xa_cs", [P, 2, 2, 2, SE], F32R)
        kT = p.sb("xa_kT", [P, 2, 2, 2, SE], F32R)
        v = p.sb("xa_v", [P, 4, 2, G, 65])
        qbd = p.sb("xa_qbd", [P, 2, 2, G, P], F32R)
        mx = p.sb("xa_mx", [P, 2, G])
        nm = p.sb("xa_nm", [P, 2, G])
        low = p.sb("xa_low", [P, 2, G])
        pr = p.sb("xa_pr", [P, 2, G, S])
        pT = p.sb("xa_pT", [P, 2, G, 2, P])
        pTl = p.sb("xa_pTl", [G, 2, P])
        unused = p.sb("xa_unused", [P, 2, S])
        rinv = p.sb("xa_rinv", [P, 2, G])
        om = p.sb("xa_om", [P, D])
        on = p.sb("xa_on", [P, D])
        kvp = p.ps("xa_kvp", [P, 2, 512])
        sc = p.ps("xa_sc", [P, G, 512])
        ptp = p.ps("xa_ptp", [P, 512])
        ob = p.ps("xa_ob", [P, 512])
        OT, PL = 260, 324

        w_loaded = p.sem("xa_w_loaded")
        cl_loaded = p.sem("xa_cl_loaded")
        bo_loaded = p.sem("xa_bo_loaded")
        xb_ready = p.sem("xa_xb_ready")
        zero_set = p.sem("xa_zero_set")
        ctx_loaded = [p.sem(f"xa_ctx_loaded{i}") for i in range(2)]
        vlp_ready = p.sem("xa_vlp_ready")
        vl_ready = p.sem("xa_vl_ready")
        vlast_loaded = p.sem("xa_vlast_loaded")
        vlast_ready = p.sem("xa_vlast_ready")
        ones_ready = p.sem("xa_ones_ready")
        floor_ready = p.sem("xa_floor_ready")
        kp_ready = p.sem("xa_kp_ready")
        kh_ready = p.sem("xa_kh_ready")
        kl_ready = p.sem("xa_kl_ready")
        wh_ready = p.sem("xa_wh_ready")
        wl_ready = p.sem("xa_wl_ready")
        pad_ready = p.sem("xa_pad_ready")
        ch_pad_ready = p.sem("xa_ch_pad_ready")
        ch_ready = p.sem("xa_ch_ready")
        cr_ready = p.sem("xa_cr_ready")
        vp_ready = p.sem("xa_vp_ready")
        v_ready = p.sem("xa_v_ready")
        q_ready = p.sem("xa_q_ready")
        s_ready = p.sem("xa_s_ready")
        mx_step = p.sem("xa_mx_step")
        nm_ready = p.sem("xa_nm_ready")
        exp_ready = p.sem("xa_exp_ready")
        low_ready = p.sem("xa_low_ready")
        pr_ready = p.sem("xa_pr_ready")
        ptp_ready = p.sem("xa_ptp_ready")
        plp_ready = p.sem("xa_plp_ready")
        pT_ready = p.sem("xa_pT_ready")
        pTl_ready = p.sem("xa_pTl_ready")
        o_ready = p.sem("xa_o_ready")
        rinv_ready = p.sem("xa_rinv_ready")
        om_ready = p.sem("xa_om_ready")
        on_ready = p.sem("xa_on_ready")
        oTp_ready = p.sem("xa_oTp_ready")
        oT_stored = p.sem("xa_oT_stored")
        csum_ready = p.sem("xa_csum_ready")
        block = st.enter_context(nc.Block())

        def run_steps(eng, step, first, last):
            for b in range(first, 4):
                step(b, b % 2, b // 2)
            with eng.Fori(1, B // 4 - 1) as i:
                for j in range(4):
                    step(i * 4 + j, j % 2, j // 2)
            for b in range(B - 4, last):
                step(b, b % 2, b // 2 % 2)

        @block.sync
        def _(sp):
            for dst, name in ((wk, "Wk"), (wv, "Wv")):
                sp.dma_start(dst[:, 0, :], io[name][0:P, :]).then_inc(w_loaded, 16)
                for r in (0, 64):
                    sp.dma_start(dst[r:r + 64, 1, :], io[name][P:DC, :]).then_inc(w_loaded, 16)
            sp.dma_start(bk[:], io["bk"]).then_inc(w_loaded, 16)
            sp.dma_start(ident[:], io["c_ident"]).then_inc(w_loaded, 16)
            sp.dma_start(istack[:], io["c_istack"]).then_inc(w_loaded, 16)
            sp.dma_start(mask8[:], io["c_mask8s"]).then_inc(w_loaded, 16)
            sp.dma_start(mask64[:], io["c_mask64"]).then_inc(w_loaded, 16)
            sp.dma_start(bo[:], io["bo"].partition_broadcast(P)).then_inc(bo_loaded, 16)
            sp.dma_start(cl[:, 0, :], io["ctx_last"][0:P, :]).then_inc(cl_loaded, 16)
            sp.dma_start(cl[0:64, 1, :], io["ctx_last"][P:DC, :]).then_inc(cl_loaded, 16)

            def load(i, slot):
                sp.dma_start(ctx[:, slot, 0, :, :], io["ctxT"][0:P, bass.ds(i * 2, 2), :]).then_inc(ctx_loaded[slot], 16)
                for r in (0, 64):
                    sp.dma_start(ctx[r:r + 64, slot, 1, :, :],
                                 io["ctxT"][P:DC, bass.ds(i * 2, 2), :]).then_inc(ctx_loaded[slot], 16)

            load(0, 0)
            load(1, 1)
            sp.dma_start(vlast[:], io["c_vlast"]).then_inc(vlast_loaded, 16)
            sp.wait_ge(vl_ready, 1)
            sp.wait_ge(vlast_loaded, 16)
            for g in range(G):
                sp.dma_start(vlast[g:g + 1, :, 65 * g:65 * g + 64],
                             vl[:, 64 * g:64 * g + 64]).then_inc(vlast_ready, 16)
            sp.wait_ge(zero_set, 1)
            zero_slots(sp, zero)
            with sp.Fori(1, B // 4) as i:
                for j in range(2):
                    sp.wait_ge(cr_ready, i * 4 + (2 * j - 2))
                    sp.wait_ge(csum_ready, i * 8 + (4 * j - 4))
                    load(i * 2 + j, j)
            sp.wait_ge(*zeroed)

        @block.tensor
        def _(pe):
            pe.wait_ge(w_loaded, 16 * 11)
            pe.wait_ge(cl_loaded, 32)
            pe.matmul(ptp[0:B, 0:D], cl[:, 0, :], wv[:, 0, :], start=True, stop=False)
            pe.matmul(ptp[0:B, 0:D], cl[0:64, 1, :], wv[0:64, 1, :], start=False, stop=True).then_inc(vlp_ready, 1)

            def project_k(b, par):
                pe.wait_ge(ch_ready, b + 1)
                pe.wait_ge(cr_ready, b + 1)
                high, rest = cs[:, par, 0], cs[:, par, 1]
                for h in range(2):
                    if h == 0:
                        pe.wait_ge(kh_ready, b * 2)
                        pe.wait_ge(kl_ready, b * 2)
                    else:
                        pe.wait_ge(v_ready, b)
                    out, c = kvp[:, (par + h) % 2, 0:SE], slice(P * h, P * h + P)
                    pe.matmul(out, wks[:, 0, c], high[:, 0, :], start=True, stop=False)
                    pe.matmul(out, wks[:, 0, c], rest[:, 0, :], start=False, stop=False)
                    pe.matmul(out, wks[:, 1, c], high[:, 0, :], start=False, stop=False)
                    pe.matmul(out, wks[:, 2, c], high[:, 1, :], start=False, stop=False)
                    pe.matmul(out, wks[0:64, 2, c], rest[0:64, 1, :], start=False, stop=True).then_inc(kp_ready, 1)

            def project_v(b, par, tiles):
                pe.wait_ge(kh_ready, b * 2 + 1)
                pe.wait_ge(kl_ready, b * 2 + 1)
                for t in tiles:
                    out = kvp[:, par, D * t:D * t + D]
                    high, rest = [[cs[:, par, a, k, P * t:P * t + P] for k in range(2)] for a in range(2)]
                    pe.matmul(out, high[0], wvs[:, 0, :], start=True, stop=False)
                    pe.matmul(out, rest[0], wvs[:, 0, :], start=False, stop=False)
                    pe.matmul(out, high[0], wvs[:, 1, :], start=False, stop=False)
                    pe.matmul(out, high[1], wvs[:, 2, :], start=False, stop=False)
                    mm = pe.matmul(out, rest[1][0:64], wvs[0:64, 2, :], start=False, stop=True)
                if t == 1:
                    mm.then_inc(vp_ready, 1)

            def scores(b, par):
                pe.wait_ge(q_ready, b * 2 + 2)
                for h in range(2):
                    pe.wait_ge(kh_ready, b * 2 + h + 1)
                    pe.wait_ge(kl_ready, b * 2 + h + 1)
                    if not (isinstance(b, int) and b == 0):
                        pe.wait_ge(exp_ready, b * 4 + (2 * h - 2))
                    for g in (2 * h, 2 * h + 1):
                        out = sc[:, g, 0:SE]
                        pe.matmul(out, qbd[:, par, 0, g, :], kT[:, par, 0, h, :], start=True, stop=False)
                        pe.matmul(out, qbd[:, par, 0, g, :], kT[:, par, 1, h, :], start=False, stop=False)
                        mm = pe.matmul(out, qbd[:, par, 1, g, :], kT[:, par, 0, h, :], start=False, stop=True)
                    mm.then_inc(s_ready, 1)

            def turn(b, par, h):
                pe.wait_ge(pr_ready, b * 4 + (2 * h + 2))
                if h == 1:
                    if not (isinstance(b, int) and b == 0):
                        pe.wait_ge(om_ready, b)
                    pe.transpose(ob[0:G, PL:PL + P], pr[:, par, :, S - 1], ident[:]).then_inc(plp_ready, 1)
                pe.wait_ge(pT_ready, b * 2 + h)
                for g in (2 * h, 2 * h + 1):
                    for t in range(2):
                        c = (2 * (g % 2) + t) * P
                        mm = pe.transpose(ptp[:, c:c + P], pr[:, par, g, P * t:P * t + P], ident[:])
                mm.then_inc(ptp_ready, 1)

            def values(b, par, vs):
                pe.wait_ge(pTl_ready, b + 1)
                pe.wait_ge(v_ready, b + 1)
                if not (isinstance(b, int) and b == 0):
                    pe.wait_ge(oT_stored, b)
                pe.matmul(ob[:, 0:G * 65], pTl[:, par, :], vlast[:, b, :], start=True, stop=False, skip_group_check=True)
                pe.wait_ge(pT_ready, b * 2 + 2)
                for g in range(G):
                    for t in range(2):
                        mm = pe.matmul(ob[:, 65 * g:65 * g + 65], pT[:, par, g, t, :], v[:, vs, t, g, :],
                                       start=False, stop=(g == G - 1 and t == 1), skip_group_check=True)
                mm.then_inc(o_ready, 1)

            def turn_output(b, par):
                pe.wait_ge(on_ready, b + 1)
                if not (isinstance(b, int) and b == B - 1):
                    pe.wait_ge(pTl_ready, b + 2)
                for h in range(2):
                    mm = pe.matmul(ob[:, OT + L * h:OT + L * h + L], on[:, P * h:P * h + P], istack[:],
                                   start=True, stop=True, skip_group_check=True)
                mm.then_inc(oTp_ready, 1)

            def step(b, par, slot):
                static = isinstance(b, int)
                scores(b, par)
                if not static or b >= 1:
                    turn(b - 1, 1 - par, 0)
                if not static or b < B - 1:
                    project_k(b + 1, 1 - par)
                if not static or b >= 1:
                    turn(b - 1, 1 - par, 1)
                if not static or b < B - 1:
                    project_v(b + 1, 1 - par, (0,))
                if not static or b >= 2:
                    turn_output(b - 2, par)
                if not static or b < B - 1:
                    project_v(b + 1, 1 - par, (1,))
                if not static or b >= 1:
                    values(b - 1, 1 - par, (2 * slot + par + 3) % 4)

            pe.wait_ge(wh_ready, 4)
            pe.wait_ge(wl_ready, 4)
            project_k(0, 0)
            pe.wait_ge(vlast_ready, 64)
            project_v(0, 0, (0, 1))
            run_steps(pe, step, 0, B)
            turn(B - 1, 1, 0)
            turn(B - 1, 1, 1)
            turn_output(B - 2, 0)
            values(B - 1, 1, 3)
            turn_output(B - 1, 1)

        @block.gpsimd
        def _(pool):
            pool.memset(floor[:], -CLAMP).then_inc(floor_ready, 1)
            pool.memset(zero[:], 0.0).then_inc(zero_set, 1)
            for i in range(4):
                pool.memset(v[:, i, :, :, 64], 1.0).then_inc(ones_ready, 1)
            pool.memset(pad[:], 0.0).then_inc(pad_ready, 1)
            pool.wait_ge(w_loaded, 16 * 11)

            def queries(b, par):
                if not (isinstance(b, int) and b < 2):
                    pool.wait_ge(s_ready, b * 2 - 2)
                msk = mask8[:].unsqueeze(1).unsqueeze(3).to_broadcast([P, 2, 8, L])
                for a in range(2):
                    src = qs[:, a, :, bass.ds(b * L, L)].unsqueeze(2).to_broadcast([P, 2, 8, L])
                    dst = qbd[:, par, a].rearrange("p (h j) (e q) -> p h (j e) q", h=2, q=L)
                    pool.tensor_tensor(dst, src, msk, ALU.mult).then_inc(q_ready, 1)

            def rest_of_context(b, par, slot):
                pool.wait_ge(ch_ready, b + 1)
                pool.tensor_tensor(cs[:, par, 1, :, 0:S], ctx[:, slot, :, par, :], cs[:, par, 0, :, 0:S],
                                   ALU.subtract).then_inc(cr_ready, 1)

            def normalise(b, par):
                pool.wait_ge(rinv_ready, b + 1)
                pool.wait_ge(om_ready, b + 1)
                pool.wait_ge(oTp_ready, b)
                pool.tensor_tensor(on[:].rearrange("p (g c) -> p g c", g=G),
                                   om[:].rearrange("p (g c) -> p g c", g=G),
                                   rinv[:, par, :].unsqueeze(2).to_broadcast([P, G, 64]),
                                   ALU.mult).then_inc(on_ready, 1)

            def step(b, par, slot):
                static = isinstance(b, int)
                if not static or b < B - 1:
                    queries(b + 1, 1 - par)
                if not static or b >= 2:
                    normalise(b - 2, par)
                if not static or b < B - 2:
                    rest_of_context(b + 2, par, 1 - slot)
                if static and b < 4:
                    if b == 0:
                        pool.wait_ge(bo_loaded, 16)
                    x = xs[:, T // 4 * b:T // 4 * b + T // 4, :]
                    pool.tensor_tensor(x, x, bo[:].unsqueeze(1).to_broadcast([P, T // 4, D]), ALU.add).then_inc(xb_ready, 1)

            queries(0, 0)
            for b in range(2):
                rest_of_context(b, b, 0)
            run_steps(pool, step, 0, B)
            normalise(B - 2, 0)
            normalise(B - 1, 1)

        @block.scalar
        def _(act):
            act.wait_ge(w_loaded, 16 * 11)
            act.wait_ge(floor_ready, 1)

            def high_k(b, par, h):
                if not (isinstance(b, int) and b < 2):
                    act.wait_ge(s_ready, b * 2 - 2)
                act.wait_ge(kp_ready, b * 2 + h + 1)
                act.activation(kT[:, par, 0, h, :], kvp[:, (par + h) % 2, 0:SE], ACT.Identity,
                               bias=bk[:, h:h + 1]).then_inc(kh_ready, 1)

            def high_context(b, par, slot):
                if isinstance(b, int):
                    act.wait_ge(ctx_loaded[slot], 48 * (b // 4 + 1))
                elif par == 0:
                    act.wait_ge(ctx_loaded[slot], b * 12 + (48 if slot == 0 else 24))
                if not (isinstance(b, int) and b < 2):
                    act.wait_ge(vp_ready, b - 1)
                act.activation(cs[:, par, 0, :, 0:S], ctx[:, slot, :, par, :], ACT.Copy).then_inc(ch_ready, 1)
                if not (isinstance(b, int) and b == 0):
                    act.wait_ge(csum_ready, b * 2)
                sum_context(b, par, slot)

            def sum_context(b, par, slot):
                for k, rows in ((0, P), (1, 64)):
                    act.activation(unused[0:rows, k, :], ctx[0:rows, slot, k, par, :], ACT.Copy,
                                   accum_out=csum[0:rows, k, bass.ds(b, 1)]).then_inc(csum_ready, 1)

            def floors(b, par, h):
                act.wait_ge(nm_ready, b * 2 + h + 1)
                if not (isinstance(b, int) and b < 2):
                    act.wait_ge(pr_ready, b * 4 - 4)
                act.activation(low[:, par, 2 * h:2 * h + 2], nm[:, par, 2 * h:2 * h + 2], ACT.Exp,
                               bias=floor[:]).then_inc(low_ready, 1)

            def exponentials(b, par, h):
                if h == 0 and not (isinstance(b, int) and b < 2):
                    act.wait_ge(plp_ready, b - 1)
                for g in (2 * h, 2 * h + 1):
                    act.activation(pr[:, par, g, :], sc[:, g, 0:S], ACT.Exp, bias=nm[:, par, g:g + 1],
                                   scale=-1.0, accum_out=rawsum[:, bass.ds(b * G + g, 1)]).then_inc(exp_ready, 1)

            def step(b, par, slot):
                static = isinstance(b, int)
                floors(b, par, 0)
                if not static or b < B - 1:
                    high_k(b + 1, 1 - par, 0)
                exponentials(b, par, 0)
                if not static or b < B - 1:
                    high_k(b + 1, 1 - par, 1)
                floors(b, par, 1)
                exponentials(b, par, 1)
                if not static or b < B - 2:
                    high_context(b + 2, par, 1 - slot)

            for w, ws in ((wk, wks), (wv, wvs)):
                for k in range(2):
                    act.activation(ws[:, 2 * k, :], w[:, k, :], ACT.Copy).then_inc(wh_ready, 1)
            act.wait_ge(pad_ready, 1)
            act.activation(cs[:, :, :, :, S].rearrange("p a b c -> p (a b c)"), pad[:], ACT.Copy).then_inc(ch_pad_ready, 1)
            for b in range(2):
                high_context(b, b, 0)
            high_k(0, 0, 0)
            high_k(0, 0, 1)
            run_steps(act, step, 0, B)

        @block.vector
        def _(dve):
            dve.wait_ge(w_loaded, 16 * 11)
            dve.wait_ge(ones_ready, 4)
            dve.wait_ge(vlp_ready, 1)
            dve.tensor_copy(vl[:], ptp[0:B, 0:D]).then_inc(vl_ready, 1)

            for n, (w, ws) in enumerate(((wk, wks), (wv, wvs))):
                dve.wait_ge(wh_ready, 2 * n + 2)
                dve.tensor_tensor(ws[:, 1, :], w[:, 0, :], ws[:, 0, :], ALU.subtract).then_inc(wl_ready, 1)
                dve.tensor_tensor(ws[64:P, 2, :], w[64:P, 1, :], ws[64:P, 2, :], ALU.subtract).then_inc(wl_ready, 1)

            def rest_k(b, par, h):
                dve.wait_ge(kh_ready, b * 2 + h + 1)
                dve.scalar_tensor_tensor(out=kT[:, par, 1, h, :], in0=kvp[:, (par + h) % 2, 0:SE], scalar=bk[:, h:h + 1],
                                         in1=kT[:, par, 0, h, :], op0=ALU.add, op1=ALU.subtract).then_inc(kl_ready, 1)

            def store_v(b, par, vs):
                dve.wait_ge(vp_ready, b + 1)
                if not (isinstance(b, int) and b < 4):
                    dve.wait_ge(o_ready, b - 3)
                dve.tensor_copy(v[:, vs, :, :, 0:64], kvp[:, par, :].rearrange("p (t g c) -> p t g c", t=2, g=G)
                                ).then_inc(v_ready, 1)

            def least(b, par, h):
                g = slice(2 * h, 2 * h + 2)
                dve.wait_ge(s_ready, b * 2 + h + 1)
                dve.tensor_reduce(mx[:, par, g], sc[:, g, 0:S], AXX, ALU.min).then_inc(mx_step, 1)

            def bounds(b, par, h):
                g = slice(2 * h, 2 * h + 2)
                dve.wait_ge(mx_step, b * 2 + h + 1)
                if not (isinstance(b, int) and b < 2):
                    dve.wait_ge(low_ready, b * 2 + (h - 3))
                dve.tensor_scalar(nm[:, par, g], mx[:, par, g], -CLAMP, CLAMP, ALU.max, ALU.min).then_inc(nm_ready, 1)

            def store_probabilities(b, par, h):
                if h == 1:
                    dve.wait_ge(plp_ready, b + 1)
                    dve.tensor_copy(pTl[:, par, :], ob[0:G, PL:PL + P]).then_inc(pTl_ready, 1)
                dve.wait_ge(ptp_ready, b * 2 + h + 1)
                dve.tensor_copy(pT[:, par, 2 * h:2 * h + 2].rearrange("p g t c -> p (g t c)"),
                                ptp[:]).then_inc(pT_ready, 1)

            def clamp(b, par, h):
                dve.wait_ge(low_ready, b * 2 + h + 1)
                for g in (2 * h, 2 * h + 1):
                    dve.wait_ge(exp_ready, b * 4 + (g + 1))
                    dve.tensor_scalar(pr[:, par, g, :], pr[:, par, g, :], 1.0, low[:, par, g:g + 1],
                                       ALU.min, ALU.max).then_inc(pr_ready, 1)

            def mask_output(b, par):
                dve.wait_ge(o_ready, b + 1)
                dve.wait_ge(on_ready, b)
                o = ob[:, 0:G * 65].rearrange("p (g c) -> p g c", g=G)
                dve.reciprocal(rinv[:, par, :], o[:, :, 64]).then_inc(rinv_ready, 1)
                dve.tensor_tensor(om[:].rearrange("p (g c) -> p g c", g=G), o[:, :, 0:64],
                                  mask64[:].unsqueeze(1).to_broadcast([P, G, 64]), ALU.mult).then_inc(om_ready, 1)

            def store_output(b):
                dve.wait_ge(oTp_ready, b + 1)
                dve.tensor_copy(oT[:, :, bass.ds(b * L, L)],
                                ob[:, OT:OT + 2 * L].rearrange("p (h q) -> p h q", h=2)).then_inc(oT_stored, 1)

            def step(b, par, slot):
                static = isinstance(b, int)
                if not static or b >= 2:
                    mask_output(b - 2, par)
                least(b, par, 0)
                bounds(b, par, 0)
                if not static or b >= 1:
                    store_probabilities(b - 1, 1 - par, 0)
                least(b, par, 1)
                if not static or b < B - 1:
                    rest_k(b + 1, 1 - par, 0)
                bounds(b, par, 1)
                if not static or b >= 1:
                    store_probabilities(b - 1, 1 - par, 1)
                if not static or b >= 2:
                    store_output(b - 2)
                if not static or b < B - 1:
                    rest_k(b + 1, 1 - par, 1)
                clamp(b, par, 0)
                if not static or b < B - 1:
                    store_v(b + 1, 1 - par, (2 * slot + par + 1) % 4)
                clamp(b, par, 1)

            rest_k(0, 0, 0)
            rest_k(0, 0, 1)
            store_v(0, 0, 0)
            run_steps(dve, step, 0, B)
            mask_output(B - 2, 0)
            store_probabilities(B - 1, 1, 0)
            store_probabilities(B - 1, 1, 1)
            store_output(B - 2)
            mask_output(B - 1, 1)
            store_output(B - 1)


def constants():
    p = np.arange(P)
    vl = np.zeros((G, B, G * 65), np.float32)
    for g in range(G):
        vl[g, :, 65 * g + 64] = 1.0
    return {
        "c_ident": np.eye(P, dtype=np.float32),
        "c_istack": (p[:, None] % L == np.arange(L)).astype(np.float32),
        "c_mask8": (p[:, None] // HD == np.arange(8)).astype(np.float32),
        "c_mask8s": -SCALE * (p[:, None] // HD == np.arange(8)).astype(np.float32),
        "c_mask64": (p[:, None] // L == np.arange(64) // HD).astype(np.float32),
        "c_mask4": (p[:, None] // L == np.arange(4)).astype(np.float32),
        "c_onesr": np.ones((1, P), np.float32),
        "c_tri": (p[:, None] < p).astype(np.float32),
        "c_ones": np.ones((P, P), np.float32),
        "c_reset": np.tile((p % T != 0).astype(np.float32), (P, 1)),
        "c_iota": np.tile(np.arange(8, dtype=np.float32), (P, 1)),
        "c_steps": np.tile(P * np.arange(T, dtype=np.float32), (P, 1)),
        "c_tiles": np.tile(np.arange(40, dtype=np.float32), (P, 1)),
        "c_first": np.tile(512 * np.arange(8, dtype=np.float32), (P, 1)),
        "one2": np.ones((P, 2), np.float32),
        "zero2": np.zeros((P, 2), np.float32),
        "zero8": np.zeros((8,), np.float32),
        "c_vlast": vl,
    }



V2 = 2 * P
NS = N // V2
BS = V2 // L


class Link:

    def __init__(self, eng, sem, base=0):
        self.eng, self.sem, self.base, self.n = eng, sem, base, 0

    def __call__(self, ins):
        self.n += 1
        ins.then_inc(self.sem, 1)
        self.eng.wait_ge(self.sem, self.base + self.n)


def refine(dve, link, ve, rt, rs, tmp):
    link(dve.reciprocal(rs, rt))
    link(dve.tensor_tensor(tmp, rs, rs, ALU.mult))
    link(dve.tensor_tensor(tmp, tmp, ve, ALU.mult))
    link(dve.tensor_scalar(tmp, tmp, -0.5, 1.5, ALU.mult, ALU.add))
    link(dve.tensor_tensor(rs, rs, tmp, ALU.mult))


def merge_phase(nc, io, m, oT, rawsum, csum, xs, xin, nT, base, base_written):
    with ExitStack() as st:
        p = Mem(nc, st)
        ident = p.sb("mg_ident", [P, P])
        onesr = p.sb("mg_onesr", [1, P])
        wv = p.sb("mg_wv", [P, 2, D])
        wo = p.sb("mg_wo", [P, 2, D])
        bv = p.sb("mg_bv", [P, 2])
        g1 = p.sb("mg_g1", [P, 2])
        b1 = p.sb("mg_b1", [P, 2])
        same = p.sb("mg_same", [P, B * G])
        ok = p.sb("mg_ok", [P, 1])
        ok1 = p.sb("mg_ok1", [1, 1])
        bad = p.sb("mg_bad", [P, 1], U32)
        mean = p.sb("mg_mean", [P, 2, B])
        ost = p.sb("mg_ost", [P, 2, 2, V2])
        stats = p.sb("mg_stats", [P, T, 6])
        mv = p.sb("mg_mv", [P, T, 2])
        ve = p.sb("mg_ve", [P, T])
        rt = p.sb("mg_rt", [P, T])
        rs = p.sb("mg_rs", [P, T])
        tmp = p.sb("mg_tmp", [P, T])
        xh = p.sb("mg_xh", [P, 2, 2, D])
        fp = p.ps("mg_fp", [P, 512])
        xo = p.ps("mg_xo", [P, 2, 2, D])
        tp = p.ps("mg_tp", [P, 2, 2, V2])
        loaded = p.sem("mg_loaded")
        guarded = p.sem("mg_guarded")
        xin_ready = p.sem("mg_xin_ready")
        base_ready = p.sem("mg_base_ready")
        okT_ready = p.sem("mg_okT_ready")
        mean_ready = p.sem("mg_mean_ready")
        ok_ready = p.sem("mg_ok_ready")
        okb_ready = p.sem("mg_okb_ready")
        ost_ready = p.sem("mg_ost_ready")
        xo_ready = p.sem("mg_xo_ready")
        xo_free = p.sem("mg_xo_free")
        var_ready = p.sem("mg_var_ready")
        sqrt_ready = p.sem("mg_sqrt_ready")
        xh_ready = p.sem("mg_xh_ready")
        tp_ready = p.sem("mg_tp_ready")
        nT_stored = p.sem("mg_nT_stored")
        step = p.sem("mg_step")
        block = st.enter_context(nc.Block())
        NLOAD = 8

        @block.sync
        def _(sp):
            for dst, src in ((ident[:], io["c_ident"]), (onesr[:], io["c_onesr"]), (wv[:, 0, :], io["Wv"][0:P, :]),
                             (wv[0:64, 1, :], io["Wv"][P:DC, :]), (wo[:], io["Wo"].rearrange("(k p) m -> p k m", p=P)),
                             (bv[:], io["bv"]), (g1[:], io["g1"]), (b1[:], io["b1"])):
                sp.dma_start(dst, src).then_inc(loaded, 16)
            for i in range(4):
                sp.wait_ge(base_ready, i + 1)
                sp.dma_start(base[:, 4 * i:4 * i + 4, :], xs[:, 4 * i:4 * i + 4, :]).then_inc(base_written, 16)
            sp.wait_ge(base_written, 64)

        @block.gpsimd
        def _(pool):
            for i in range(4):
                pool.wait_ge(xin_ready, 4 * i + 4)
                pool.tensor_tensor(xs[:, 4 * i:4 * i + 4, :], xs[:, 4 * i:4 * i + 4, :],
                                   xin[:, 4 * i:4 * i + 4, :], ALU.add).then_inc(base_ready, 1)

        @block.tensor
        def _(pe):
            pe.wait_ge(loaded, 16 * NLOAD)
            for h in range(2):
                for k, rows in ((0, P), (1, 64)):
                    mm = pe.matmul(fp[:, B * h:B * h + B], wv[0:rows, k, P * h:P * h + P], csum[0:rows, k, :],
                                   start=(k == 0), stop=(k == 1))
            mm.then_inc(mean_ready, 1)
            pe.wait_ge(ok_ready, 2)
            pe.transpose(fp[0:1, 0:P], ok[:], ident[:]).then_inc(okT_ready, 1)
            pe.wait_ge(ok_ready, 3)
            pe.matmul(fp[:, 256:257], onesr[:], ok1[:], start=True, stop=True).then_inc(okb_ready, 1)
            for s in range(NS):
                pe.wait_ge(ost_ready, s * 2 + 2)
                if s >= 2:
                    pe.wait_ge(xo_free, s - 1)
                for t in range(2):
                    for k in range(2):
                        mm = pe.matmul(xo[:, s % 2, t, :], ost[:, s % 2, k, P * t:P * t + P], wo[:, k, :],
                                       start=(k == 0), stop=(k == 1))
                mm.then_inc(xo_ready, 1)
            with pe.Fori(0, NS // 2) as i:
                for j in range(2):
                    s = i * 2 + j
                    pe.wait_ge(xh_ready, s * 2 + 2)
                    pe.wait_ge(nT_stored, s * 2 + 2)
                    for k in range(2):
                        for t in range(2):
                            mm = pe.transpose(tp[:, j, k, P * t:P * t + P], xh[:, j, t, P * k:P * k + P], ident[:])
                    mm.then_inc(tp_ready, 1)

        @block.vector
        def _(dve):
            link = Link(dve, step)
            dve.wait_ge(loaded, 16 * NLOAD)
            link(dve.tensor_tensor(same[:], rawsum[:], rawsum[:], ALU.is_equal))
            dve.wait_ge(mean_ready, 1)
            dve.tensor_scalar(mean[:].rearrange("p h b -> p (h b)"), fp[:, 0:2 * B], 1.0 / S, None, ALU.mult).then_inc(ok_ready, 1)
            dve.tensor_reduce(ok[:], same[:], AXX, ALU.min).then_inc(ok_ready, 1)
            dve.wait_ge(okT_ready, 1)
            dve.tensor_reduce(ok1[:], fp[0:1, 0:P], AXX, ALU.min).then_inc(ok_ready, 1)
            dve.wait_ge(okb_ready, 1)
            link(dve.tensor_scalar(bad[:], fp[:, 256:257], 0.0, None, ALU.is_equal))
            for c in range(4):
                for h in range(2):
                    b4 = slice(c * B // 4, (c + 1) * B // 4)
                    dve.copy_predicated(oT[:, h, N // 4 * c:N // 4 * c + N // 4].rearrange("p (b q) -> p b q", q=L),
                                        bad[:].unsqueeze(2).to_broadcast([P, B // 4, L]),
                                        mean[:, h, b4].unsqueeze(2).to_broadcast([P, B // 4, L])).then_inc(guarded, 1)
            for s in range(NS):
                dve.wait_ge(xo_ready, s + 1)
                x1 = xs[:, 2 * s:2 * s + 2, :]
                dve.tensor_tensor(x1, xo[:, s % 2], x1, ALU.add).then_inc(xo_free, 1)
                if s:
                    dve.wait_ge(xo_free, s)
                    for t in (2 * s - 2, 2 * s - 1):
                        dve.bn_stats(stats[:, t, :], xs[:, t, :]).then_inc(step, 1)
            dve.wait_ge(xo_free, NS)
            for t in (T - 2, T - 1):
                dve.bn_stats(stats[:, t, :], xs[:, t, :]).then_inc(step, 1)
            link = Link(dve, step, link.n + T)
            dve.wait_ge(step, link.base)

            def aggregate(n):
                for t in range(T):
                    ins = dve.bn_aggr(mv[:, t, :], stats[:, t, :])
                    if t < T - 1:
                        link.n += 1
                        ins.then_inc(step, 1)
                link(ins)
                link(dve.tensor_scalar(ve[:], mv[:, :, 1], EPS, None, ALU.add))
                dve.sem_inc(var_ready, 1)
                dve.wait_ge(sqrt_ready, n)
                refine(dve, link, ve[:], rt[:], rs[:], tmp[:])

            aggregate(1)
            for t in range(T):
                dve.tensor_scalar(xin[:, t, :], xs[:, t, :], mv[:, t, 0:1], rs[:, t:t + 1],
                                  ALU.subtract, ALU.mult).then_inc(xin_ready, 1)
            for t in range(T):
                dve.wait_ge(xin_ready, t + 1)
                dve.bn_stats(stats[:, t, :], xin[:, t, :]).then_inc(step, 1)
                link.n += 1
            dve.wait_ge(step, link.base + link.n)
            aggregate(2)
            for s in range(NS):
                for t in range(2):
                    if s >= 2:
                        dve.wait_ge(tp_ready, s - 1)
                    dve.tensor_scalar(xh[:, s % 2, t, :], xin[:, 2 * s + t, :], mv[:, 2 * s + t, 0:1],
                                      rs[:, 2 * s + t:2 * s + t + 1], ALU.subtract, ALU.mult).then_inc(xh_ready, 1)

        @block.scalar
        def _(act):
            act.wait_ge(loaded, 16 * NLOAD)
            for s in range(NS):
                act.wait_ge(guarded, s // 2 * 2 + 2)
                if s >= 2:
                    act.wait_ge(xo_ready, s - 1)
                for k in range(2):
                    act.activation(ost[:, s % 2, k, :], oT[:, k, V2 * s:V2 * s + V2], ACT.Identity,
                                   bias=bv[:, k:k + 1]).then_inc(ost_ready, 1)
            for n in range(2):
                act.wait_ge(var_ready, n + 1)
                act.activation(rt[:], ve[:], ACT.Sqrt).then_inc(sqrt_ready, 1)
            act.sem_inc(nT_stored, 4)
            with act.Fori(0, NS // 2) as i:
                for j in range(2):
                    s = i * 2 + j
                    act.wait_ge(tp_ready, s + 1)
                    for k in range(2):
                        act.activation(nT[:, k, bass.ds(s * V2, V2)], tp[:, j, k, :], ACT.Identity,
                                       bias=b1[:, k:k + 1], scale=g1[:, k:k + 1]).then_inc(nT_stored, 1)


def state_space_phase(nc, io, m, nT, ssm, sg, r_all, load_experts):
    with ExitStack() as st:
        p = Mem(nc, st)
        wzx = p.sb("ss_wzx", [P, 2, 2 * D])
        wg = p.sb("ss_wg", [P, 2, D])
        wr = p.sb("ss_wr", [P, 2, 2])
        wos = p.sb("ss_wos", [P, 2, D])
        cw = p.sb("ss_cw", [P, 2, 4])
        cb = p.sb("ss_cb", [P, 2])
        br = p.sb("ss_br", [P, 2])
        nS = p.sb("ss_nS", [P, 2, 2, V2])
        sz = p.sb("ss_sz", [P, 2, V2])
        xp = p.sb("ss_xp", [P, 2, BS, L + 3])
        y = p.sb("ss_y", [P, 2, V2])
        sy = p.sb("ss_sy", [P, 2, V2])
        yz = p.sb("ss_yz", [P, 2, V2])
        gT = p.sb("ss_gT", [P, 2, 2, V2])
        zb = p.ps("ss_zb", [P, 2, V2])
        xb = p.ps("ss_xb", [P, 2, V2])
        gb = p.ps("ss_gb", [P, 2, D])
        rb = p.ps("ss_rb", [P, 2, 2])
        ob = p.ps("ss_ob", [P, 2, D])
        loaded = p.sem("ss_loaded")
        pad_ready = p.sem("ss_pad_ready")
        nS_ready = p.sem("ss_nS_ready")
        z_ready = p.sem("ss_z_ready")
        x_ready = p.sem("ss_x_ready")
        g_ready = p.sem("ss_g_ready")
        o_ready = p.sem("ss_o_ready")
        z_stored = p.sem("ss_z_stored")
        x_stored = p.sem("ss_x_stored")
        g_stored = p.sem("ss_g_stored")
        r_stored = p.sem("ss_r_stored")
        o_stored = p.sem("ss_o_stored")
        conv = p.sem("ss_conv")
        sy_ready = p.sem("ss_sy_ready")
        yz_ready = p.sem("ss_yz_ready")
        gT_ready = p.sem("ss_gT_ready")
        block = st.enter_context(nc.Block())
        loads = [(cw[:], io["cw"]), (cb[:], io["cb"]), (br[:], io["br"].partition_broadcast(P))]
        loads += [(dst[:], io[name].rearrange("(k p) m -> p k m", p=P))
                  for dst, name in ((wzx, "Wzx"), (wg, "Wgate"), (wr, "Wr"), (wos, "Wos"))]
        NLOAD = 16 * len(loads)

        def steps(eng, step):
            for s in range(2):
                step(s, s)
            with eng.Fori(1, NS // 2) as i:
                for j in range(2):
                    step(i * 2 + j, j)

        @block.sync
        def _(sp):
            for dst, src in loads:
                sp.dma_start(dst, src).then_inc(loaded, 16)
            load_experts(sp)

        @block.tensor
        def _(pe):
            pe.wait_ge(loaded, NLOAD)

            def output(s, par):
                pe.wait_ge(gT_ready, s + 1)
                pe.wait_ge(o_stored, s)
                for t in range(2):
                    for k in range(2):
                        mm = pe.matmul(ob[:, t, :], gT[:, par, k, P * t:P * t + P], wos[:, k, :],
                                       start=(k == 0), stop=(k == 1))
                mm.then_inc(o_ready, 1)

            def step(s, par):
                src = [nT[:, k, bass.ds(s * V2, V2)] for k in range(2)]
                for bank, o, ready, stored in ((xb, 0, x_ready, x_stored), (zb, D, z_ready, z_stored)):
                    pe.wait_ge(stored, s)
                    for h in range(2):
                        for k in range(2):
                            mm = pe.matmul(bank[:, h, :], wzx[:, k, o + P * h:o + P * h + P], src[k],
                                           start=(k == 0), stop=(k == 1))
                    mm.then_inc(ready, 1)
                pe.wait_ge(nS_ready, s + 1)
                pe.wait_ge(g_stored, s)
                pe.wait_ge(r_stored, s)
                for t in range(2):
                    for k in range(2):
                        lhs = nS[:, par, k, P * t:P * t + P]
                        pe.matmul(gb[:, t, :], lhs, wg[:, k, :], start=(k == 0), stop=(k == 1))
                    for k in range(2):
                        lhs = nS[:, par, k, P * t:P * t + P]
                        mm = pe.matmul(rb[:, t, :], lhs, wr[:, k, :], start=(k == 0), stop=(k == 1))
                mm.then_inc(g_ready, 1)
                if not isinstance(s, int) or s >= 1:
                    output(s - 1, 1 - par)

            steps(pe, step)
            output(NS - 1, 1)

        @block.gpsimd
        def _(pool):
            def step(s, par):
                if not isinstance(s, int) or s >= 2:
                    pool.wait_ge(g_ready, s - 1)
                pool.tensor_copy(nS[:, par], nT[:, :, bass.ds(s * V2, V2)]).then_inc(nS_ready, 1)
                pool.wait_ge(sy_ready, s + 1)
                pool.wait_ge(z_stored, s + 1)
                pool.wait_ge(gT_ready, s)
                pool.tensor_tensor(yz[:], y[:], sz[:], ALU.mult).then_inc(yz_ready, 1)
                pool.wait_ge(yz_ready, s + 1)
                if not isinstance(s, int) or s >= 2:
                    pool.wait_ge(o_ready, s - 1)
                pool.tensor_tensor(gT[:, par], yz[:], sy[:], ALU.mult).then_inc(gT_ready, 1)

            pool.memset(xp[:, :, :, 0:3], 0.0).then_inc(pad_ready, 1)
            steps(pool, step)

        @block.scalar
        def _(act):
            act.wait_ge(loaded, NLOAD)

            def step(s, par):
                act.wait_ge(x_ready, s + 1)
                act.wait_ge(conv, s * 8)
                act.activation(xp[:, :, :, 3:], xb[:].rearrange("p h (b q) -> p h b q", q=L), ACT.Copy).then_inc(x_stored, 1)
                act.wait_ge(z_ready, s + 1)
                act.wait_ge(gT_ready, s)
                act.activation(sz[:], zb[:], ACT.Sigmoid).then_inc(z_stored, 1)
                act.wait_ge(conv, s * 8 + 8)
                act.activation(sy[:], y[:], ACT.Sigmoid).then_inc(sy_ready, 1)
                act.wait_ge(g_ready, s + 1)
                act.activation(sg[:, bass.ds(s * 2, 2), :], gb[:], ACT.Sigmoid).then_inc(g_stored, 1)

            steps(act, step)

        @block.vector
        def _(dve):
            dve.wait_ge(loaded, NLOAD)
            dve.wait_ge(pad_ready, 1)

            def output(s):
                dve.wait_ge(o_ready, s + 1)
                dve.tensor_copy(ssm[:, bass.ds(s * 2, 2), :], ob[:]).then_inc(o_stored, 1)

            def step(s, par):
                dve.wait_ge(x_stored, s + 1)
                dve.wait_ge(gT_ready, s)
                yv = y[:].rearrange("p h (b q) -> p h b q", q=L)
                for n in range(4):
                    for h in range(2):
                        src, w = xp[:, h, :, 3 - n:3 - n + L], cw[:, h, 3 - n:4 - n]
                        if n == 0:
                            ins = dve.tensor_scalar(yv[:, h], src, w, cb[:, h:h + 1], ALU.mult, ALU.add)
                        else:
                            dve.wait_ge(conv, s * 8 + (2 * n - 1 + h))
                            ins = dve.scalar_tensor_tensor(out=yv[:, h], in0=src, scalar=w, in1=yv[:, h],
                                                           op0=ALU.mult, op1=ALU.add)
                        ins.then_inc(conv, 1)
                dve.wait_ge(g_ready, s + 1)
                dve.tensor_tensor(r_all[:, bass.ds(s * 2, 2), :], rb[:], br[:].unsqueeze(1).to_broadcast([P, 2, 2]),
                                  ALU.add).then_inc(r_stored, 1)
                if not isinstance(s, int) or s >= 1:
                    output(s - 1)

            steps(dve, step)
            output(NS - 1)


def self_attention_phase(nc, io, m, nT, ssm, sg, r_all, alpha, xb):
    with ExitStack() as st:
        p = Mem(nc, st, clear=True)
        ident = p.sb("sa_ident", [P, P])
        istack = p.sb("sa_istack", [P, L])
        mask8 = p.sb("sa_mask8", [P, 8])
        mask64 = p.sb("sa_mask64", [P, 64])
        mask4 = p.sb("sa_mask4", [P, 4])
        wqk = p.sb("sa_wqk", [P, 2, 2 * D])
        wv = p.sb("sa_wv", [P, 2, D])
        wout = p.sb("sa_wout", [P, 2, D])
        ls1 = p.sb("sa_ls1", [P, D])
        nS = p.sb("sa_nS", [P, 2, P])
        qkT = p.sb("sa_qkT", [P, 2, 4, P])
        qbd = p.sb("sa_qbd", [P, 2, 4, G, P])
        vbd = p.sb("sa_vbd", [P, G, 4, 64])
        mx = p.sb("sa_mx", [P, G * 4])
        es = p.sb("sa_es", [P, G * 4, L])
        sm = p.sb("sa_sm", [P, G * 4])
        ri = p.sb("sa_ri", [P, G * 4])
        pT = p.sb("sa_pT", [P, G, P])
        om = p.sb("sa_om", [P, 4, G, 64])
        oT = p.sb("sa_oT", [P, 2, P])
        qkb = p.ps("sa_qkb", [P, 4, P])
        vb = p.ps("sa_vb", [P, 512])
        sb_ = p.ps("sa_sb", [P, G * 4 * L])
        pb = p.ps("sa_pb", [P, G, P])
        pv = p.ps("sa_pv", [P, G, 4, 64])
        otb = p.ps("sa_otb", [P, 4, P])
        outb = p.ps("sa_outb", [P, 512])
        names = ("loaded nS_ready qk_ready v_ready s_ready pt_ready pv_ready ot_ready out_ready qk_stored q_ready "
                 "v_stored mx_ready es_ready exp_ready sm_ready ri_ready p_ready pT_stored om_ready oT_stored "
                 "a1_ready a2_ready a3_ready a4_ready xb_ready alpha_ready")
        S_ = {n: p.sem("sa_" + n) for n in names.split()}
        (loaded, nS_ready, qk_ready, v_ready, s_ready, pt_ready, pv_ready, ot_ready, out_ready, qk_stored, q_ready,
         v_stored, mx_ready, es_ready, exp_ready, sm_ready, ri_ready, p_ready, pT_stored, om_ready, oT_stored,
         a1_ready, a2_ready, a3_ready, a4_ready, xb_ready, alpha_ready) = S_.values()
        block = st.enter_context(nc.Block())
        loads = [(ident[:], io["c_ident"]), (istack[:], io["c_istack"]), (mask8[:], io["c_mask8"]),
                 (mask64[:], io["c_mask64"]), (mask4[:], io["c_mask4"]), (ls1[:], io["ls1"].partition_broadcast(P))]
        loads += [(dst[:], io[name].rearrange("(k p) m -> p k m", p=P))
                  for dst, name in ((wqk, "Wqk2"), (wv, "Wv2"), (wout, "Wout2"))]
        NLOAD = 16 * len(loads)

        def tiles(eng, step):
            for t in range(-1, 3):
                step(t, t % 2)
            with eng.Fori(1, T // 2 - 1) as i:
                for j in (1, 2):
                    step(i * 2 + j, j % 2)
            for t in range(T - 1, T + 2):
                step(t, t % 2)

        def there(t, back):
            return not isinstance(t, int) or 0 <= t - back < T

        @block.sync
        def _(sp):
            for dst, src in loads:
                sp.dma_start(dst, src).then_inc(loaded, 16)

        @block.tensor
        def _(pe):
            pe.wait_ge(loaded, NLOAD)

            def step(t, par):
                if there(t, -1):
                    if there(t, 0):
                        pe.wait_ge(qk_stored, t + 1)
                    for c in range(4):
                        for k in range(2):
                            mm = pe.matmul(qkb[:, c, :], wqk[:, k, P * c:P * c + P],
                                           nT[:, k, bass.ds((t + 1) * P, P)], start=(k == 0), stop=(k == 1))
                    mm.then_inc(qk_ready, 1)
                if there(t, 1):
                    pe.wait_ge(p_ready, t)
                    pe.wait_ge(pT_stored, t - 1)
                    for g in range(G):
                        mm = pe.transpose(pb[:, g, :], es[:, 4 * g:4 * g + 4, :].rearrange("p b k -> p (b k)"), ident[:])
                    mm.then_inc(pt_ready, 1)
                if there(t, 0):
                    pe.wait_ge(es_ready, t)
                    pe.wait_ge(q_ready, t * 4 + 4)
                    for g in range(G):
                        for b in range(4):
                            n = L if b == 3 else 2 * L
                            mm = pe.matmul(sb_[:, L * (4 * g + b):L * (4 * g + b) + n], qbd[:, par, b, g, :],
                                           qkT[:, par, 2 + g // 2, L * b:L * b + n], start=True, stop=True)
                    mm.then_inc(s_ready, 1)
                if there(t, 2):
                    pe.wait_ge(om_ready, t - 1)
                    pe.wait_ge(oT_stored, t - 2)
                    for b in range(4):
                        for h in range(2):
                            mm = pe.matmul(otb[:, h, L * b:L * b + L],
                                           om[:, b, 2 * h:2 * h + 2, :].rearrange("p g c -> p (g c)"), istack[:],
                                           start=True, stop=True)
                    mm.then_inc(ot_ready, 1)
                if there(t, 1):
                    pe.wait_ge(pT_stored, t)
                    pe.wait_ge(v_stored, t)
                    pe.wait_ge(om_ready, t - 1)
                    for g in range(G):
                        mm = pe.matmul(pv[:, g, :, :].rearrange("p b c -> p (b c)"), pT[:, g, :],
                                       vbd[:, g, :, :].rearrange("p b c -> p (b c)"), start=True, stop=True)
                    mm.then_inc(pv_ready, 1)
                if there(t, 2):
                    pe.wait_ge(oT_stored, t - 1)
                    pe.wait_ge(a1_ready, t - 2)
                    for k in range(2):
                        mm = pe.matmul(outb[:, 0:D], oT[:, k, :], wout[:, k, :], start=(k == 0), stop=(k == 1))
                    mm.then_inc(out_ready, 1)
                if there(t, 0):
                    pe.wait_ge(nS_ready, t + 1)
                    pe.wait_ge(v_stored, t)
                    for k in range(2):
                        mm = pe.matmul(vb[:, 0:D], nS[:, k, :], wv[:, k, :], start=(k == 0), stop=(k == 1))
                    mm.then_inc(v_ready, 1)

            tiles(pe, step)

        @block.gpsimd
        def _(pool):
            pool.wait_ge(loaded, NLOAD)

            def step(t, par):
                if there(t, -1):
                    pool.wait_ge(qk_stored, t + 2)
                    if there(t, 0):
                        pool.wait_ge(s_ready, t)
                    for b in range(4):
                        src = qkT[:, 1 - par, 0:2, L * b:L * b + L].unsqueeze(2).to_broadcast([P, 2, 8, L])
                        msk = mask8[:].unsqueeze(1).unsqueeze(3).to_broadcast([P, 2, 8, L])
                        pool.tensor_tensor(qbd[:, 1 - par, b].rearrange("p (h j) (e q) -> p h (j e) q", h=2, q=L),
                                           src, msk, ALU.mult).then_inc(q_ready, 1)
                if there(t, 0):
                    pool.wait_ge(ri_ready, t + 1)
                    pool.tensor_tensor(es[:], es[:], ri[:].unsqueeze(2).to_broadcast([P, G * 4, L]),
                                       ALU.mult).then_inc(p_ready, 1)
                if there(t, 2):
                    c = t - 2
                    pool.wait_ge(a3_ready, c + 1)
                    mix = ssm[:, bass.ds(c, 1), :].rearrange("p t c -> p (t c)")
                    pool.tensor_tensor(mix, mix, ls1[:], ALU.mult).then_inc(a4_ready, 1)
                    pool.wait_ge(a4_ready, c + 1)
                    x = xb[:, bass.ds(c, 1), :].rearrange("p t c -> p (t c)")
                    pool.tensor_tensor(x, mix, x, ALU.add).then_inc(xb_ready, 1)

            tiles(pool, step)

        @block.scalar
        def _(act):
            act.activation(alpha[:], r_all[:, :, 0], ACT.Sigmoid).then_inc(alpha_ready, 1)
            act.wait_ge(alpha_ready, 1)

            def step(t, par):
                if there(t, 0):
                    act.wait_ge(v_ready, t)
                    act.activation(nS[:], nT[:, :, bass.ds(t * P, P)], ACT.Copy).then_inc(nS_ready, 1)
                if there(t, -1):
                    act.wait_ge(qk_ready, t + 2)
                    if there(t, 0):
                        act.wait_ge(s_ready, t)
                    act.activation(qkT[:, 1 - par], qkb[:], ACT.Copy).then_inc(qk_stored, 1)
                if there(t, 1):
                    act.wait_ge(pt_ready, t)
                    act.wait_ge(pv_ready, t - 1)
                    act.activation(pT[:], pb[:], ACT.Copy).then_inc(pT_stored, 1)
                if there(t, 0):
                    act.wait_ge(es_ready, t + 1)
                    act.activation(es[:], es[:], ACT.Exp, scale=SCALE).then_inc(exp_ready, 1)

            tiles(act, step)

        @block.vector
        def _(dve):
            dve.wait_ge(loaded, NLOAD)
            dve.wait_ge(alpha_ready, 1)

            def step(t, par):
                if there(t, 0):
                    dve.wait_ge(s_ready, t + 1)
                    scores = sb_[:].rearrange("p (g k) -> p g k", k=L)
                    dve.tensor_reduce(mx[:], scores, AXX, ALU.max).then_inc(mx_ready, 1)
                    dve.wait_ge(mx_ready, t + 1)
                    dve.wait_ge(pt_ready, t)
                    dve.tensor_tensor(es[:], scores, mx[:].unsqueeze(2).to_broadcast([P, G * 4, L]),
                                      ALU.subtract).then_inc(es_ready, 1)
                if there(t, 2):
                    dve.wait_ge(ot_ready, t - 1)
                    dve.wait_ge(out_ready, t - 2)
                    dve.tensor_copy(oT[:], otb[:, 0:2, :]).then_inc(oT_stored, 1)
                if there(t, 0):
                    dve.wait_ge(exp_ready, t + 1)
                    dve.tensor_reduce(sm[:], es[:], AXX, ALU.add).then_inc(sm_ready, 1)
                    dve.wait_ge(sm_ready, t + 1)
                    dve.wait_ge(p_ready, t)
                    dve.reciprocal(ri[:], sm[:]).then_inc(ri_ready, 1)
                if there(t, 1):
                    dve.wait_ge(pv_ready, t)
                    dve.wait_ge(ot_ready, t - 1)
                    dve.tensor_tensor(om[:].rearrange("p b g c -> p g b c"), pv[:],
                                      mask64[:].unsqueeze(1).unsqueeze(1).to_broadcast([P, G, 4, 64]),
                                      ALU.mult).then_inc(om_ready, 1)
                if there(t, 2):
                    c = t - 2
                    row = [a[:, bass.ds(c, 1), :].rearrange("p t c -> p (t c)") for a in (sg, ssm)]
                    dve.wait_ge(out_ready, c + 1)
                    dve.tensor_tensor(row[0], outb[:, 0:D], row[0], ALU.mult).then_inc(a1_ready, 1)
                    dve.wait_ge(a1_ready, c + 1)
                    dve.tensor_tensor(row[0], row[0], row[1], ALU.subtract).then_inc(a2_ready, 1)
                    dve.wait_ge(a2_ready, c + 1)
                    dve.scalar_tensor_tensor(out=row[1], in0=row[0], scalar=alpha[:, bass.ds(c, 1)], in1=row[1],
                                             op0=ALU.mult, op1=ALU.add).then_inc(a3_ready, 1)
                if there(t, 0):
                    dve.wait_ge(v_ready, t + 1)
                    dve.wait_ge(pv_ready, t)
                    dve.tensor_tensor(vbd[:], vb[:, 0:D].rearrange("p (g c) -> p g c", g=G).unsqueeze(2).to_broadcast([P, G, 4, 64]),
                                      mask4[:].unsqueeze(1).unsqueeze(3).to_broadcast([P, G, 4, 64]),
                                      ALU.mult).then_inc(v_stored, 1)

            tiles(dve, step)



E = 8
F1 = 512
F2 = 1024
CAP = 2 * N // E
J1 = 40
GA = 4


def normed_router_phase(nc, io, pre, src, dst, lg, wr, gain, bias, b_router, load_later=None):
    with ExitStack() as st:
        p = Mem(nc, st)
        ident = p.sb(pre + "ident", [P, P])
        w = p.sb(pre + "w", [P, 2, E])
        gb = p.sb(pre + "gb", [P, 2, 2])
        brt = p.sb(pre + "brt", [P, E])
        stats = p.sb(pre + "stats", [P, T, 6])
        mv = p.sb(pre + "mv", [P, T, 2])
        ve = p.sb(pre + "ve", [P, T])
        rt = p.sb(pre + "rt", [P, T])
        rs = p.sb(pre + "rs", [P, T])
        tmp = p.sb(pre + "tmp", [P, T])
        xh = p.sb(pre + "xh", [P, 2, 2, D])
        xT = p.sb(pre + "xT", [P, 2, 2, V2])
        tp = p.ps(pre + "tp", [P, 2, 2, V2])
        lp = p.ps(pre + "lp", [P, 2, 512])
        loaded = p.sem(pre + "loaded")
        step = p.sem(pre + "step")
        var_ready = p.sem(pre + "var_ready")
        sqrt_ready = p.sem(pre + "sqrt_ready")
        xh_ready = p.sem(pre + "xh_ready")
        xh_copied = p.sem(pre + "xh_copied")
        tp_ready = p.sem(pre + "tp_ready")
        xT_ready = p.sem(pre + "xT_ready")
        lp_ready = p.sem(pre + "lp_ready")
        lg_ready = p.sem(pre + "lg_ready")
        block = st.enter_context(nc.Block())
        loads = [(ident[:], io["c_ident"]), (w[:], io[wr].rearrange("(k p) m -> p k m", p=P)),
                 (brt[:], io[b_router].partition_broadcast(P)), (gb[:, 0, :], io[gain]), (gb[:, 1, :], io[bias])]
        NLOAD = 16 * len(loads)

        @block.sync
        def _(sp):
            for d, s in loads:
                sp.dma_start(d, s).then_inc(loaded, 16)
            if load_later:
                load_later(sp)

        @block.vector
        def _(dve):
            for t in range(T):
                dve.bn_stats(stats[:, t, :], src[:, t, :]).then_inc(step, 1)
            dve.wait_ge(step, T)
            for t in range(T):
                dve.bn_aggr(mv[:, t, :], stats[:, t, :]).then_inc(step, 1)
            dve.wait_ge(step, 2 * T)
            dve.tensor_scalar(ve[:], mv[:, :, 1], EPS, None, ALU.add).then_inc(var_ready, 1)
            dve.wait_ge(sqrt_ready, 1)
            link = Link(dve, step, 2 * T)
            refine(dve, link, ve[:], rt[:], rs[:], tmp[:])
            dve.wait_ge(loaded, NLOAD)

            def logits(s):
                dve.wait_ge(lp_ready, s + 1)
                dve.tensor_tensor(lg[:, 2 * s:2 * s + 2, :], lp[:, s % 2, 0:2 * E].rearrange("p (t e) -> p t e", t=2),
                                  brt[:].unsqueeze(1).to_broadcast([P, 2, E]), ALU.add).then_inc(lg_ready, 1)

            for s in range(NS):
                if s >= 2:
                    dve.wait_ge(tp_ready, s - 1)
                    dve.wait_ge(xh_copied, s - 1)
                for t in range(2):
                    dve.tensor_scalar(xh[:, s % 2, t, :], src[:, 2 * s + t, :], mv[:, 2 * s + t, 0:1],
                                      rs[:, 2 * s + t:2 * s + t + 1], ALU.subtract, ALU.mult).then_inc(xh_ready, 1)
                if s >= 2:
                    logits(s - 2)
            logits(NS - 2)
            logits(NS - 1)

        @block.gpsimd
        def _(pool):
            for s in range(NS):
                pool.wait_ge(xh_ready, 2 * s + 2)
                pool.tensor_copy(dst[:, 2 * s:2 * s + 2, :], xh[:, s % 2]).then_inc(xh_copied, 1)

        @block.scalar
        def _(act):
            act.wait_ge(var_ready, 1)
            act.activation(rt[:], ve[:], ACT.Sqrt).then_inc(sqrt_ready, 1)
            act.wait_ge(loaded, NLOAD)
            for s in range(NS):
                act.wait_ge(tp_ready, s + 1)
                if s >= 2:
                    act.wait_ge(lp_ready, s - 1)
                for k in range(2):
                    act.activation(xT[:, s % 2, k, :], tp[:, s % 2, k, :], ACT.Identity,
                                   bias=gb[:, 1, k:k + 1], scale=gb[:, 0, k:k + 1]).then_inc(xT_ready, 1)

        @block.tensor
        def _(pe):
            pe.wait_ge(loaded, NLOAD)

            def products(s):
                pe.wait_ge(xT_ready, 2 * s + 2)
                if s >= 2:
                    pe.wait_ge(lg_ready, s - 1)
                for t in range(2):
                    for k in range(2):
                        mm = pe.matmul(lp[:, s % 2, E * t:E * t + E], xT[:, s % 2, k, P * t:P * t + P], w[:, k, :],
                                       start=(k == 0), stop=(k == 1))
                mm.then_inc(lp_ready, 1)

            for s in range(NS):
                pe.wait_ge(xh_ready, 2 * s + 2)
                if s >= 2:
                    pe.wait_ge(xT_ready, 2 * s - 2)
                for k in range(2):
                    for t in range(2):
                        mm = pe.transpose(tp[:, s % 2, k, P * t:P * t + P], xh[:, s % 2, t, P * k:P * k + P], ident[:])
                mm.then_inc(tp_ready, 1)
                if s >= 1:
                    products(s - 1)
            products(NS - 1)


def route_phase(nc, io, pre, lg, slot, weight, te, capped):
    with ExitStack() as st:
        p = Mem(nc, st)

        def sb(name, shape, dt=F32):
            return p.sb(pre + name, shape, dt)

        tri, ones, reset = sb("tri", [P, P]), sb("ones", [P, P]), sb("reset", [P, P])
        iota = sb("iota", [P, E])
        steps = sb("steps", [P, T])
        tiles = sb("tiles", [P, J1])
        first = sb("first", [P, E])
        mx, z, rz = sb("mx", [P, T]), sb("z", [P, T]), sb("rz", [P, T])
        v = sb("v", [P, T, E])
        top = sb("top", [P, T, 8])
        ix = sb("ix", [P, T, 8], U32)
        ixf = sb("ixf", [P, T, 8])
        sel = sb("sel", [P, 3, T, E])
        tot, incl, rank = sb("tot", [P, E, T]), sb("incl", [P, E, T]), sb("rank", [P, E, T])
        keep = sb("keep", [P, E, T])
        nt, tb, tx = sb("nt", [P, E]), sb("tb", [P, E]), sb("tx", [P, E])
        ge = sb("ge", [1, J1, E])
        tef = sb("tef", [1, J1])
        sf = sb("sf", [P, 2, T])
        t1, t2 = sb("t1", [P, T]), sb("t2", [P, T])
        pb = p.ps(pre + "pb", [P, 2, P])
        loaded = p.sem(pre + "loaded")
        step = p.sem(pre + "step")
        exp_in = p.sem(pre + "exp_in")
        exp_out = p.sem(pre + "exp_out")
        sel_ready = p.sem(pre + "sel_ready")
        rank_ready = p.sem(pre + "rank_ready")
        block = st.enter_context(nc.Block())
        loads = [(tri, "c_tri"), (ones, "c_ones"), (reset, "c_reset"), (iota, "c_iota"), (steps, "c_steps"),
                 (tiles, "c_tiles"), (first, "c_first")]
        NLOAD = 16 * len(loads)

        @block.sync
        def _(sp):
            for d, name in loads:
                sp.dma_start(d[:], io[name]).then_inc(loaded, 16)

        @block.scalar
        def _(act):
            act.wait_ge(exp_in, 1)
            if capped:
                act.activation(z[:], z[:], ACT.Exp).then_inc(exp_out, 1)
            else:
                act.activation(v[:], v[:], ACT.Exp).then_inc(exp_out, 1)

        @block.tensor
        def _(pe):
            pe.wait_ge(loaded, NLOAD)
            pe.wait_ge(sel_ready, 1)
            both = sel[:, 2].rearrange("p t e -> p e t")
            pe.matmul(pb[:, 0, :], tri[:], both, start=True, stop=True)
            pe.matmul(pb[:, 1, :], ones[:], both, start=True, stop=True).then_inc(rank_ready, 1)

        @block.vector
        def _(dve):
            link = Link(dve, step)
            dve.wait_ge(loaded, NLOAD)

            def along(a):
                return a.unsqueeze(2).to_broadcast([P, T, E])

            src = lg
            if not capped:
                link(dve.tensor_reduce(mx[:], lg[:], AXX, ALU.max))
                dve.tensor_tensor(v[:], lg[:], along(mx[:]), ALU.subtract).then_inc(exp_in, 1)
                dve.wait_ge(exp_out, 1)
                link(dve.tensor_reduce(z[:], v[:], AXX, ALU.add))
                link(dve.reciprocal(rz[:], z[:]))
                link(dve.tensor_tensor(v[:], v[:], along(rz[:]), ALU.mult))
                src = v
            for t in range(T):
                dve.max(top[:, t, :], src[:, t, :]).then_inc(step, 1)
                link.n += 1
            dve.wait_ge(step, link.n)
            for t in range(T):
                dve.max_index(ix[:, t, :], top[:, t, :], src[:, t, :]).then_inc(step, 1)
                link.n += 1
            dve.wait_ge(step, link.n)
            link(dve.tensor_copy(ixf[:], ix[:]))
            for c in range(2):
                link(dve.tensor_tensor(sel[:, c], iota[:].unsqueeze(1).to_broadcast([P, T, E]), along(ixf[:, :, c]),
                                       ALU.is_equal))
            dve.tensor_tensor(sel[:, 2], sel[:, 0], sel[:, 1], ALU.add).then_inc(sel_ready, 1)
            if capped:
                dve.tensor_tensor(z[:], top[:, :, 1], top[:, :, 0], ALU.subtract).then_inc(exp_in, 1)
                dve.wait_ge(exp_out, 1)
                link(dve.tensor_scalar(t1[:], z[:], 1.0, None, ALU.add))
                link(dve.reciprocal(weight[:, 0, :], t1[:]))
                link(dve.tensor_tensor(weight[:, 1, :], z[:], weight[:, 0, :], ALU.mult))
            else:
                link(dve.tensor_tensor(t1[:], top[:, :, 0], top[:, :, 1], ALU.add))
                link(dve.tensor_scalar(t2[:], t1[:], 1e-8, None, ALU.add))
                link(dve.reciprocal(t1[:], t2[:]))
                for c in range(2):
                    link(dve.tensor_tensor(weight[:, c, :], top[:, :, c], t1[:], ALU.mult))
            dve.wait_ge(rank_ready, 1)
            link(dve.tensor_copy(tot[:].rearrange("p e t -> p (e t)"), pb[:, 1, :]))
            link(dve.tensor_tensor_scan(out=incl[:].rearrange("p e t -> p (e t)"), data0=reset[:],
                                        data1=tot[:].rearrange("p e t -> p (e t)"), initial=0.0,
                                        op0=ALU.mult, op1=ALU.add))
            link(dve.tensor_tensor(rank[:], incl[:], tot[:], ALU.subtract))
            link(dve.tensor_tensor(rank[:].rearrange("p e t -> p (e t)"), pb[:, 0, :],
                                   rank[:].rearrange("p e t -> p (e t)"), ALU.add))
            base = first
            if capped:
                link(dve.tensor_scalar(keep[:], rank[:], float(CAP), None, ALU.is_lt))
            else:
                link(dve.tensor_tensor(keep[:], incl[:, :, T - 1:T].to_broadcast([P, E, T]),
                                       steps[:].unsqueeze(1).to_broadcast([P, E, T]), ALU.is_gt))
                link(dve.tensor_reduce(nt[:], keep[:], AXX, ALU.add))
                link(dve.tensor_tensor_scan(out=tb[:], data0=ones[:, 0:E], data1=nt[:], initial=0.0,
                                            op0=ALU.mult, op1=ALU.add))
                link(dve.tensor_tensor(tx[:], tb[:], nt[:], ALU.subtract))
                link(dve.tensor_scalar(tx[:], tx[:], float(P), None, ALU.mult))
                base = tx
                link(dve.tensor_tensor(ge[:], tiles[0:1, :].unsqueeze(2).to_broadcast([1, J1, E]),
                                       tb[0:1, :].unsqueeze(1).to_broadcast([1, J1, E]), ALU.is_ge))
                link(dve.tensor_reduce(tef[:], ge[:], AXX, ALU.add))
                link(dve.tensor_scalar(te[:], tef[:], float(E - 1), None, ALU.min))
            link(dve.tensor_tensor(rank[:], rank[:], base[:].unsqueeze(2).to_broadcast([P, E, T]), ALU.add))
            if capped:
                link(dve.tensor_scalar(rank[:], rank[:], -2.0 * N, None, ALU.add))
                link(dve.tensor_tensor(rank[:], rank[:], keep[:], ALU.mult))
                link(dve.tensor_scalar(rank[:], rank[:], 2.0 * N, None, ALU.add))
            for c in range(2):
                link(dve.tensor_tensor(v[:], sel[:, c], rank[:].rearrange("p e t -> p t e"), ALU.mult))
                link(dve.tensor_reduce(sf[:, c, :], v[:], AXX, ALU.add))
                link(dve.tensor_copy(slot[:, c, :], sf[:, c, :]))


def scatter_phase(nc, pre, rows, slot, buf, n_slots, zeroed):
    with ExitStack() as st:
        scattered = Mem(nc, st).sem(pre + "scattered")
        block = st.enter_context(nc.Block())

        @block.gpsimd
        def _(pool):
            pool.wait_ge(*zeroed)
            for t in range(T):
                for c in range(2):
                    pool.indirect_dma_start(out=buf, out_offset=bass.IndirectOffsetOnAxis(ap=slot[:, c, t:t + 1], axis=0),
                                            in_=rows[:, t, :], in_offset=None, bounds_check=n_slots - 1,
                                            oob_is_err=False).then_inc(scattered, 16)
            pool.wait_ge(scattered, 16 * 2 * T)


def first_experts_phase(nc, io, xg, yg, te, w13, w2, w_loaded):
    with ExitStack() as st:
        p = Mem(nc, st)
        ident = p.sb("e1_ident", [P, P])
        gb = p.sb("e1_gb", [P, 2, 2])
        x = p.sb("e1_x", [P, 2, D])
        xT = p.sb("e1_xT", [P, 2, 2, P])
        s = p.sb("e1_s", [P, F1])
        h = p.sb("e1_h", [P, F1])
        hT = p.sb("e1_hT", [P, 4, P])
        y = p.sb("e1_y", [P, 2, D])
        tb = p.ps("e1_tb", [P, 2, P])
        ab = p.ps("e1_ab", [P, F1])
        bb = p.ps("e1_bb", [P, F1])
        hb = p.ps("e1_hb", [P, 4, P])
        yb = p.ps("e1_yb", [P, D])
        loaded = p.sem("e1_loaded")
        x_loaded = [p.sem(f"e1_x_loaded{i}") for i in range(2)]
        y_written = [p.sem(f"e1_y_written{i}") for i in range(2)]
        t_ready = p.sem("e1_t_ready")
        xT_ready = p.sem("e1_xT_ready")
        a_ready = p.sem("e1_a_ready")
        b_ready = p.sem("e1_b_ready")
        s_ready = p.sem("e1_s_ready")
        h_ready = p.sem("e1_h_ready")
        hb_ready = p.sem("e1_hb_ready")
        hT_ready = p.sem("e1_hT_ready")
        yb_ready = p.sem("e1_yb_ready")
        y_ready = p.sem("e1_y_ready")
        block = st.enter_context(nc.Block())

        def tiles(eng, step, lag=0):
            for j in range(4):
                step(j, j % 2)
            with eng.Fori(2, J1 // 2 - 1) as i:
                for j in range(2):
                    step(i * 2 + j, j)
            for j in range(J1 - 2, J1 + lag):
                step(j, j % 2)

        def there(j, back):
            return not isinstance(j, int) or 0 <= j - back < J1

        @block.sync
        def _(sp):
            sp.dma_start(ident[:], io["c_ident"]).then_inc(loaded, 16)
            sp.dma_start(gb[:, 0, :], io["g2"]).then_inc(loaded, 16)
            sp.dma_start(gb[:, 1, :], io["b2"]).then_inc(loaded, 16)
            for j in range(2):
                sp.dma_start(x[:, j, :], xg[P * j:P * j + P, :]).then_inc(x_loaded[j], 16)

            def step(j, par):
                if there(j, -2):
                    sp.wait_ge(t_ready, j + 1)
                    sp.dma_start(x[:, par, :], xg[bass.ds(j * P + 2 * P, P), :]).then_inc(x_loaded[par], 16)
                if there(j, 1):
                    sp.wait_ge(y_ready, j)
                    sp.dma_start(yg[bass.ds(j * P - P, P), :], y[:, 1 - par, :]).then_inc(y_written[1 - par], 16)

            tiles(sp, step, 1)
            for c in range(2):
                sp.wait_ge(y_written[c], 16 * J1 // 2)

        @block.tensor
        def _(pe):
            pe.wait_ge(loaded, 48)
            pe.wait_ge(*w_loaded)

            def loads_of(j, par):
                return 16 * (j // 2 + 1) if isinstance(j, int) else j * 8 + (16 if par == 0 else 8)

            def turn_x(j, par):
                pe.wait_ge(x_loaded[par], loads_of(j, par))
                pe.wait_ge(xT_ready, j * 2)
                for k in range(2):
                    mm = pe.transpose(tb[:, k, :], x[:, par, P * k:P * k + P], ident[:])
                mm.then_inc(t_ready, 1)

            def step(j, par):
                if there(j, 0):
                    e = pe.value_load(te[0:1, bass.ds(j, 1)], min_val=0, max_val=E - 1)
                    pe.wait_ge(xT_ready, j * 2 + 2)
                    pe.wait_ge(s_ready, j)
                    for k in range(2):
                        mm = pe.matmul(ab[:], xT[:, par, k, :], w13[:, bass.ds(e * 4 + k, 1), :].rearrange("p a f -> p (a f)"),
                                       start=(k == 0), stop=(k == 1))
                    mm.then_inc(a_ready, 1)
                if there(j, 1):
                    pe.wait_ge(h_ready, j)
                    pe.wait_ge(hT_ready, j - 1)
                    for f in range(4):
                        mm = pe.transpose(hb[:, f, :], h[:, P * f:P * f + P], ident[:])
                    mm.then_inc(hb_ready, 1)
                if there(j, 0):
                    pe.wait_ge(h_ready, j)
                    for k in range(2):
                        mm = pe.matmul(bb[:], xT[:, par, k, :], w13[:, bass.ds(e * 4 + (2 + k), 1), :].rearrange("p a f -> p (a f)"),
                                       start=(k == 0), stop=(k == 1))
                    mm.then_inc(b_ready, 1)
                if there(j, -1):
                    turn_x(j + 1, 1 - par)
                if there(j, 1):
                    d = pe.value_load(te[0:1, bass.ds(j - 1, 1)], min_val=0, max_val=E - 1)
                    pe.wait_ge(hT_ready, j)
                    pe.wait_ge(y_ready, j - 1)
                    for f in range(4):
                        mm = pe.matmul(yb[:], hT[:, f, :], w2[:, bass.ds(d * 4 + f, 1), :].rearrange("p a c -> p (a c)"),
                                       start=(f == 0), stop=(f == 3))
                    mm.then_inc(yb_ready, 1)

            turn_x(0, 0)
            tiles(pe, step, 1)

        @block.scalar
        def _(act):
            act.wait_ge(loaded, 48)

            def turn_x(j, par):
                act.wait_ge(t_ready, j + 1)
                if not isinstance(j, int) or j >= 2:
                    act.wait_ge(b_ready, j - 1)
                for k in range(2):
                    act.activation(xT[:, par, k, :], tb[:, k, :], ACT.Identity,
                                   bias=gb[:, 1, k:k + 1], scale=gb[:, 0, k:k + 1]).then_inc(xT_ready, 1)

            def step(j, par):
                if there(j, 0):
                    act.wait_ge(a_ready, j + 1)
                    act.wait_ge(h_ready, j)
                    act.activation(s[:], ab[:], ACT.Silu).then_inc(s_ready, 1)
                if there(j, -1):
                    turn_x(j + 1, 1 - par)
                if there(j, 1):
                    act.wait_ge(yb_ready, j)
                    if not isinstance(j, int) or j >= 3:
                        act.wait_ge(y_written[1 - par], (j - 1) // 2 * 16 if isinstance(j, int) else j * 8 - (16 if par == 0 else 8))
                    act.activation(y[:, 1 - par, :], yb[:], ACT.Copy).then_inc(y_ready, 1)

            turn_x(0, 0)
            tiles(act, step, 1)

        @block.vector
        def _(dve):
            def step(j, par):
                if there(j, 1):
                    dve.wait_ge(hb_ready, j)
                    dve.wait_ge(yb_ready, j - 1)
                    dve.tensor_copy(hT[:], hb[:]).then_inc(hT_ready, 1)
                if there(j, 0):
                    dve.wait_ge(s_ready, j + 1)
                    dve.wait_ge(b_ready, j + 1)
                    dve.wait_ge(hb_ready, j)
                    dve.tensor_tensor(h[:], bb[:], s[:], ALU.mult).then_inc(h_ready, 1)

            tiles(dve, step, 1)


def first_combine_phase(nc, io, yg, slot, weight, r_all, xb, base, x2):
    with ExitStack() as st:
        p = Mem(nc, st)
        ls2 = p.sb("c1_ls2", [P, D])
        sb_ = p.sb("c1_sb", [P, 3])
        y = p.sb("c1_y", [P, GA, 2, D])
        bs = p.sb("c1_bs", [P, GA, D])
        c1 = p.sb("c1_c1", [P, 2, D])
        c2 = p.sb("c1_c2", [P, 2, D])
        c3 = p.sb("c1_c3", [P, 2, D])
        c4 = p.sb("c1_c4", [P, 2, D])
        halt = p.sb("c1_halt", [P, 2, T])
        rem = p.sb("c1_rem", [P, 2, T])
        w1 = p.sb("c1_w1", [P, T])
        ws = p.sb("c1_ws", [P, 2, T])
        loaded = p.sem("c1_loaded")
        halt_ready = p.sem("c1_halt_ready")
        y_gathered = [p.sem(f"c1_y_gathered{i}") for i in range(GA)]
        bs_loaded = [p.sem(f"c1_bs_loaded{i}") for i in range(GA)]
        c1_ready = p.sem("c1_c1_ready")
        c2_ready = p.sem("c1_c2_ready")
        c3_ready = p.sem("c1_c3_ready")
        c4_ready = p.sem("c1_c4_ready")
        x2_ready = p.sem("c1_x2_ready")
        step = p.sem("c1_step")
        block = st.enter_context(nc.Block())

        @block.sync
        def _(sp):
            sp.dma_start(ls2[:], io["ls2"].partition_broadcast(P)).then_inc(loaded, 16)
            sp.dma_start(sb_[:], io["step_bias"].partition_broadcast(P)).then_inc(loaded, 16)
            for t in range(T):
                if t >= GA:
                    sp.wait_ge(x2_ready, t - GA + 1)
                sp.dma_start(bs[:, t % GA, :], base[:, t, :]).then_inc(bs_loaded[t % GA], 16)

        @block.gpsimd
        def _(pool):
            def gather(t):
                if t >= GA:
                    pool.wait_ge(c2_ready, t - GA + 1)
                for c in range(2):
                    pool.indirect_dma_start(out=y[:, t % GA, c, :], out_offset=None, in_=yg,
                                            in_offset=bass.IndirectOffsetOnAxis(ap=slot[:, c, t:t + 1], axis=0),
                                            ).then_inc(y_gathered[t % GA], 16)

            pool.wait_ge(loaded, 32)
            for t in range(2):
                gather(t)
            for t in range(T):
                if t + 2 < T:
                    gather(t + 2)
                j = t % 2
                pool.wait_ge(c2_ready, t + 1)
                if t >= 2:
                    pool.wait_ge(c4_ready, t - 1)
                pool.tensor_tensor(c3[:, j, :], c2[:, j, :], ls2[:], ALU.mult).then_inc(c3_ready, 1)
                pool.wait_ge(c3_ready, t + 1)
                if t >= 2:
                    pool.wait_ge(x2_ready, t - 1)
                pool.tensor_tensor(c4[:, j, :], c3[:, j, :], xb[:, t, :], ALU.add).then_inc(c4_ready, 1)

        @block.scalar
        def _(act):
            act.wait_ge(loaded, 32)
            for s in range(2):
                act.activation(halt[:, s, :], r_all[:, :, 1], ACT.Sigmoid, bias=sb_[:, s:s + 1]).then_inc(halt_ready, 1)
            for t in range(T):
                act.wait_ge(y_gathered[t % GA], 32 * (t // GA + 1))
                if t >= 2:
                    act.wait_ge(c2_ready, t - 1)
                act.activation(c1[:, t % 2, :], y[:, t % GA, 0, :], ACT.Copy, scale=weight[:, 0, t:t + 1]).then_inc(c1_ready, 1)

        @block.vector
        def _(dve):
            link = Link(dve, step)
            dve.wait_ge(halt_ready, 2)
            link(dve.tensor_scalar(rem[:, 0, :], halt[:, 0, :], -1.0, 1.0, ALU.mult, ALU.add))
            link(dve.tensor_scalar(rem[:, 0, :], rem[:, 0, :], 0.0, None, ALU.max))
            link(dve.tensor_tensor(w1[:], halt[:, 1, :], rem[:, 0, :], ALU.mult))
            link(dve.tensor_tensor(rem[:, 1, :], rem[:, 0, :], w1[:], ALU.subtract))
            link(dve.tensor_scalar(rem[:, 1, :], rem[:, 1, :], 0.0, None, ALU.max))
            link(dve.tensor_tensor(ws[:, 0, :], halt[:, 0, :], w1[:], ALU.add))
            link(dve.tensor_tensor(ws[:, 1, :], ws[:, 0, :], rem[:, 1, :], ALU.add))

            def finish(t):
                dve.wait_ge(c4_ready, t + 1)
                dve.wait_ge(bs_loaded[t % GA], 16 * (t // GA + 1))
                dve.scalar_tensor_tensor(out=x2[:, t, :], in0=c4[:, t % 2, :], scalar=ws[:, 1, t:t + 1],
                                         in1=bs[:, t % GA, :], op0=ALU.mult, op1=ALU.add).then_inc(x2_ready, 1)

            for t in range(T):
                dve.wait_ge(c1_ready, t + 1)
                if t >= 2:
                    dve.wait_ge(c3_ready, t - 1)
                dve.scalar_tensor_tensor(out=c2[:, t % 2, :], in0=y[:, t % GA, 1, :], scalar=weight[:, 1, t:t + 1],
                                         in1=c1[:, t % 2, :], op0=ALU.mult, op1=ALU.add).then_inc(c2_ready, 1)
                if t >= 1:
                    finish(t - 1)
            finish(T - 1)


def load_second_experts(sp, io, w, w_loaded, e, par):
    w1, w2 = w
    sp.dma_start(w1[:, par], io["F_W1"][bass.ds(e, 1), :, :].rearrange("a (k p) f -> p (a k) f", p=P)).then_inc(w_loaded[par], 16)
    sp.dma_start(w2[:, par], io["F_W2"][bass.ds(e, 1), :, :].rearrange("a (k p) d -> p (a k) d", p=P)).then_inc(w_loaded[par], 16)


def second_experts_phase(nc, io, xg, yg, w, w_loaded):
    ST = CAP // P
    M = F2 // P
    w1, w2 = w
    with ExitStack() as st:
        p = Mem(nc, st)
        ident = p.sb("e2_ident", [P, P])
        b1 = p.sb("e2_b1", [P, E, M])
        b2 = p.sb("e2_b2", [P, 2, D])
        w1s = p.sb("e2_w1s", [P, 2, 2, F2], F32R)
        w2s = p.sb("e2_w2s", [P, 2, M, D], F32R)
        x = p.sb("e2_x", [P, 2, ST, D])
        xTs = p.sb("e2_xTs", [P, 2, 2, CAP], F32R)
        h = p.sb("e2_h", [P, 2, CAP])
        hTs = p.sb("e2_hTs", [P, 2, M, CAP], F32R)
        y = p.sb("e2_y", [P, 2, ST, D])
        tb = p.ps("e2_tb", [P, 2, CAP])
        hb = p.ps("e2_hb", [P, 2, CAP])
        yb = p.ps("e2_yb", [P, 2, 512])
        loaded = p.sem("e2_loaded")
        b_loaded = [p.sem(f"e2_b_loaded{i}") for i in range(2)]
        x_loaded = [p.sem(f"e2_x_loaded{i}") for i in range(2)]
        y_written = [p.sem(f"e2_y_written{i}") for i in range(2)]
        t_ready = p.sem("e2_t_ready")
        xh_ready = p.sem("e2_xh_ready")
        xl_ready = p.sem("e2_xl_ready")
        w1h_ready = p.sem("e2_w1h_ready")
        w1l_ready = p.sem("e2_w1l_ready")
        w2h_ready = p.sem("e2_w2h_ready")
        w2l_ready = p.sem("e2_w2l_ready")
        hb_ready = p.sem("e2_hb_ready")
        h_ready = p.sem("e2_h_ready")
        hh_ready = p.sem("e2_hh_ready")
        hl_ready = p.sem("e2_hl_ready")
        yb_ready = p.sem("e2_yb_ready")
        y_ready = p.sem("e2_y_ready")
        block = st.enter_context(nc.Block())

        def experts(eng, step):
            for e in range(2):
                step(e, e)
            with eng.Fori(1, E // 2 - 1) as i:
                for j in range(2):
                    step(i * 2 + j, j)
            for e in range(E - 2, E):
                step(e, e % 2)

        def static(e):
            return isinstance(e, int)

        def uses(e, par, each):
            return each * (e // 2 + 1) if static(e) else e * (each // 2) + (each if par == 0 else each // 2)

        @block.sync
        def _(sp):
            sp.dma_start(ident[:], io["c_ident"]).then_inc(loaded, 16)
            sp.dma_start(b1[:], io["F_b1"]).then_inc(loaded, 16)

            def load(e, par):
                sp.dma_start(x[:, par], xg[bass.ds(e * CAP, CAP), :].rearrange("(s p) d -> p s d", p=P)).then_inc(x_loaded[par], 16)
                sp.dma_start(b2[:, par, :], io["F_b2"][bass.ds(e, 1), :].partition_broadcast(P).rearrange("p a d -> p (a d)")).then_inc(b_loaded[par], 16)

            for e in range(2):
                load(e, e)

            def step(e, par):
                if not static(e) or e + 2 < E:
                    sp.wait_ge(w2l_ready, e * 2 + 2)
                    sp.wait_ge(w2h_ready, e * 2 + 2)
                    load_second_experts(sp, io, w, w_loaded, e + 2, par)
                sp.wait_ge(y_ready, e * ST + ST)
                sp.dma_start(yg[bass.ds(e * CAP, CAP), :].rearrange("(s p) d -> p s d", p=P), y[:, par]).then_inc(y_written[par], 16)
                if not static(e) or e + 2 < E:
                    load(e + 2, par)

            experts(sp, step)
            for c in range(2):
                sp.wait_ge(y_written[c], 16 * E // 2)

        PARTS = ((0, 0), (0, 1), (1, 0))

        @block.tensor
        def _(pe):
            pe.wait_ge(loaded, 32)

            def turn_x(e, par):
                pe.wait_ge(x_loaded[par], uses(e, par, 16))
                for k in range(2):
                    if not (static(e) and e == 0):
                        pe.wait_ge(xl_ready, e * 2)
                    for s in range(ST):
                        mm = pe.transpose(tb[:, k, P * s:P * s + P], x[:, par, s, P * k:P * k + P], ident[:])
                    mm.then_inc(t_ready, 1)

            def step(e, par):
                pe.wait_ge(xh_ready, e * 2 + 2)
                pe.wait_ge(xl_ready, e * 2 + 2)
                pe.wait_ge(w1h_ready, e * 2 + 2)
                pe.wait_ge(w1l_ready, e * 2 + 2)
                for f in range(M):
                    if f >= 2:
                        pe.wait_ge(h_ready, e * M + (f - 1))
                    elif not (static(e) and e == 0):
                        pe.wait_ge(h_ready, e * M)
                    n = 0
                    for k in range(2):
                        for a, b in PARTS:
                            mm = pe.matmul(hb[:, f % 2, :], w1s[:, a, k, P * f:P * f + P], xTs[:, b, k, :],
                                           start=(n == 0), stop=(n == 5))
                            n += 1
                    mm.then_inc(hb_ready, 1)
                if not static(e) or e + 1 < E:
                    turn_x(e + 1, 1 - par)
                pe.wait_ge(w2h_ready, e * 2 + 2)
                pe.wait_ge(w2l_ready, e * 2 + 2)
                for s in range(ST):
                    if not (static(e) and e == 0 and s < 2):
                        pe.wait_ge(y_ready, e * ST + (s - 1))
                    for f in range(M):
                        if s == 0:
                            pe.wait_ge(hh_ready, e * M + (f + 1))
                            pe.wait_ge(hl_ready, e * M + (f + 1))
                        for a, b in PARTS:
                            mm = pe.matmul(yb[:, s % 2, 0:D], hTs[:, a, f, P * s:P * s + P], w2s[:, b, f, :],
                                           start=(f == 0 and (a, b) == (0, 0)), stop=(f == M - 1 and a == 1))
                    mm.then_inc(yb_ready, 1)

            turn_x(0, 0)
            experts(pe, step)

        @block.scalar
        def _(act):
            act.wait_ge(loaded, 32)

            def high_w1(e, par):
                act.wait_ge(w_loaded[par], uses(e, par, 32))
                if not (static(e) and e == 0):
                    act.wait_ge(hb_ready, e * M)
                for k in range(2):
                    act.activation(w1s[:, 0, k, :], w1[:, par, k, :], ACT.Copy).then_inc(w1h_ready, 1)

            def step(e, par):
                for f in range(M):
                    act.wait_ge(hb_ready, e * M + (f + 1))
                    if not (static(e) and e == 0 and f < 2):
                        act.wait_ge(hh_ready, e * M + (f - 1))
                        act.wait_ge(hl_ready, e * M + (f - 1))
                    act.activation(h[:, f % 2, :], hb[:, f % 2, :], ACT.Gelu,
                                   bias=b1[:, bass.ds(e, 1), f:f + 1].rearrange("p a b -> p (a b)")).then_inc(h_ready, 1)
                    if f in (1, 3):
                        if not (static(e) and e == 0):
                            act.wait_ge(yb_ready, e * ST)
                        m = slice(M // 2 * (f // 2), M // 2 * (f // 2) + M // 2)
                        act.activation(w2s[:, 0, m, :], w2[:, par, m, :], ACT.Copy).then_inc(w2h_ready, 1)
                if not static(e) or e + 1 < E:
                    high_w1(e + 1, 1 - par)

            high_w1(0, 0)
            experts(act, step)

        @block.gpsimd
        def _(pool):
            def rest_w1(e, par):
                for k in range(2):
                    pool.wait_ge(w1h_ready, e * 2 + (k + 1))
                    pool.tensor_tensor(w1s[:, 1, k, :], w1[:, par, k, :], w1s[:, 0, k, :], ALU.subtract).then_inc(w1l_ready, 1)

            def step(e, par):
                for c in range(2):
                    m = slice(M // 2 * c, M // 2 * c + M // 2)
                    pool.wait_ge(w2h_ready, e * 2 + (c + 1))
                    pool.tensor_tensor(w2s[:, 1, m, :], w2[:, par, m, :], w2s[:, 0, m, :], ALU.subtract).then_inc(w2l_ready, 1)
                if not static(e) or e + 1 < E:
                    rest_w1(e + 1, 1 - par)

            rest_w1(0, 0)
            experts(pool, step)

        @block.vector
        def _(dve):
            def split_x(e, par):
                if not (static(e) and e == 0):
                    dve.wait_ge(hb_ready, e * M)
                for k in range(2):
                    dve.wait_ge(t_ready, e * 2 + (k + 1))
                    dve.tensor_copy(xTs[:, 0, k, :], tb[:, k, :]).then_inc(xh_ready, 1)
                for k in range(2):
                    dve.wait_ge(xh_ready, e * 2 + (k + 1))
                    dve.tensor_tensor(xTs[:, 1, k, :], tb[:, k, :], xTs[:, 0, k, :], ALU.subtract).then_inc(xl_ready, 1)

            def step(e, par):
                if not (static(e) and e == 0):
                    dve.wait_ge(yb_ready, e * ST)
                for f in range(M):
                    dve.wait_ge(h_ready, e * M + (f + 1))
                    dve.tensor_copy(hTs[:, 0, f, :], h[:, f % 2, :]).then_inc(hh_ready, 1)
                    dve.wait_ge(hh_ready, e * M + (f + 1))
                    dve.tensor_tensor(hTs[:, 1, f, :], h[:, f % 2, :], hTs[:, 0, f, :], ALU.subtract).then_inc(hl_ready, 1)
                if not static(e) or e + 1 < E:
                    split_x(e + 1, 1 - par)
                dve.wait_ge(b_loaded[par], uses(e, par, 16))
                if not (static(e) and e < 2):
                    dve.wait_ge(y_written[par], uses(e, par, 16) - 16)
                for s in range(ST):
                    dve.wait_ge(yb_ready, e * ST + (s + 1))
                    dve.tensor_tensor(y[:, par, s, :], yb[:, s % 2, 0:D], b2[:, par, :], ALU.add).then_inc(y_ready, 1)

            split_x(0, 0)
            experts(dve, step)


def output_phase(nc, io, yg, slot, weight, x2):
    with ExitStack() as st:
        p = Mem(nc, st)
        y = p.sb("o_y", [P, GA, 2, D])
        c1 = p.sb("o_c1", [P, GA, D])
        res = p.sb("o_res", [P, GA, D])
        gathered = [p.sem(f"o_gathered{i}") for i in range(GA)]
        written = [p.sem(f"o_written{i}") for i in range(GA)]
        c1_ready = p.sem("o_c1_ready")
        res_ready = p.sem("o_res_ready")
        block = st.enter_context(nc.Block())
        out = io["out"].rearrange("(t p) d -> p t d", p=P)

        @block.gpsimd
        def _(pool):
            for t in range(T):
                if t >= GA:
                    pool.wait_ge(res_ready, t - GA + 1)
                for c in range(2):
                    pool.indirect_dma_start(out=y[:, t % GA, c, :], out_offset=None, in_=yg,
                                            in_offset=bass.IndirectOffsetOnAxis(ap=slot[:, c, t:t + 1], axis=0),
                                            ).then_inc(gathered[t % GA], 16)

        @block.vector
        def _(dve):
            for t in range(T):
                g = t % GA
                dve.wait_ge(gathered[g], 32 * (t // GA + 1))
                dve.scalar_tensor_tensor(out=c1[:, g, :], in0=y[:, g, 0, :], scalar=weight[:, 0, t:t + 1],
                                         in1=x2[:, t, :], op0=ALU.mult, op1=ALU.add).then_inc(c1_ready, 1)
                dve.wait_ge(c1_ready, t + 1)
                if t >= GA:
                    dve.wait_ge(written[g], 16 * (t // GA))
                dve.scalar_tensor_tensor(out=res[:, g, :], in0=y[:, g, 1, :], scalar=weight[:, 1, t:t + 1],
                                         in1=c1[:, g, :], op0=ALU.mult, op1=ALU.add).then_inc(res_ready, 1)

        @block.sync
        def _(sp):
            for t in range(T):
                sp.wait_ge(res_ready, t + 1)
                sp.dma_start(out[:, t, :], res[:, t % GA, :]).then_inc(written[t % GA], 16)
            for g in range(GA):
                sp.wait_ge(written[g], 16 * (T // GA))


def build_program(nc, io):
    with ExitStack() as st:
        m = Mem(nc, st)
        xg1 = nc.dram_tensor("xg1", (J1 * P, D), F32, kind="Internal").ap()
        yg1 = nc.dram_tensor("yg1", (J1 * P, D), F32, kind="Internal").ap()
        xg2 = nc.dram_tensor("xg2", (2 * N, D), F32, kind="Internal").ap()
        yg2 = nc.dram_tensor("yg2", (2 * N + P, D), F32, kind="Internal").ap()
        base = nc.dram_tensor("base", (P, T, D), F32, kind="Internal").ap()
        zeroed = m.sem("zeroed")
        w_loaded = m.sem("w_loaded")
        base_written = m.sem("base_written")
        slot1 = m.sb("slot1", [P, 2, T], I32)
        slot2 = m.sb("slot2", [P, 2, T], I32)
        weight1 = m.sb("weight1", [P, 2, T])
        weight2 = m.sb("weight2", [P, 2, T])
        te = m.sb("te", [1, J1], I32)
        r_all = m.sb("r_all", [P, T, 2])
        alpha = m.sb("alpha", [P, T])
        lg = m.sb("lg", [P, T, E])

        def zero_slots(sp, zero):
            z8 = zero[:].to_broadcast([P, 8, D])
            for buf, tiles in ((xg1, J1), (xg2, 2 * N // P)):
                for i in range(tiles // 8):
                    sp.dma_start(buf[8 * P * i:8 * P * i + 8 * P, :].rearrange("(t p) d -> p t d", p=P),
                                 z8).then_inc(zeroed, 16)
            sp.dma_start(yg2[2 * N:2 * N + P, :], zero[:, 0, :]).then_inc(zeroed, 16)

        NZ = 16 * (J1 // 8 + 2 * N // P // 8 + 1)
        xs = m.sb("xs", [P, T, D])
        with ExitStack() as s0:
            m0 = Mem(nc, s0)
            oT = m0.sb("oT", [P, 2, N])
            rawsum = m0.sb("rawsum", [P, B * G])
            csum = m0.sb("csum", [P, 2, B])
            with ExitStack() as s1:
                m1 = Mem(nc, s1)
                qs = m1.sb("qs", [P, 2, 2, N], F32R)
                query_phase(nc, io, m1, xs, qs)
                cross_attention_phase(nc, io, m1, xs, qs, oT, rawsum, csum, zero_slots, (zeroed, NZ))
            nT = m0.sb("nT", [P, 2, N])
            xb = m0.sb("xb", [P, T, D])
            merge_phase(nc, io, m0, oT, rawsum, csum, xs, xb, nT, base, base_written)
            w13 = m0.sb("w13", [P, E * 4, F1])
            w2 = m0.sb("w2", [P, E * 4, D])

            def load_experts(sp):
                for e in range(E):
                    for c, name in enumerate(("W1", "W3")):
                        sp.dma_start(w13[:, 4 * e + 2 * c:4 * e + 2 * c + 2, :],
                                     io[name][e].rearrange("(k p) f -> p k f", p=P)).then_inc(w_loaded, 16)
                    sp.dma_start(w2[:, 4 * e:4 * e + 4, :],
                                 io["W2"][e].rearrange("(k p) d -> p k d", p=P)).then_inc(w_loaded, 16)

            ssm, sg = xs, oT[:].rearrange("p k (t c) -> p (k t) c", c=D)
            state_space_phase(nc, io, m0, nT, ssm, sg, r_all, load_experts)
            self_attention_phase(nc, io, m0, nT, ssm, sg, r_all, alpha, xb)
            rows = xs
            normed_router_phase(nc, io, "n1_", xb, rows, lg, "Wg", "g2", "b2", "zero8")
            route_phase(nc, io, "r1_", lg, slot1, weight1, te, False)
            scatter_phase(nc, "s1_", rows, slot1, xg1, J1 * P, (zeroed, NZ))
            first_experts_phase(nc, io, xg1, yg1, te, w13, w2, (w_loaded, 16 * 3 * E))
            first_combine_phase(nc, io, yg1, slot1, weight1, r_all, xb, base, xs)
        x2 = xs
        e2w = m.sb("e2_w1", [P, 2, 2, F2]), m.sb("e2_w2", [P, 2, F2 // P, D])
        e2w_loaded = [m.sem(f"e2_w_loaded{i}") for i in range(2)]
        with ExitStack() as s3:
            m3 = Mem(nc, s3)
            rows = m3.sb("rows2", [P, T, D])
            normed_router_phase(nc, io, "n2_", x2, rows, lg, "F_Wr", "one2", "zero2", "F_br",
                                lambda sp: [load_second_experts(sp, io, e2w, e2w_loaded, e, e) for e in range(2)])
            route_phase(nc, io, "r2_", lg, slot2, weight2, None, True)
            scatter_phase(nc, "s2_", rows, slot2, xg2, 2 * N, (zeroed, NZ))
        second_experts_phase(nc, io, xg2, yg2, e2w, e2w_loaded)
        output_phase(nc, io, yg2, slot2, weight2, x2)


def kernel(**inputs):
    import concourse.bacc as bacc
    from concourse.bass_utils import run_bass_kernel_spmd

    a = {k: np.ascontiguousarray(v) for k, v in inputs.items()}
    X, A, Fn = "L0_xattn_", "L0_attn_", "L0_ffn_"

    def by_partition(v):
        return np.ascontiguousarray(v.reshape(2, P).T)

    ctxT = np.ascontiguousarray(a["ctx_768"].transpose(2, 0, 1))
    arrays = {"x": a["x"].reshape(N, D), "ctxT": ctxT, "ctx_last": np.ascontiguousarray(ctxT[:, :, -1])}
    for k in ("Wq", "Wk", "Wv", "Wo", "bo"):
        arrays[k] = a[X + k]
    for k in ("bq", "bk", "bv"):
        arrays[k] = by_partition(a[X + k])
    for k, name in (("g1", "ln1_g"), ("b1", "ln1_b"), ("g2", "ln2_g"), ("b2", "ln2_b"), ("cb", "conv_b")):
        arrays[k] = by_partition(a[A + name])
    for k, name in (("Wzx", "Win_ssm"), ("Wgate", "Wgate"), ("Wr", "Wr"), ("br", "br"), ("Wos", "Wout_ssm"),
                    ("Wout2", "Wout"), ("ls1", "ls1"), ("ls2", "ls2"), ("step_bias", "step_bias"), ("Wg", "Wg"),
                    ("W1", "W1"), ("W2", "W2"), ("W3", "W3")):
        arrays[k] = a[A + name]
    arrays["cw"] = np.ascontiguousarray(a[A + "conv_w"].reshape(2, P, 4).transpose(1, 0, 2))
    arrays["Wqk2"] = np.ascontiguousarray(a[A + "Wqkv"][:, :2 * D])
    arrays["Wv2"] = np.ascontiguousarray(a[A + "Wqkv"][:, 2 * D:])
    for k, name in (("F_Wr", "Wr"), ("F_br", "br"), ("F_W1", "W1"), ("F_W2", "W2"), ("F_b2", "b2")):
        arrays[k] = a[Fn + name]
    arrays["F_b1"] = np.ascontiguousarray(a[Fn + "b1"].reshape(E, F2 // P, P).transpose(2, 0, 1))
    arrays.update(constants())

    nc = bacc.Bacc("TRN2", target_bir_lowering=False, num_devices=1)
    io = {}
    ins = {}
    for name, v in arrays.items():
        ins["in_" + name] = v
        io[name] = nc.dram_tensor("in_" + name, v.shape, mybir.dt.from_np(v.dtype), kind="ExternalInput").ap()
    io["out"] = nc.dram_tensor("out_x", (N, D), F32, kind="ExternalOutput").ap()
    build_program(nc, io)
    r = run_bass_kernel_spmd(nc, [ins], core_ids=[0])
    return r.results[0]["out_x"].reshape(B, L, D)
```

```python
from contextlib import ExitStack

import numpy as np
import concourse.bass as bass
from concourse import mybir

F32 = mybir.dt.float32
I32 = mybir.dt.int32
U32 = mybir.dt.uint32
F32R = mybir.dt.float32r
ALU = mybir.AluOpType
ACT = mybir.ActivationFunctionType
AXX = mybir.AxisListType.X

P = 128
B, L, D = 64, 32, 256
S, DC = 257, 192
H, HD = 16, 16
N = B * L
T = N // P
SE = S + 1
G = 4
CLAMP = 10000.0
SCALE = HD ** -0.5
EPS = 1e-5


class Mem:

    def __init__(self, nc, st, clear=False):
        self.nc, self.st, self.sems = nc, st, []
        if clear:
            st.callback(self.clear)

    def clear(self):
        self.nc.clear_and_free_semaphores(self.sems)
        self.nc.all_engine_barrier()

    def sb(self, name, shape, dt=F32):
        return self.st.enter_context(self.nc.sbuf_tensor(name, shape, dt))

    def ps(self, name, shape, dt=F32):
        return self.st.enter_context(self.nc.psum_tensor(name, shape, dt))

    def sem(self, name):
        self.sems.append(self.nc.alloc_semaphore(name))
        return self.sems[-1]


class Early:

    def __init__(self, mem, pre):
        self.mem, self.pre, self.loads, self.tensors = mem, pre, [], {}
        self.loaded = mem.sem(pre + "loaded")

    def add(self, name, shape, *loads):
        t = self.mem.sb(self.pre + name, shape)
        self.tensors[name] = t
        self.loads += [(part(t), src) for part, src in loads]
        self.total = 16 * len(self.loads)

    def load(self, sp):
        for dst, src in self.loads:
            sp.dma_start(dst, src).then_inc(self.loaded, 16)

    def __getitem__(self, name):
        return self.tensors[name]


def whole(t):
    return t[:]


def by_rows(w):
    return w.rearrange("(k p) m -> p k m", p=P)


def rsqrt_refined(dve, rt, r, t, sem, n0, var):
    dve.reciprocal(r, rt).then_inc(sem, 1)
    dve.wait_ge(sem, n0 + 1)
    dve.tensor_tensor(t, r, r, ALU.mult).then_inc(sem, 1)
    dve.wait_ge(sem, n0 + 2)
    dve.tensor_tensor(t, t, var, ALU.mult).then_inc(sem, 1)
    dve.wait_ge(sem, n0 + 3)
    dve.tensor_scalar(t, t, -0.5, 1.5, ALU.mult, ALU.add).then_inc(sem, 1)
    dve.wait_ge(sem, n0 + 4)
    dve.tensor_tensor(r, r, t, ALU.mult).then_inc(sem, 1)
    dve.wait_ge(sem, n0 + 5)


def query_phase(nc, io, xs, qs, load_early):
    with ExitStack() as st:
        p = Mem(nc, st)
        ident = p.sb("qa_ident", [P, P])
        wq = p.sb("qa_wq", [P, 2, D])
        bq = p.sb("qa_bq", [P, 2])
        stats = p.sb("qa_stats", [P, T, 6])
        mv = p.sb("qa_mv", [P, T, 2])
        ve = p.sb("qa_ve", [P, T])
        rt = p.sb("qa_rt", [P, T])
        rs = p.sb("qa_rs", [P, T])
        tmp = p.sb("qa_tmp", [P, T])
        xn = p.sb("qa_xn", [P, 4, D])
        xnT = p.sb("qa_xnT", [P, 2, 2, 4 * P])
        tp = p.ps("qa_tp", [P, 2, 2, 4 * P])
        qp = p.ps("qa_qp", [P, 2, 2, 4 * P])
        x_loaded = [p.sem(f"qa_x_loaded{c}") for c in range(4)]
        w_loaded = p.sem("qa_w_loaded")
        step = p.sem("qa_step")
        var_ready = p.sem("qa_var_ready")
        sqrt_ready = p.sem("qa_sqrt_ready")
        xn_ready = p.sem("qa_xn_ready")
        tp_ready = p.sem("qa_tp_ready")
        xnT_ready = p.sem("qa_xnT_ready")
        qp_ready = p.sem("qa_qp_ready")
        q_stored = p.sem("qa_q_stored")
        rest_stored = p.sem("qa_rest_stored")
        block = st.enter_context(nc.Block())

        @block.sync
        def _(sp):
            for c in range(4):
                sp.dma_start(xs[:, 4 * c:4 * c + 4, :],
                             io["x"].rearrange("(t p) d -> p t d", p=P)[:, 4 * c:4 * c + 4, :]).then_inc(x_loaded[c], 16)
            sp.dma_start(wq[:], io["Wq"].rearrange("(k p) m -> p k m", p=P)).then_inc(w_loaded, 16)
            sp.dma_start(bq[:], io["bq"]).then_inc(w_loaded, 16)
            sp.dma_start(ident[:], io["c_ident"]).then_inc(w_loaded, 16)
            load_early(sp)

        @block.vector
        def _(dve):
            for t in range(T):
                dve.wait_ge(x_loaded[t // 4], 16)
                dve.bn_stats(stats[:, t, :], xs[:, t, :]).then_inc(step, 1)
            for t in range(T):
                dve.wait_ge(step, t + 1)
                dve.bn_aggr(mv[:, t, :], stats[:, t, :]).then_inc(step, 1)
            dve.wait_ge(step, 2 * T)
            dve.tensor_scalar(ve[:], mv[:, :, 1], EPS, None, ALU.add).then_inc(var_ready, 1)
            dve.wait_ge(sqrt_ready, 1)
            rsqrt_refined(dve, rt[:], rs[:], tmp[:], step, 2 * T, ve[:])

            def rest(c):
                for h in range(2):
                    dve.wait_ge(q_stored, 2 * c + h + 1)
                    part = [qs[:, a, h, 512 * c:512 * c + 512] for a in range(2)]
                    dve.scalar_tensor_tensor(out=part[1], in0=qp[:, c % 2, h, :], scalar=bq[:, h:h + 1], in1=part[0],
                                             op0=ALU.add, op1=ALU.subtract).then_inc(rest_stored, 1)

            def normalise(c):
                for j in range(4):
                    t = 4 * c + j
                    if c:
                        dve.wait_ge(tp_ready, 2 * c)
                    dve.tensor_scalar(xn[:, j, :], xs[:, t, :], mv[:, t, 0:1], rs[:, t:t + 1],
                                      ALU.subtract, ALU.mult).then_inc(xn_ready, 1)

            normalise(0)
            for c in range(4):
                if c < 3:
                    normalise(c + 1)
                if c >= 2:
                    dve.wait_ge(qp_ready, 2 * c - 2)
                for k in range(2):
                    dve.wait_ge(tp_ready, 2 * c + k + 1)
                    dve.tensor_copy(xnT[:, c % 2, k, :], tp[:, c % 2, k, :]).then_inc(xnT_ready, 1)
                if c:
                    rest(c - 1)
            rest(3)

        @block.scalar
        def _(act):
            act.wait_ge(var_ready, 1)
            act.activation(rt[:], ve[:], ACT.Sqrt).then_inc(sqrt_ready, 1)
            act.wait_ge(w_loaded, 48)
            for c in range(4):
                for h in range(2):
                    act.wait_ge(qp_ready, 2 * c + h + 1)
                    act.activation(qs[:, 0, h, 512 * c:512 * c + 512], qp[:, c % 2, h, :], ACT.Identity,
                                   bias=bq[:, h:h + 1]).then_inc(q_stored, 1)

        @block.tensor
        def _(pe):
            pe.wait_ge(w_loaded, 48)

            def turn(c):
                if c >= 2:
                    pe.wait_ge(xnT_ready, 2 * c - 2)
                pe.wait_ge(xn_ready, 4 * c + 4)
                for k in range(2):
                    for j in range(4):
                        mm = pe.transpose(tp[:, c % 2, k, P * j:P * j + P], xn[:, j, P * k:P * k + P], ident[:])
                    mm.then_inc(tp_ready, 1)

            turn(0)
            for c in range(4):
                if c < 3:
                    turn(c + 1)
                pe.wait_ge(xnT_ready, 2 * c + 2)
                if c >= 2:
                    pe.wait_ge(q_stored, 2 * c - 2)
                    pe.wait_ge(rest_stored, 2 * c - 2)
                for h in range(2):
                    for k in range(2):
                        mm = pe.matmul(qp[:, c % 2, h, :], wq[:, k, P * h:P * h + P], xnT[:, c % 2, k, :],
                                       start=(k == 0), stop=(k == 1))
                    mm.then_inc(qp_ready, 1)


def cross_attention_weights(io, m):
    w = Early(m, "xw_")
    for name in ("Wk", "Wv"):
        w.add(name, [P, 2, D], (lambda t: t[:, 0, :], io[name][0:P, :]),
              (lambda t: t[0:64, 1, :], io[name][P:DC, :]), (lambda t: t[64:P, 1, :], io[name][P:DC, :]))
    for name, shape in (("bk", [P, 2]), ("c_ident", [P, P]), ("c_istack", [P, L]), ("c_mask8s", [P, 8]),
                        ("c_mask64", [P, 64])):
        w.add(name, shape, (whole, io[name]))
    w.add("bo", [P, D], (whole, io["bo"].partition_broadcast(P)))
    w.add("ctx_last", [P, 2, B], (lambda t: t[:, 0, :], io["ctx_last"][0:P, :]),
          (lambda t: t[0:64, 1, :], io["ctx_last"][P:DC, :]))
    return w


def cross_attention_phase(nc, io, w, xs, qs, oT, rawsum, csum, zero_slots, zeroed):
    with ExitStack() as st:
        p = Mem(nc, st, clear=True)
        wk, wv, bk, bo, cl = w["Wk"], w["Wv"], w["bk"], w["bo"], w["ctx_last"]
        ident, istack, mask8, mask64 = w["c_ident"], w["c_istack"], w["c_mask8s"], w["c_mask64"]
        zero = p.sb("xa_zero", [P, 1, D])
        wks = p.sb("xa_wks", [P, 3, D], F32R)
        wvs = p.sb("xa_wvs", [P, 3, D], F32R)
        pad = p.sb("xa_pad", [P, 8])
        floor = p.sb("xa_floor", [P, 1])
        vl = p.sb("xa_vl", [B, D])
        vlast = p.sb("xa_vlast", [G, B, G * 65])
        ctx = p.sb("xa_ctx", [P, 2, 2, 2, S])
        cs = p.sb("xa_cs", [P, 2, 2, 2, SE], F32R)
        kT = p.sb("xa_kT", [P, 2, 2, 2, SE], F32R)
        v = p.sb("xa_v", [P, 4, 2, G, 65])
        qbd = p.sb("xa_qbd", [P, 2, 2, G, P], F32R)
        mx = p.sb("xa_mx", [P, 2, G])
        nm = p.sb("xa_nm", [P, 2, G])
        low = p.sb("xa_low", [P, 2, G])
        pr = p.sb("xa_pr", [P, 2, G, S])
        pT = p.sb("xa_pT", [P, 2, G, 2, P])
        pTl = p.sb("xa_pTl", [G, 2, P])
        unused = p.sb("xa_unused", [P, 2, S])
        rinv = p.sb("xa_rinv", [P, 2, G])
        om = p.sb("xa_om", [P, D])
        on = p.sb("xa_on", [P, D])
        kvp = p.ps("xa_kvp", [P, 2, 512])
        sc = p.ps("xa_sc", [P, G, 512])
        ptp = p.ps("xa_ptp", [P, 512])
        ob = p.ps("xa_ob", [P, 512])
        OT, PL = 260, 324

        xs_ready = p.sem("xa_xs_ready")
        zero_set = p.sem("xa_zero_set")
        ctx_loaded = [p.sem(f"xa_ctx_loaded{i}") for i in range(2)]
        vlp_ready = p.sem("xa_vlp_ready")
        vl_ready = p.sem("xa_vl_ready")
        vlast_loaded = p.sem("xa_vlast_loaded")
        vlast_ready = p.sem("xa_vlast_ready")
        ones_ready = p.sem("xa_ones_ready")
        floor_ready = p.sem("xa_floor_ready")
        kp_ready = p.sem("xa_kp_ready")
        kh_ready = p.sem("xa_kh_ready")
        kl_ready = p.sem("xa_kl_ready")
        wh_ready = p.sem("xa_wh_ready")
        wl_ready = p.sem("xa_wl_ready")
        pad_ready = p.sem("xa_pad_ready")
        ch_pad_ready = p.sem("xa_ch_pad_ready")
        ch_ready = p.sem("xa_ch_ready")
        cr_ready = p.sem("xa_cr_ready")
        vp_ready = p.sem("xa_vp_ready")
        v_ready = p.sem("xa_v_ready")
        q_ready = p.sem("xa_q_ready")
        s_ready = p.sem("xa_s_ready")
        mx_step = p.sem("xa_mx_step")
        nm_ready = p.sem("xa_nm_ready")
        exp_ready = p.sem("xa_exp_ready")
        low_ready = p.sem("xa_low_ready")
        pr_ready = p.sem("xa_pr_ready")
        ptp_ready = p.sem("xa_ptp_ready")
        plp_ready = p.sem("xa_plp_ready")
        pT_ready = [p.sem(f"xa_pT_ready{h}") for h in range(2)]
        pTl_ready = p.sem("xa_pTl_ready")
        o_ready = p.sem("xa_o_ready")
        rinv_ready = p.sem("xa_rinv_ready")
        om_ready = p.sem("xa_om_ready")
        on_ready = p.sem("xa_on_ready")
        oTp_ready = p.sem("xa_oTp_ready")
        oT_stored = p.sem("xa_oT_stored")
        csum_ready = p.sem("xa_csum_ready")
        block = st.enter_context(nc.Block())

        def run_steps(eng, step, first, last):
            for b in range(first, 4):
                step(b, b % 2, b // 2)
            with eng.Fori(1, B // 4 - 1) as i:
                for j in range(4):
                    step(i * 4 + j, j % 2, j // 2)
            for b in range(B - 4, last):
                step(b, b % 2, b // 2 % 2)

        @block.sync
        def _(sp):
            def load(i, slot):
                sp.dma_start(ctx[:, slot, 0, :, :], io["ctxT"][0:P, bass.ds(i * 2, 2), :]).then_inc(ctx_loaded[slot], 16)
                for r in (0, 64):
                    sp.dma_start(ctx[r:r + 64, slot, 1, :, :],
                                 io["ctxT"][P:DC, bass.ds(i * 2, 2), :]).then_inc(ctx_loaded[slot], 16)

            load(0, 0)
            load(1, 1)
            sp.dma_start(vlast[:], io["c_vlast"]).then_inc(vlast_loaded, 16)
            sp.wait_ge(vl_ready, 1)
            sp.wait_ge(vlast_loaded, 16)
            for g in range(G):
                sp.dma_start(vlast[g:g + 1, :, 65 * g:65 * g + 64],
                             vl[:, 64 * g:64 * g + 64]).then_inc(vlast_ready, 16)
            sp.wait_ge(zero_set, 1)
            zero_slots(sp, zero)
            with sp.Fori(1, B // 4) as i:
                for j in range(2):
                    sp.wait_ge(cr_ready, i * 4 + (2 * j - 2))
                    sp.wait_ge(csum_ready, i * 8 + (4 * j - 4))
                    load(i * 2 + j, j)
            sp.wait_ge(*zeroed)

        @block.tensor
        def _(pe):
            pe.wait_ge(w.loaded, w.total)
            pe.matmul(ptp[0:B, 0:D], cl[:, 0, :], wv[:, 0, :], start=True, stop=False)
            pe.matmul(ptp[0:B, 0:D], cl[0:64, 1, :], wv[0:64, 1, :], start=False, stop=True).then_inc(vlp_ready, 1)

            def project_k(b, par):
                pe.wait_ge(ch_ready, b + 1)
                pe.wait_ge(cr_ready, b + 1)
                high, rest = cs[:, par, 0], cs[:, par, 1]
                for h in range(2):
                    if h == 0:
                        pe.wait_ge(kh_ready, b * 2)
                        pe.wait_ge(kl_ready, b * 2)
                    else:
                        pe.wait_ge(v_ready, b)
                    out, c = kvp[:, (par + h) % 2, 0:SE], slice(P * h, P * h + P)
                    pe.matmul(out, wks[:, 0, c], high[:, 0, :], start=True, stop=False)
                    pe.matmul(out, wks[:, 0, c], rest[:, 0, :], start=False, stop=False)
                    pe.matmul(out, wks[:, 1, c], high[:, 0, :], start=False, stop=False)
                    pe.matmul(out, wks[:, 2, c], high[:, 1, :], start=False, stop=False)
                    pe.matmul(out, wks[0:64, 2, c], rest[0:64, 1, :], start=False, stop=True).then_inc(kp_ready, 1)

            def project_v(b, par):
                pe.wait_ge(kh_ready, b * 2 + 1)
                pe.wait_ge(kl_ready, b * 2 + 1)
                for t in range(2):
                    out = kvp[:, par, D * t:D * t + D]
                    high, rest = [[cs[:, par, a, k, P * t:P * t + P] for k in range(2)] for a in range(2)]
                    pe.matmul(out, high[0], wvs[:, 0, :], start=True, stop=False)
                    pe.matmul(out, rest[0], wvs[:, 0, :], start=False, stop=False)
                    pe.matmul(out, high[0], wvs[:, 1, :], start=False, stop=False)
                    pe.matmul(out, high[1], wvs[:, 2, :], start=False, stop=False)
                    mm = pe.matmul(out, rest[1][0:64], wvs[0:64, 2, :], start=False, stop=True)
                mm.then_inc(vp_ready, 1)

            def scores(b, par):
                pe.wait_ge(q_ready, b * 2 + 2)
                for h in range(2):
                    pe.wait_ge(kh_ready, b * 2 + h + 1)
                    pe.wait_ge(kl_ready, b * 2 + h + 1)
                    if not (isinstance(b, int) and b == 0):
                        pe.wait_ge(exp_ready, b * 4 + (2 * h - 2))
                    for g in (2 * h, 2 * h + 1):
                        out = sc[:, g, 0:SE]
                        pe.matmul(out, qbd[:, par, 0, g, :], kT[:, par, 0, h, :], start=True, stop=False)
                        pe.matmul(out, qbd[:, par, 0, g, :], kT[:, par, 1, h, :], start=False, stop=False)
                        mm = pe.matmul(out, qbd[:, par, 1, g, :], kT[:, par, 0, h, :], start=False, stop=True)
                    mm.then_inc(s_ready, 1)

            def turn(b, par, h):
                pe.wait_ge(pr_ready, b * 4 + (2 * h + 2))
                if h == 1:
                    if not (isinstance(b, int) and b == 0):
                        pe.wait_ge(om_ready, b)
                        pe.wait_ge(oT_stored, b - 1)
                    pe.transpose(ob[0:G, PL:PL + P], pr[:, par, :, S - 1], ident[:]).then_inc(plp_ready, 1)
                pe.wait_ge(pT_ready[1 - h], b + h)
                for g in (2 * h, 2 * h + 1):
                    for t in range(2):
                        c = (2 * (g % 2) + t) * P
                        mm = pe.transpose(ptp[:, c:c + P], pr[:, par, g, P * t:P * t + P], ident[:])
                mm.then_inc(ptp_ready, 1)

            def values(b, par, vs):
                pe.wait_ge(pTl_ready, b + 1)
                pe.wait_ge(v_ready, b + 1)
                pe.matmul(ob[:, 0:G * 65], pTl[:, par, :], vlast[:, b, :], start=True, stop=False, skip_group_check=True)
                for h in range(2):
                    pe.wait_ge(pT_ready[h], b + 1)
                for g in range(G):
                    for t in range(2):
                        mm = pe.matmul(ob[:, 65 * g:65 * g + 65], pT[:, par, g, t, :], v[:, vs, t, g, :],
                                       start=False, stop=(g == G - 1 and t == 1), skip_group_check=True)
                mm.then_inc(o_ready, 1)

            def turn_output(b, par):
                pe.wait_ge(on_ready, b + 1)
                pe.wait_ge(oT_stored, b)
                for h in range(2):
                    mm = pe.matmul(ob[:, OT + L * h:OT + L * h + L], on[:, P * h:P * h + P], istack[:],
                                   start=True, stop=True, skip_group_check=True)
                mm.then_inc(oTp_ready, 1)

            def step(b, par, slot):
                static = isinstance(b, int)
                scores(b, par)
                if not static or b >= 1:
                    turn(b - 1, 1 - par, 0)
                if not static or b < B - 1:
                    project_k(b + 1, 1 - par)
                if not static or b >= 1:
                    turn(b - 1, 1 - par, 1)
                if not static or b < B - 1:
                    project_v(b + 1, 1 - par)
                if not static or b >= 1:
                    values(b - 1, 1 - par, (2 * slot + par + 3) % 4)
                if not static or b >= 2:
                    turn_output(b - 2, par)

            pe.wait_ge(wh_ready, 4)
            pe.wait_ge(wl_ready, 4)
            project_k(0, 0)
            pe.wait_ge(vlast_ready, 64)
            project_v(0, 0)
            run_steps(pe, step, 0, B)
            turn(B - 1, 1, 0)
            turn(B - 1, 1, 1)
            values(B - 1, 1, 3)
            turn_output(B - 2, 0)
            turn_output(B - 1, 1)

        @block.gpsimd
        def _(pool):
            pool.memset(floor[:], -CLAMP).then_inc(floor_ready, 1)
            pool.memset(zero[:], 0.0).then_inc(zero_set, 1)
            for i in range(4):
                pool.memset(v[:, i, :, :, 64], 1.0).then_inc(ones_ready, 1)
            pool.memset(pad[:], 0.0).then_inc(pad_ready, 1)
            pool.wait_ge(w.loaded, w.total)

            def queries(b, par):
                if not (isinstance(b, int) and b < 2):
                    pool.wait_ge(s_ready, b * 2 - 2)
                msk = mask8[:].unsqueeze(1).unsqueeze(3).to_broadcast([P, 2, 8, L])
                for a in range(2):
                    src = qs[:, a, :, bass.ds(b * L, L)].unsqueeze(2).to_broadcast([P, 2, 8, L])
                    dst = qbd[:, par, a].rearrange("p (h j) (e q) -> p h (j e) q", h=2, q=L)
                    pool.tensor_tensor(dst, src, msk, ALU.mult).then_inc(q_ready, 1)

            def rest_of_context(b, par, slot):
                pool.wait_ge(ch_ready, b + 1)
                pool.tensor_tensor(cs[:, par, 1, :, 0:S], ctx[:, slot, :, par, :], cs[:, par, 0, :, 0:S],
                                   ALU.subtract).then_inc(cr_ready, 1)

            def normalise(b, par):
                pool.wait_ge(rinv_ready, b + 1)
                pool.wait_ge(om_ready, b + 1)
                pool.wait_ge(oTp_ready, b)
                pool.tensor_tensor(on[:].rearrange("p (g c) -> p g c", g=G),
                                   om[:].rearrange("p (g c) -> p g c", g=G),
                                   rinv[:, par, :].unsqueeze(2).to_broadcast([P, G, 64]),
                                   ALU.mult).then_inc(on_ready, 1)

            def step(b, par, slot):
                static = isinstance(b, int)
                if not static or b < B - 1:
                    queries(b + 1, 1 - par)
                if not static or b >= 2:
                    normalise(b - 2, par)
                if not static or b < B - 2:
                    rest_of_context(b + 2, par, 1 - slot)
                if static:
                    c = b if b < 4 else b - B + 8
                    x = xs[:, T // 8 * c:T // 8 * c + T // 8, :]
                    pool.tensor_tensor(x, x, bo[:].unsqueeze(1).to_broadcast([P, T // 8, D]), ALU.add).then_inc(xs_ready, 1)

            queries(0, 0)
            for b in range(2):
                rest_of_context(b, b, 0)
            run_steps(pool, step, 0, B)
            normalise(B - 2, 0)
            normalise(B - 1, 1)

        @block.scalar
        def _(act):
            act.wait_ge(w.loaded, w.total)
            act.wait_ge(floor_ready, 1)

            def high_k(b, par, h):
                if not (isinstance(b, int) and b < 2):
                    act.wait_ge(s_ready, b * 2 - 2)
                act.wait_ge(kp_ready, b * 2 + h + 1)
                act.activation(kT[:, par, 0, h, :], kvp[:, (par + h) % 2, 0:SE], ACT.Identity,
                               bias=bk[:, h:h + 1]).then_inc(kh_ready, 1)

            def high_context(b, par, slot):
                if isinstance(b, int):
                    act.wait_ge(ctx_loaded[slot], 48 * (b // 4 + 1))
                elif par == 0:
                    act.wait_ge(ctx_loaded[slot], b * 12 + (48 if slot == 0 else 24))
                if not (isinstance(b, int) and b < 2):
                    act.wait_ge(vp_ready, b - 1)
                act.activation(cs[:, par, 0, :, 0:S], ctx[:, slot, :, par, :], ACT.Copy).then_inc(ch_ready, 1)
                if not (isinstance(b, int) and b == 0):
                    act.wait_ge(csum_ready, b * 2)
                sum_context(b, par, slot)

            def sum_context(b, par, slot):
                for k, rows in ((0, P), (1, 64)):
                    act.activation(unused[0:rows, k, :], ctx[0:rows, slot, k, par, :], ACT.Copy,
                                   accum_out=csum[0:rows, k, bass.ds(b, 1)]).then_inc(csum_ready, 1)

            def floors(b, par, h):
                act.wait_ge(nm_ready, b * 2 + h + 1)
                if not (isinstance(b, int) and b < 2):
                    act.wait_ge(pr_ready, b * 4 - 4)
                act.activation(low[:, par, 2 * h:2 * h + 2], nm[:, par, 2 * h:2 * h + 2], ACT.Exp,
                               bias=floor[:]).then_inc(low_ready, 1)

            def exponentials(b, par, h):
                if h == 0 and not (isinstance(b, int) and b < 2):
                    act.wait_ge(plp_ready, b - 1)
                for g in (2 * h, 2 * h + 1):
                    act.activation(pr[:, par, g, :], sc[:, g, 0:S], ACT.Exp, bias=nm[:, par, g:g + 1],
                                   scale=-1.0, accum_out=rawsum[:, bass.ds(b * G + g, 1)]).then_inc(exp_ready, 1)

            def store_probabilities(b, par):
                act.wait_ge(ptp_ready, b * 2 + 1)
                if not (isinstance(b, int) and b < 2):
                    act.wait_ge(o_ready, b - 1)
                act.activation(pT[:, par, 0:2].rearrange("p g t c -> p (g t c)"), ptp[:], ACT.Copy).then_inc(pT_ready[0], 1)

            def step(b, par, slot):
                static = isinstance(b, int)
                if not static or b >= 1:
                    store_probabilities(b - 1, 1 - par)
                if not static or b < B - 1:
                    high_k(b + 1, 1 - par, 0)
                floors(b, par, 0)
                exponentials(b, par, 0)
                if not static or b < B - 1:
                    high_k(b + 1, 1 - par, 1)
                floors(b, par, 1)
                exponentials(b, par, 1)
                if not static or b < B - 2:
                    high_context(b + 2, par, 1 - slot)

            for a, ws in ((wk, wks), (wv, wvs)):
                for k in range(2):
                    act.activation(ws[:, 2 * k, :], a[:, k, :], ACT.Copy).then_inc(wh_ready, 1)
            act.wait_ge(pad_ready, 1)
            act.activation(cs[:, :, :, :, S].rearrange("p a b c -> p (a b c)"), pad[:], ACT.Copy).then_inc(ch_pad_ready, 1)
            for b in range(2):
                high_context(b, b, 0)
            high_k(0, 0, 0)
            high_k(0, 0, 1)
            run_steps(act, step, 0, B)
            store_probabilities(B - 1, 1)

        @block.vector
        def _(dve):
            dve.wait_ge(w.loaded, w.total)
            dve.wait_ge(ones_ready, 4)
            dve.wait_ge(vlp_ready, 1)
            dve.tensor_copy(vl[:], ptp[0:B, 0:D]).then_inc(vl_ready, 1)

            for n, (a, ws) in enumerate(((wk, wks), (wv, wvs))):
                dve.wait_ge(wh_ready, 2 * n + 2)
                dve.tensor_tensor(ws[:, 1, :], a[:, 0, :], ws[:, 0, :], ALU.subtract).then_inc(wl_ready, 1)
                dve.tensor_tensor(ws[64:P, 2, :], a[64:P, 1, :], ws[64:P, 2, :], ALU.subtract).then_inc(wl_ready, 1)

            def rest_k(b, par, h):
                dve.wait_ge(kh_ready, b * 2 + h + 1)
                dve.scalar_tensor_tensor(out=kT[:, par, 1, h, :], in0=kvp[:, (par + h) % 2, 0:SE], scalar=bk[:, h:h + 1],
                                         in1=kT[:, par, 0, h, :], op0=ALU.add, op1=ALU.subtract).then_inc(kl_ready, 1)

            def store_v(b, par, vs):
                dve.wait_ge(vp_ready, b + 1)
                if not (isinstance(b, int) and b < 4):
                    dve.wait_ge(o_ready, b - 3)
                dve.tensor_copy(v[:, vs, :, :, 0:64], kvp[:, par, :].rearrange("p (t g c) -> p t g c", t=2, g=G)
                                ).then_inc(v_ready, 1)

            def least(b, par, h):
                g = slice(2 * h, 2 * h + 2)
                dve.wait_ge(s_ready, b * 2 + h + 1)
                dve.tensor_reduce(mx[:, par, g], sc[:, g, 0:S], AXX, ALU.min).then_inc(mx_step, 1)

            def bounds(b, par, h):
                g = slice(2 * h, 2 * h + 2)
                dve.wait_ge(mx_step, b * 2 + h + 1)
                if not (isinstance(b, int) and b < 2):
                    dve.wait_ge(low_ready, b * 2 + (h - 3))
                dve.tensor_scalar(nm[:, par, g], mx[:, par, g], -CLAMP, CLAMP, ALU.max, ALU.min).then_inc(nm_ready, 1)

            def store_probabilities(b, par):
                dve.wait_ge(plp_ready, b + 1)
                dve.tensor_copy(pTl[:, par, :], ob[0:G, PL:PL + P]).then_inc(pTl_ready, 1)
                dve.wait_ge(ptp_ready, b * 2 + 2)
                dve.tensor_copy(pT[:, par, 2:4].rearrange("p g t c -> p (g t c)"), ptp[:]).then_inc(pT_ready[1], 1)

            def clamp(b, par, h):
                dve.wait_ge(low_ready, b * 2 + h + 1)
                for g in (2 * h, 2 * h + 1):
                    dve.wait_ge(exp_ready, b * 4 + (g + 1))
                    dve.tensor_scalar(pr[:, par, g, :], pr[:, par, g, :], 1.0, low[:, par, g:g + 1],
                                       ALU.min, ALU.max).then_inc(pr_ready, 1)

            def mask_output(b, par):
                dve.wait_ge(o_ready, b + 1)
                dve.wait_ge(oTp_ready, b)
                dve.wait_ge(on_ready, b)
                o = ob[:, 0:G * 65].rearrange("p (g c) -> p g c", g=G)
                dve.reciprocal(rinv[:, par, :], o[:, :, 64]).then_inc(rinv_ready, 1)
                dve.tensor_tensor(om[:].rearrange("p (g c) -> p g c", g=G), o[:, :, 0:64],
                                  mask64[:].unsqueeze(1).to_broadcast([P, G, 64]), ALU.mult).then_inc(om_ready, 1)

            def store_output(b):
                dve.wait_ge(oTp_ready, b + 1)
                dve.tensor_copy(oT[:, :, bass.ds(b * L, L)],
                                ob[:, OT:OT + 2 * L].rearrange("p (h q) -> p h q", h=2)).then_inc(oT_stored, 1)

            def step(b, par, slot):
                static = isinstance(b, int)
                if not static or b >= 3:
                    store_output(b - 3)
                if not static or b >= 2:
                    mask_output(b - 2, par)
                least(b, par, 0)
                bounds(b, par, 0)
                least(b, par, 1)
                if not static or b < B - 1:
                    rest_k(b + 1, 1 - par, 0)
                bounds(b, par, 1)
                if not static or b >= 1:
                    store_probabilities(b - 1, 1 - par)
                if not static or b < B - 1:
                    rest_k(b + 1, 1 - par, 1)
                clamp(b, par, 0)
                if not static or b < B - 1:
                    store_v(b + 1, 1 - par, (2 * slot + par + 1) % 4)
                clamp(b, par, 1)

            rest_k(0, 0, 0)
            rest_k(0, 0, 1)
            store_v(0, 0, 0)
            run_steps(dve, step, 0, B)
            store_output(B - 3)
            mask_output(B - 2, 0)
            store_probabilities(B - 1, 1)
            store_output(B - 2)
            mask_output(B - 1, 1)
            store_output(B - 1)


def constants():
    p = np.arange(P)
    vl = np.zeros((G, B, G * 65), np.float32)
    for g in range(G):
        vl[g, :, 65 * g + 64] = 1.0
    return {
        "c_ident": np.eye(P, dtype=np.float32),
        "c_istack": (p[:, None] % L == np.arange(L)).astype(np.float32),
        "c_mask8": (p[:, None] // HD == np.arange(8)).astype(np.float32),
        "c_mask8s": -SCALE * (p[:, None] // HD == np.arange(8)).astype(np.float32),
        "c_mask64": (p[:, None] // L == np.arange(64) // HD).astype(np.float32),
        "c_mask4": (p[:, None] // L == np.arange(4)).astype(np.float32),
        "c_onesr": np.ones((1, P), np.float32),
        "c_tri": (p[:, None] < p).astype(np.float32),
        "c_ones": np.ones((P, P), np.float32),
        "c_reset": np.tile((p % T != 0).astype(np.float32), (P, 1)),
        "c_iota": np.tile(np.arange(8, dtype=np.float32), (P, 1)),
        "c_steps": np.tile(P * np.arange(T, dtype=np.float32), (P, 1)),
        "c_tiles": np.tile(np.arange(40, dtype=np.float32), (P, 1)),
        "c_starts": np.tile(P * np.arange(41, dtype=np.float32), (P, 1)),
        "c_low": np.tile(p - float(P), (P, 1)).astype(np.float32),
        "c_p1": (p[:, None] + 1).astype(np.float32),
        "c_copies": np.tile(np.arange(2 * T, dtype=np.float32), (P, 1)),
        "c_first": np.tile(512 * np.arange(8, dtype=np.float32), (P, 1)),
        "one2": np.ones((P, 2), np.float32),
        "zero2": np.zeros((P, 2), np.float32),
        "zero8": np.zeros((8,), np.float32),
        "c_vlast": vl,
    }



V2 = 2 * P
NS = N // V2
BS = V2 // L


class Link:

    def __init__(self, eng, sem, base=0):
        self.eng, self.sem, self.base, self.n = eng, sem, base, 0

    def __call__(self, ins):
        self.n += 1
        ins.then_inc(self.sem, 1)
        self.eng.wait_ge(self.sem, self.base + self.n)


def refine(dve, link, ve, rt, rs, tmp):
    link(dve.reciprocal(rs, rt))
    link(dve.tensor_tensor(tmp, rs, rs, ALU.mult))
    link(dve.tensor_tensor(tmp, tmp, ve, ALU.mult))
    link(dve.tensor_scalar(tmp, tmp, -0.5, 1.5, ALU.mult, ALU.add))
    link(dve.tensor_tensor(rs, rs, tmp, ALU.mult))


def merge_phase(nc, io, oT, rawsum, csum, xs, xin, nT, base, base_written, load_early):
    with ExitStack() as st:
        p = Mem(nc, st)
        ident = p.sb("mg_ident", [P, P])
        onesr = p.sb("mg_onesr", [1, P])
        wv = p.sb("mg_wv", [P, 2, D])
        wo = p.sb("mg_wo", [P, 2, D])
        bv = p.sb("mg_bv", [P, 2])
        g1 = p.sb("mg_g1", [P, 2])
        b1 = p.sb("mg_b1", [P, 2])
        same = p.sb("mg_same", [P, B * G])
        ok = p.sb("mg_ok", [P, 1])
        ok1 = p.sb("mg_ok1", [1, 1])
        bad = p.sb("mg_bad", [P, 1], U32)
        mean = p.sb("mg_mean", [P, 2, B])
        ost = p.sb("mg_ost", [P, 2, 2, V2])
        stats = p.sb("mg_stats", [P, T, 6])
        mv = p.sb("mg_mv", [P, T, 2])
        ve = p.sb("mg_ve", [P, T])
        rt = p.sb("mg_rt", [P, T])
        rs = p.sb("mg_rs", [P, T])
        tmp = p.sb("mg_tmp", [P, T])
        xh = p.sb("mg_xh", [P, 2, 2, D])
        fp = p.ps("mg_fp", [P, 512])
        xo = p.ps("mg_xo", [P, 2, 2, D])
        tp = p.ps("mg_tp", [P, 2, 2, V2])
        loaded = p.sem("mg_loaded")
        guarded = p.sem("mg_guarded")
        xin_ready = p.sem("mg_xin_ready")
        base_ready = p.sem("mg_base_ready")
        okT_ready = p.sem("mg_okT_ready")
        mean_ready = p.sem("mg_mean_ready")
        ok_ready = p.sem("mg_ok_ready")
        okb_ready = p.sem("mg_okb_ready")
        ost_ready = p.sem("mg_ost_ready")
        xo_ready = p.sem("mg_xo_ready")
        xo_free = p.sem("mg_xo_free")
        var_ready = p.sem("mg_var_ready")
        sqrt_ready = p.sem("mg_sqrt_ready")
        xh_ready = p.sem("mg_xh_ready")
        tp_ready = p.sem("mg_tp_ready")
        nT_stored = p.sem("mg_nT_stored")
        step = p.sem("mg_step")
        block = st.enter_context(nc.Block())
        NLOAD = 8

        @block.sync
        def _(sp):
            for dst, src in ((ident[:], io["c_ident"]), (onesr[:], io["c_onesr"]), (wv[:, 0, :], io["Wv"][0:P, :]),
                             (wv[0:64, 1, :], io["Wv"][P:DC, :]), (wo[:], io["Wo"].rearrange("(k p) m -> p k m", p=P)),
                             (bv[:], io["bv"]), (g1[:], io["g1"]), (b1[:], io["b1"])):
                sp.dma_start(dst, src).then_inc(loaded, 16)
            load_early(sp)
            for i in range(4):
                sp.wait_ge(base_ready, i + 1)
                sp.dma_start(base[:, 4 * i:4 * i + 4, :], xs[:, 4 * i:4 * i + 4, :]).then_inc(base_written, 16)
            sp.wait_ge(base_written, 64)

        @block.gpsimd
        def _(pool):
            for i in range(4):
                pool.wait_ge(xin_ready, 4 * i + 4)
                pool.tensor_tensor(xs[:, 4 * i:4 * i + 4, :], xs[:, 4 * i:4 * i + 4, :],
                                   xin[:, 4 * i:4 * i + 4, :], ALU.add).then_inc(base_ready, 1)

        @block.tensor
        def _(pe):
            pe.wait_ge(loaded, 16 * NLOAD)
            for h in range(2):
                for k, rows in ((0, P), (1, 64)):
                    mm = pe.matmul(fp[:, B * h:B * h + B], wv[0:rows, k, P * h:P * h + P], csum[0:rows, k, :],
                                   start=(k == 0), stop=(k == 1))
            mm.then_inc(mean_ready, 1)
            pe.wait_ge(ok_ready, 2)
            pe.transpose(fp[0:1, 0:P], ok[:], ident[:]).then_inc(okT_ready, 1)
            pe.wait_ge(ok_ready, 3)
            pe.matmul(fp[:, 256:257], onesr[:], ok1[:], start=True, stop=True).then_inc(okb_ready, 1)
            for s in range(NS):
                pe.wait_ge(ost_ready, s * 2 + 2)
                if s >= 2:
                    pe.wait_ge(xo_free, s - 1)
                for t in range(2):
                    for k in range(2):
                        mm = pe.matmul(xo[:, s % 2, t, :], ost[:, s % 2, k, P * t:P * t + P], wo[:, k, :],
                                       start=(k == 0), stop=(k == 1))
                mm.then_inc(xo_ready, 1)
            with pe.Fori(0, NS // 2) as i:
                for j in range(2):
                    s = i * 2 + j
                    pe.wait_ge(xh_ready, s * 2 + 2)
                    pe.wait_ge(nT_stored, s * 2 + 2)
                    for k in range(2):
                        for t in range(2):
                            mm = pe.transpose(tp[:, j, k, P * t:P * t + P], xh[:, j, t, P * k:P * k + P], ident[:])
                    mm.then_inc(tp_ready, 1)

        @block.vector
        def _(dve):
            link = Link(dve, step)
            dve.wait_ge(loaded, 16 * NLOAD)
            link(dve.tensor_tensor(same[:], rawsum[:], rawsum[:], ALU.is_equal))
            dve.wait_ge(mean_ready, 1)
            dve.tensor_scalar(mean[:].rearrange("p h b -> p (h b)"), fp[:, 0:2 * B], 1.0 / S, None,
                              ALU.mult).then_inc(ok_ready, 1)
            dve.tensor_reduce(ok[:], same[:], AXX, ALU.min).then_inc(ok_ready, 1)
            dve.wait_ge(okT_ready, 1)
            dve.tensor_reduce(ok1[:], fp[0:1, 0:P], AXX, ALU.min).then_inc(ok_ready, 1)
            dve.wait_ge(okb_ready, 1)
            link(dve.tensor_scalar(bad[:], fp[:, 256:257], 0.0, None, ALU.is_equal))
            for c in range(4):
                for h in range(2):
                    b4 = slice(c * B // 4, (c + 1) * B // 4)
                    dve.copy_predicated(oT[:, h, N // 4 * c:N // 4 * c + N // 4].rearrange("p (b q) -> p b q", q=L),
                                        bad[:].unsqueeze(2).to_broadcast([P, B // 4, L]),
                                        mean[:, h, b4].unsqueeze(2).to_broadcast([P, B // 4, L])).then_inc(guarded, 1)
            for s in range(NS):
                dve.wait_ge(xo_ready, s + 1)
                x1 = xs[:, 2 * s:2 * s + 2, :]
                dve.tensor_tensor(x1, xo[:, s % 2], x1, ALU.add).then_inc(xo_free, 1)
                if s:
                    dve.wait_ge(xo_free, s)
                    for t in (2 * s - 2, 2 * s - 1):
                        dve.bn_stats(stats[:, t, :], xs[:, t, :]).then_inc(step, 1)
            dve.wait_ge(xo_free, NS)
            for t in (T - 2, T - 1):
                dve.bn_stats(stats[:, t, :], xs[:, t, :]).then_inc(step, 1)
            link = Link(dve, step, link.n + T)
            dve.wait_ge(step, link.base)

            def aggregate(n):
                for t in range(T):
                    ins = dve.bn_aggr(mv[:, t, :], stats[:, t, :])
                    if t < T - 1:
                        link.n += 1
                        ins.then_inc(step, 1)
                link(ins)
                link(dve.tensor_scalar(ve[:], mv[:, :, 1], EPS, None, ALU.add))
                dve.sem_inc(var_ready, 1)
                dve.wait_ge(sqrt_ready, n)
                refine(dve, link, ve[:], rt[:], rs[:], tmp[:])

            aggregate(1)
            for t in range(T):
                dve.tensor_scalar(xin[:, t, :], xs[:, t, :], mv[:, t, 0:1], rs[:, t:t + 1],
                                  ALU.subtract, ALU.mult).then_inc(xin_ready, 1)
            for t in range(T):
                dve.wait_ge(xin_ready, t + 1)
                dve.bn_stats(stats[:, t, :], xin[:, t, :]).then_inc(step, 1)
                link.n += 1
            dve.wait_ge(step, link.base + link.n)
            aggregate(2)
            for s in range(NS):
                for t in range(2):
                    if s >= 2:
                        dve.wait_ge(tp_ready, s - 1)
                    dve.tensor_scalar(xh[:, s % 2, t, :], xin[:, 2 * s + t, :], mv[:, 2 * s + t, 0:1],
                                      rs[:, 2 * s + t:2 * s + t + 1], ALU.subtract, ALU.mult).then_inc(xh_ready, 1)

        @block.scalar
        def _(act):
            act.wait_ge(loaded, 16 * NLOAD)
            for s in range(NS):
                act.wait_ge(guarded, s // 2 * 2 + 2)
                if s >= 2:
                    act.wait_ge(xo_ready, s - 1)
                for k in range(2):
                    act.activation(ost[:, s % 2, k, :], oT[:, k, V2 * s:V2 * s + V2], ACT.Identity,
                                   bias=bv[:, k:k + 1]).then_inc(ost_ready, 1)
            for n in range(2):
                act.wait_ge(var_ready, n + 1)
                act.activation(rt[:], ve[:], ACT.Sqrt).then_inc(sqrt_ready, 1)
            act.sem_inc(nT_stored, 4)
            with act.Fori(0, NS // 2) as i:
                for j in range(2):
                    s = i * 2 + j
                    act.wait_ge(tp_ready, s + 1)
                    for k in range(2):
                        act.activation(nT[:, k, bass.ds(s * V2, V2)], tp[:, j, k, :], ACT.Identity,
                                       bias=b1[:, k:k + 1], scale=g1[:, k:k + 1]).then_inc(nT_stored, 1)


def state_space_weights(io, m):
    w = Early(m, "sw_")
    for name, shape in (("cw", [P, 2, 4]), ("cb", [P, 2])):
        w.add(name, shape, (whole, io[name]))
    w.add("br", [P, 2], (whole, io["br"].partition_broadcast(P)))
    w.add("Wgr", [P, 2, D + 2], (lambda t: t[:, :, 0:D], by_rows(io["Wgate"])),
          (lambda t: t[:, :, D:D + 2], by_rows(io["Wr"])))
    for name, n in (("Wzx", 2 * D), ("Wos", D)):
        w.add(name, [P, 2, n], (whole, by_rows(io[name])))
    return w


def state_space_phase(nc, w, nT, ssm, sg, r_all, load_early):
    with ExitStack() as st:
        p = Mem(nc, st)
        wzx, wgr, wos, cw, cb, br = [w[n] for n in ("Wzx", "Wgr", "Wos", "cw", "cb", "br")]
        nS = p.sb("ss_nS", [P, 2, 2, V2])
        sz = p.sb("ss_sz", [P, 2, V2])
        xp = p.sb("ss_xp", [P, 2, BS, L + 3])
        y = p.sb("ss_y", [P, 2, V2])
        sy = p.sb("ss_sy", [P, 2, V2])
        yz = p.sb("ss_yz", [P, 2, V2])
        gT = p.sb("ss_gT", [P, 2, 2, V2])
        zb = p.ps("ss_zb", [P, 2, V2])
        xb = p.ps("ss_xb", [P, 2, V2])
        gb = p.ps("ss_gb", [P, 2, 512])
        ob = p.ps("ss_ob", [P, 2, D])
        pad_ready = p.sem("ss_pad_ready")
        nS_ready = p.sem("ss_nS_ready")
        z_ready = p.sem("ss_z_ready")
        x_ready = p.sem("ss_x_ready")
        g_ready = p.sem("ss_g_ready")
        o_ready = p.sem("ss_o_ready")
        z_stored = p.sem("ss_z_stored")
        x_stored = p.sem("ss_x_stored")
        g_stored = p.sem("ss_g_stored")
        r_stored = p.sem("ss_r_stored")
        o_stored = p.sem("ss_o_stored")
        conv = p.sem("ss_conv")
        sy_ready = p.sem("ss_sy_ready")
        yz_ready = p.sem("ss_yz_ready")
        gT_ready = p.sem("ss_gT_ready")
        block = st.enter_context(nc.Block())
        def steps(eng, step):
            for s in range(2):
                step(s, s)
            with eng.Fori(1, NS // 2) as i:
                for j in range(2):
                    step(i * 2 + j, j)

        @block.sync
        def _(sp):
            load_early(sp)

        @block.tensor
        def _(pe):
            pe.wait_ge(w.loaded, w.total)

            def output(s, par):
                pe.wait_ge(gT_ready, s + 1)
                pe.wait_ge(o_stored, s)
                for t in range(2):
                    for k in range(2):
                        mm = pe.matmul(ob[:, t, :], gT[:, par, k, P * t:P * t + P], wos[:, k, :],
                                       start=(k == 0), stop=(k == 1))
                mm.then_inc(o_ready, 1)

            def step(s, par):
                src = [nT[:, k, bass.ds(s * V2, V2)] for k in range(2)]
                for bank, o, ready, stored in ((xb, 0, x_ready, x_stored), (zb, D, z_ready, z_stored)):
                    pe.wait_ge(stored, s)
                    for h in range(2):
                        for k in range(2):
                            mm = pe.matmul(bank[:, h, :], wzx[:, k, o + P * h:o + P * h + P], src[k],
                                           start=(k == 0), stop=(k == 1))
                    mm.then_inc(ready, 1)
                pe.wait_ge(nS_ready, s + 1)
                pe.wait_ge(g_stored, s)
                pe.wait_ge(r_stored, s)
                for t in range(2):
                    for k in range(2):
                        lhs = nS[:, par, k, P * t:P * t + P]
                        mm = pe.matmul(gb[:, t, 0:D + 2], lhs, wgr[:, k, :], start=(k == 0), stop=(k == 1))
                mm.then_inc(g_ready, 1)
                if not isinstance(s, int) or s >= 1:
                    output(s - 1, 1 - par)

            steps(pe, step)
            output(NS - 1, 1)

        @block.gpsimd
        def _(pool):
            def step(s, par):
                if not isinstance(s, int) or s >= 2:
                    pool.wait_ge(g_ready, s - 1)
                pool.tensor_copy(nS[:, par], nT[:, :, bass.ds(s * V2, V2)]).then_inc(nS_ready, 1)
                pool.wait_ge(sy_ready, s + 1)
                pool.wait_ge(z_stored, s + 1)
                pool.wait_ge(gT_ready, s)
                pool.tensor_tensor(yz[:], y[:], sz[:], ALU.mult).then_inc(yz_ready, 1)
                pool.wait_ge(yz_ready, s + 1)
                if not isinstance(s, int) or s >= 2:
                    pool.wait_ge(o_ready, s - 1)
                pool.tensor_tensor(gT[:, par], yz[:], sy[:], ALU.mult).then_inc(gT_ready, 1)

            pool.memset(xp[:, :, :, 0:3], 0.0).then_inc(pad_ready, 1)
            steps(pool, step)

        @block.scalar
        def _(act):
            act.wait_ge(w.loaded, w.total)

            def step(s, par):
                act.wait_ge(x_ready, s + 1)
                act.wait_ge(conv, s * 8)
                act.activation(xp[:, :, :, 3:], xb[:].rearrange("p h (b q) -> p h b q", q=L), ACT.Copy).then_inc(x_stored, 1)
                act.wait_ge(z_ready, s + 1)
                act.wait_ge(gT_ready, s)
                act.activation(sz[:], zb[:], ACT.Sigmoid).then_inc(z_stored, 1)
                act.wait_ge(conv, s * 8 + 8)
                act.activation(sy[:], y[:], ACT.Sigmoid).then_inc(sy_ready, 1)
                act.wait_ge(g_ready, s + 1)
                act.activation(sg[:, bass.ds(s * 2, 2), :], gb[:, :, 0:D], ACT.Sigmoid).then_inc(g_stored, 1)

            steps(act, step)

        @block.vector
        def _(dve):
            dve.wait_ge(w.loaded, w.total)
            dve.wait_ge(pad_ready, 1)

            def output(s):
                dve.wait_ge(o_ready, s + 1)
                dve.tensor_copy(ssm[:, bass.ds(s * 2, 2), :], ob[:]).then_inc(o_stored, 1)

            def step(s, par):
                dve.wait_ge(x_stored, s + 1)
                dve.wait_ge(gT_ready, s)
                yv = y[:].rearrange("p h (b q) -> p h b q", q=L)
                for n in range(4):
                    for h in range(2):
                        src, tap = xp[:, h, :, 3 - n:3 - n + L], cw[:, h, 3 - n:4 - n]
                        if n == 0:
                            ins = dve.tensor_scalar(yv[:, h], src, tap, cb[:, h:h + 1], ALU.mult, ALU.add)
                        else:
                            dve.wait_ge(conv, s * 8 + (2 * n - 1 + h))
                            ins = dve.scalar_tensor_tensor(out=yv[:, h], in0=src, scalar=tap, in1=yv[:, h],
                                                           op0=ALU.mult, op1=ALU.add)
                        ins.then_inc(conv, 1)
                dve.wait_ge(g_stored, s + 1)
                dve.tensor_tensor(r_all[:, bass.ds(s * 2, 2), :], gb[:, :, D:D + 2],
                                  br[:].unsqueeze(1).to_broadcast([P, 2, 2]),
                                  ALU.add).then_inc(r_stored, 1)
                if not isinstance(s, int) or s >= 1:
                    output(s - 1)

            steps(dve, step)
            output(NS - 1)


def self_attention_weights(io, m):
    w = Early(m, "aw_")
    for name, shape in (("c_ident", [P, P]), ("c_istack", [P, L]), ("c_mask8", [P, 8]), ("c_mask64", [P, 64]),
                        ("c_mask4", [P, 4])):
        w.add(name, shape, (whole, io[name]))
    w.add("ls1", [P, D], (whole, io["ls1"].partition_broadcast(P)))
    for name, n in (("Wqk2", 2 * D), ("Wv2", D), ("Wout2", D)):
        w.add(name, [P, 2, n], (whole, by_rows(io[name])))
    return w


def self_attention_phase(nc, w, nT, ssm, sg, r_all, alpha, xb, stats):
    with ExitStack() as st:
        p = Mem(nc, st, clear=True)
        ident, istack, mask8, mask64, mask4 = [w["c_" + n] for n in ("ident", "istack", "mask8", "mask64", "mask4")]
        wqk, wv, wout, ls1 = [w[n] for n in ("Wqk2", "Wv2", "Wout2", "ls1")]
        nS = p.sb("sa_nS", [P, 2, P])
        qkT = p.sb("sa_qkT", [P, 2, 4, P])
        qbd = p.sb("sa_qbd", [P, 2, 4, G, P])
        vbd = p.sb("sa_vbd", [P, G, 4, 64])
        mx = p.sb("sa_mx", [P, G * 4])
        es = p.sb("sa_es", [P, G * 4, L])
        sm = p.sb("sa_sm", [P, G * 4])
        ri = p.sb("sa_ri", [P, G * 4])
        pT = p.sb("sa_pT", [P, G, P])
        om = p.sb("sa_om", [P, 4, G, 64])
        oT = p.sb("sa_oT", [P, 2, P])
        qkb = p.ps("sa_qkb", [P, 4, P])
        vb = p.ps("sa_vb", [P, 512])
        sb_ = p.ps("sa_sb", [P, G * 4 * L])
        pb = p.ps("sa_pb", [P, G, P])
        pv = p.ps("sa_pv", [P, G, 4, 64])
        otb = p.ps("sa_otb", [P, 4, P])
        outb = p.ps("sa_outb", [P, 512])
        names = ("nS_ready qk_ready v_ready s_ready pt_ready pv_ready ot_ready out_ready qk_stored q_ready "
                 "v_stored mx_ready es_ready exp_ready sm_ready ri_ready p_ready pT_stored om_ready oT_stored "
                 "a1_ready a2_ready a3_ready a4_ready xb_ready stats_ready alpha_ready")
        S_ = {n: p.sem("sa_" + n) for n in names.split()}
        (nS_ready, qk_ready, v_ready, s_ready, pt_ready, pv_ready, ot_ready, out_ready, qk_stored, q_ready,
         v_stored, mx_ready, es_ready, exp_ready, sm_ready, ri_ready, p_ready, pT_stored, om_ready, oT_stored,
         a1_ready, a2_ready, a3_ready, a4_ready, xb_ready, stats_ready, alpha_ready) = S_.values()
        block = st.enter_context(nc.Block())
        def tiles(eng, step):
            for t in range(-1, 3):
                step(t, t % 2)
            with eng.Fori(1, T // 2 - 1) as i:
                for j in (1, 2):
                    step(i * 2 + j, j % 2)
            for t in range(T - 1, T + 2):
                step(t, t % 2)

        def there(t, back):
            return not isinstance(t, int) or 0 <= t - back < T

        @block.tensor
        def _(pe):
            pe.wait_ge(w.loaded, w.total)

            def step(t, par):
                if there(t, -1):
                    if there(t, 0):
                        pe.wait_ge(qk_stored, t + 1)
                    for c in range(4):
                        for k in range(2):
                            mm = pe.matmul(qkb[:, c, :], wqk[:, k, P * c:P * c + P],
                                           nT[:, k, bass.ds((t + 1) * P, P)], start=(k == 0), stop=(k == 1))
                    mm.then_inc(qk_ready, 1)
                if there(t, 1):
                    pe.wait_ge(p_ready, t)
                    pe.wait_ge(pT_stored, t - 1)
                    for g in range(G):
                        mm = pe.transpose(pb[:, g, :], es[:, 4 * g:4 * g + 4, :].rearrange("p b k -> p (b k)"), ident[:])
                    mm.then_inc(pt_ready, 1)
                if there(t, 0):
                    pe.wait_ge(es_ready, t)
                    pe.wait_ge(q_ready, t * 4 + 4)
                    for g in range(G):
                        for b in range(4):
                            n = L if b == 3 else 2 * L
                            mm = pe.matmul(sb_[:, L * (4 * g + b):L * (4 * g + b) + n], qbd[:, par, b, g, :],
                                           qkT[:, par, 2 + g // 2, L * b:L * b + n], start=True, stop=True)
                    mm.then_inc(s_ready, 1)
                if there(t, 2):
                    pe.wait_ge(om_ready, t - 1)
                    pe.wait_ge(oT_stored, t - 2)
                    for b in range(4):
                        for h in range(2):
                            mm = pe.matmul(otb[:, h, L * b:L * b + L],
                                           om[:, b, 2 * h:2 * h + 2, :].rearrange("p g c -> p (g c)"), istack[:],
                                           start=True, stop=True)
                    mm.then_inc(ot_ready, 1)
                if there(t, 1):
                    pe.wait_ge(pT_stored, t)
                    pe.wait_ge(v_stored, t)
                    pe.wait_ge(om_ready, t - 1)
                    for g in range(G):
                        mm = pe.matmul(pv[:, g, :, :].rearrange("p b c -> p (b c)"), pT[:, g, :],
                                       vbd[:, g, :, :].rearrange("p b c -> p (b c)"), start=True, stop=True)
                    mm.then_inc(pv_ready, 1)
                if there(t, 2):
                    pe.wait_ge(oT_stored, t - 1)
                    pe.wait_ge(a1_ready, t - 2)
                    for k in range(2):
                        mm = pe.matmul(outb[:, 0:D], oT[:, k, :], wout[:, k, :], start=(k == 0), stop=(k == 1))
                    mm.then_inc(out_ready, 1)
                if there(t, 0):
                    pe.wait_ge(nS_ready, t + 1)
                    pe.wait_ge(v_stored, t)
                    for k in range(2):
                        mm = pe.matmul(vb[:, 0:D], nS[:, k, :], wv[:, k, :], start=(k == 0), stop=(k == 1))
                    mm.then_inc(v_ready, 1)

            tiles(pe, step)

        @block.gpsimd
        def _(pool):
            pool.wait_ge(w.loaded, w.total)

            def step(t, par):
                if there(t, -1):
                    pool.wait_ge(qk_stored, t + 2)
                    if there(t, 0):
                        pool.wait_ge(s_ready, t)
                    for b in range(4):
                        src = qkT[:, 1 - par, 0:2, L * b:L * b + L].unsqueeze(2).to_broadcast([P, 2, 8, L])
                        msk = mask8[:].unsqueeze(1).unsqueeze(3).to_broadcast([P, 2, 8, L])
                        pool.tensor_tensor(qbd[:, 1 - par, b].rearrange("p (h j) (e q) -> p h (j e) q", h=2, q=L),
                                           src, msk, ALU.mult).then_inc(q_ready, 1)
                if there(t, 0):
                    pool.wait_ge(ri_ready, t + 1)
                    pool.tensor_tensor(es[:], es[:], ri[:].unsqueeze(2).to_broadcast([P, G * 4, L]),
                                       ALU.mult).then_inc(p_ready, 1)
                if there(t, 2):
                    c = t - 2
                    pool.wait_ge(a3_ready, c + 1)
                    mix = ssm[:, bass.ds(c, 1), :].rearrange("p t c -> p (t c)")
                    pool.tensor_tensor(mix, mix, ls1[:], ALU.mult).then_inc(a4_ready, 1)
                    pool.wait_ge(a4_ready, c + 1)
                    x = xb[:, bass.ds(c, 1), :].rearrange("p t c -> p (t c)")
                    pool.tensor_tensor(x, mix, x, ALU.add).then_inc(xb_ready, 1)

            tiles(pool, step)

        @block.scalar
        def _(act):
            act.activation(alpha[:], r_all[:, :, 0], ACT.Sigmoid).then_inc(alpha_ready, 1)
            act.wait_ge(alpha_ready, 1)

            def step(t, par):
                if there(t, 0):
                    act.wait_ge(v_ready, t)
                    act.activation(nS[:], nT[:, :, bass.ds(t * P, P)], ACT.Copy).then_inc(nS_ready, 1)
                if there(t, -1):
                    act.wait_ge(qk_ready, t + 2)
                    if there(t, 0):
                        act.wait_ge(s_ready, t)
                    act.activation(qkT[:, 1 - par], qkb[:], ACT.Copy).then_inc(qk_stored, 1)
                if there(t, 1):
                    act.wait_ge(pt_ready, t)
                    act.wait_ge(pv_ready, t - 1)
                    act.activation(pT[:], pb[:], ACT.Copy).then_inc(pT_stored, 1)
                if there(t, 0):
                    act.wait_ge(es_ready, t + 1)
                    act.activation(es[:], es[:], ACT.Exp, scale=SCALE).then_inc(exp_ready, 1)

            tiles(act, step)

        @block.vector
        def _(dve):
            dve.wait_ge(w.loaded, w.total)
            dve.wait_ge(alpha_ready, 1)

            def measure(c):
                dve.wait_ge(xb_ready, c + 1)
                dve.bn_stats(stats[:, bass.ds(c, 1), :].rearrange("p t c -> p (t c)"),
                             xb[:, bass.ds(c, 1), :].rearrange("p t c -> p (t c)")).then_inc(stats_ready, 1)

            def step(t, par):
                if there(t, 0):
                    dve.wait_ge(s_ready, t + 1)
                    scores = sb_[:].rearrange("p (g k) -> p g k", k=L)
                    dve.tensor_reduce(mx[:], scores, AXX, ALU.max).then_inc(mx_ready, 1)
                    dve.wait_ge(mx_ready, t + 1)
                    dve.wait_ge(pt_ready, t)
                    dve.tensor_tensor(es[:], scores, mx[:].unsqueeze(2).to_broadcast([P, G * 4, L]),
                                      ALU.subtract).then_inc(es_ready, 1)
                if there(t, 2):
                    dve.wait_ge(ot_ready, t - 1)
                    dve.wait_ge(out_ready, t - 2)
                    dve.tensor_copy(oT[:], otb[:, 0:2, :]).then_inc(oT_stored, 1)
                if there(t, 0):
                    dve.wait_ge(exp_ready, t + 1)
                    dve.tensor_reduce(sm[:], es[:], AXX, ALU.add).then_inc(sm_ready, 1)
                    dve.wait_ge(sm_ready, t + 1)
                    dve.wait_ge(p_ready, t)
                    dve.reciprocal(ri[:], sm[:]).then_inc(ri_ready, 1)
                if there(t, 1):
                    dve.wait_ge(pv_ready, t)
                    dve.wait_ge(ot_ready, t - 1)
                    dve.tensor_tensor(om[:].rearrange("p b g c -> p g b c"), pv[:],
                                      mask64[:].unsqueeze(1).unsqueeze(1).to_broadcast([P, G, 4, 64]),
                                      ALU.mult).then_inc(om_ready, 1)
                if there(t, 2):
                    c = t - 2
                    row = [a[:, bass.ds(c, 1), :].rearrange("p t c -> p (t c)") for a in (sg, ssm)]
                    dve.wait_ge(out_ready, c + 1)
                    dve.tensor_tensor(row[0], outb[:, 0:D], row[0], ALU.mult).then_inc(a1_ready, 1)
                    dve.wait_ge(a1_ready, c + 1)
                    dve.tensor_tensor(row[0], row[0], row[1], ALU.subtract).then_inc(a2_ready, 1)
                    dve.wait_ge(a2_ready, c + 1)
                    dve.scalar_tensor_tensor(out=row[1], in0=row[0], scalar=alpha[:, bass.ds(c, 1)], in1=row[1],
                                             op0=ALU.mult, op1=ALU.add).then_inc(a3_ready, 1)
                if there(t, 0):
                    dve.wait_ge(v_ready, t + 1)
                    dve.wait_ge(pv_ready, t)
                    dve.tensor_tensor(vbd[:], vb[:, 0:D].rearrange("p (g c) -> p g c", g=G).unsqueeze(2)
                                      .to_broadcast([P, G, 4, 64]),
                                      mask4[:].unsqueeze(1).unsqueeze(3).to_broadcast([P, G, 4, 64]),
                                      ALU.mult).then_inc(v_stored, 1)
                if there(t, 3):
                    measure(t - 3)

            tiles(dve, step)
            measure(T - 1)



E = 8
F1 = 512
F2 = 1024
CAP = 2 * N // E
J1 = 39
J2 = 2 * N // P
GA = 4
EMPTY = 4 * N
BF16 = mybir.dt.bfloat16


def normed_router_phase(nc, io, pre, src, rows, rows_written, lg, wr, gain, bias, b_router, load_early, load_later,
                        stats):
    with ExitStack() as st:
        p = Mem(nc, st)
        ident = p.sb(pre + "ident", [P, P])
        w = p.sb(pre + "w", [P, 2, E])
        gb = p.sb(pre + "gb", [P, 2, 2])
        brt = p.sb(pre + "brt", [P, E])
        mv = p.sb(pre + "mv", [P, T, 2])
        ve = p.sb(pre + "ve", [P, T])
        rt = p.sb(pre + "rt", [P, T])
        rs = p.sb(pre + "rs", [P, T])
        tmp = p.sb(pre + "tmp", [P, T])
        xh = p.sb(pre + "xh", [P, 4, 2, D])
        xT = p.sb(pre + "xT", [P, 2, 2, V2])
        tp = p.ps(pre + "tp", [P, 2, 2, V2])
        lp = p.ps(pre + "lp", [P, 2, 512])
        loaded = p.sem(pre + "loaded")
        step = p.sem(pre + "step")
        var_ready = p.sem(pre + "var_ready")
        sqrt_ready = p.sem(pre + "sqrt_ready")
        xh_ready = p.sem(pre + "xh_ready")
        tp_ready = p.sem(pre + "tp_ready")
        xT_ready = p.sem(pre + "xT_ready")
        lp_ready = p.sem(pre + "lp_ready")
        lg_ready = p.sem(pre + "lg_ready")
        block = st.enter_context(nc.Block())
        loads = [(ident[:], io["c_ident"]), (w[:], io[wr].rearrange("(k p) m -> p k m", p=P)),
                 (brt[:], io[b_router].partition_broadcast(P)), (gb[:, 0, :], io[gain]), (gb[:, 1, :], io[bias])]
        NLOAD = 16 * len(loads)

        @block.sync
        def _(sp):
            for d, s in loads:
                sp.dma_start(d, s).then_inc(loaded, 16)
            load_early(sp)
            for s in range(NS):
                sp.wait_ge(xh_ready, 2 * s + 2)
                sp.dma_start(rows.rearrange("(t p) d -> p t d", p=P)[:, 2 * s:2 * s + 2, :],
                             xh[:, s % 4]).then_inc(rows_written[s % 4], 16)
            load_later(sp)
            for i in range(4):
                sp.wait_ge(rows_written[i], 16 * NS // 4)

        @block.vector
        def _(dve):
            for t in range(T):
                dve.bn_aggr(mv[:, t, :], stats[:, t, :]).then_inc(step, 1)
            dve.wait_ge(step, T)
            dve.tensor_scalar(ve[:], mv[:, :, 1], EPS, None, ALU.add).then_inc(var_ready, 1)
            dve.wait_ge(sqrt_ready, 1)
            link = Link(dve, step, T)
            refine(dve, link, ve[:], rt[:], rs[:], tmp[:])
            dve.wait_ge(loaded, NLOAD)

            def logits(s):
                dve.wait_ge(lp_ready, s + 1)
                dve.tensor_tensor(lg[:, 2 * s:2 * s + 2, :], lp[:, s % 2, 0:2 * E].rearrange("p (t e) -> p t e", t=2),
                                  brt[:].unsqueeze(1).to_broadcast([P, 2, E]), ALU.add).then_inc(lg_ready, 1)

            for s in range(NS):
                if s >= 4:
                    dve.wait_ge(tp_ready, s - 3)
                    dve.wait_ge(rows_written[s % 4], 16 * (s // 4))
                for t in range(2):
                    dve.tensor_scalar(xh[:, s % 4, t, :], src[:, 2 * s + t, :], mv[:, 2 * s + t, 0:1],
                                      rs[:, 2 * s + t:2 * s + t + 1], ALU.subtract, ALU.mult).then_inc(xh_ready, 1)
                if s >= 2:
                    logits(s - 2)
            logits(NS - 2)
            logits(NS - 1)

        @block.scalar
        def _(act):
            act.wait_ge(var_ready, 1)
            act.activation(rt[:], ve[:], ACT.Sqrt).then_inc(sqrt_ready, 1)
            act.wait_ge(loaded, NLOAD)
            for s in range(NS):
                act.wait_ge(tp_ready, s + 1)
                if s >= 2:
                    act.wait_ge(lp_ready, s - 1)
                for k in range(2):
                    act.activation(xT[:, s % 2, k, :], tp[:, s % 2, k, :], ACT.Identity,
                                   bias=gb[:, 1, k:k + 1], scale=gb[:, 0, k:k + 1]).then_inc(xT_ready, 1)

        @block.tensor
        def _(pe):
            pe.wait_ge(loaded, NLOAD)

            def products(s):
                pe.wait_ge(xT_ready, 2 * s + 2)
                if s >= 2:
                    pe.wait_ge(lg_ready, s - 1)
                for t in range(2):
                    for k in range(2):
                        mm = pe.matmul(lp[:, s % 2, E * t:E * t + E], xT[:, s % 2, k, P * t:P * t + P], w[:, k, :],
                                       start=(k == 0), stop=(k == 1))
                mm.then_inc(lp_ready, 1)

            for s in range(NS):
                pe.wait_ge(xh_ready, 2 * s + 2)
                if s >= 2:
                    pe.wait_ge(xT_ready, 2 * s - 2)
                for k in range(2):
                    for t in range(2):
                        mm = pe.transpose(tp[:, s % 2, k, P * t:P * t + P], xh[:, s % 4, t, P * k:P * k + P], ident[:])
                mm.then_inc(tp_ready, 1)
                if s >= 1:
                    products(s - 1)
            products(NS - 1)


def route_constants(io, m, pre):
    w = Early(m, pre)
    for name, n in (("tri", P), ("ones", P), ("reset", P), ("iota", E), ("steps", T), ("tiles", 40), ("first", E),
                    ("starts", 41), ("low", P), ("p1", 1), ("copies", 2 * T)):
        w.add(name, [P, n], (whole, io["c_" + name]))
    return w


def route_phase(nc, pre, w, lg, weight, te, source, target, capped):
    J = J2 if capped else J1
    with ExitStack() as st:
        p = Mem(nc, st)

        def sb(name, shape, dt=F32):
            return p.sb(pre + name, shape, dt)

        tri, ones, reset, iota, first = [w[n] for n in ("tri", "ones", "reset", "iota", "first")]
        steps, tiles, starts, lows, p1, copies = [w[n] for n in ("steps", "tiles", "starts", "low", "p1", "copies")]
        mx, z, rz = sb("mx", [P, T]), sb("z", [P, T]), sb("rz", [P, T])
        v = sb("v", [P, T, E])
        top = sb("top", [P, T, 8])
        ix = sb("ix", [P, T, 8], U32)
        ixf = sb("ixf", [P, T, 8])
        sel = sb("sel", [P, 3, T, E])
        tot, incl, rank = sb("tot", [P, E, T]), sb("incl", [P, E, T]), sb("rank", [P, E, T])
        keep = sb("keep", [P, E, T])
        nt, tb, tx = sb("nt", [P, E]), sb("tb", [P, E]), sb("tx", [P, E])
        ge = sb("ge", [1, J1, E])
        tef = sb("tef", [1, J1])
        sf = sb("sf", [P, 2, T])
        t1, t2 = sb("t1", [P, T]), sb("t2", [P, T])
        begun = sb("begun", [P, 2 * T, J + 1])
        count, low = sb("count", [P, 2 * T]), sb("low", [P, 2 * T])
        in_tile = sb("in_tile", [P, 2 * T, J])
        at_slot = sb("at_slot", [P, 2 * T, P], BF16)
        values = sb("values", [P, 2 * T, 2, J], BF16)
        row, empty, second = sb("row", [P, J]), sb("empty", [P, J]), sb("second", [P, J])
        pb = p.ps(pre + "pb", [P, 2, P])
        inv = p.ps(pre + "inv", [P, 2, J])
        values_ready = p.sem(pre + "values_ready")
        at_ready = p.sem(pre + "at_ready")
        inv_ready = p.sem(pre + "inv_ready")
        step = p.sem(pre + "step")
        exp_in = p.sem(pre + "exp_in")
        exp_out = p.sem(pre + "exp_out")
        sel_ready = p.sem(pre + "sel_ready")
        rank_ready = p.sem(pre + "rank_ready")
        block = st.enter_context(nc.Block())
        @block.scalar
        def _(act):
            act.wait_ge(exp_in, 1)
            if capped:
                act.activation(z[:], z[:], ACT.Exp).then_inc(exp_out, 1)
            else:
                act.activation(v[:], v[:], ACT.Exp).then_inc(exp_out, 1)

        @block.tensor
        def _(pe):
            pe.wait_ge(w.loaded, w.total)
            pe.wait_ge(sel_ready, 1)
            both = sel[:, 2].rearrange("p t e -> p e t")
            pe.matmul(pb[:, 0, :], tri[:], both, start=True, stop=True)
            pe.matmul(pb[:, 1, :], ones[:], both, start=True, stop=True).then_inc(rank_ready, 1)
            pe.wait_ge(values_ready, 1)
            for m in range(2 * T):
                if m % (T // 2) == 0:
                    pe.wait_ge(at_ready, m // (T // 2) + 1)
                mm = pe.matmul(inv[:].rearrange("p a j -> p (a j)"), at_slot[:, m, :],
                               values[:, m].rearrange("p a j -> p (a j)"), start=(m == 0), stop=(m == 2 * T - 1))
            mm.then_inc(inv_ready, 1)

        @block.vector
        def _(dve):
            link = Link(dve, step)
            dve.wait_ge(w.loaded, w.total)

            def along(a):
                return a.unsqueeze(2).to_broadcast([P, T, E])

            src = lg
            if not capped:
                link(dve.tensor_reduce(mx[:], lg[:], AXX, ALU.max))
                dve.tensor_tensor(v[:], lg[:], along(mx[:]), ALU.subtract).then_inc(exp_in, 1)
                dve.wait_ge(exp_out, 1)
                link(dve.tensor_reduce(z[:], v[:], AXX, ALU.add))
                link(dve.reciprocal(rz[:], z[:]))
                link(dve.tensor_tensor(v[:], v[:], along(rz[:]), ALU.mult))
                src = v
            for t in range(T):
                dve.max(top[:, t, :], src[:, t, :]).then_inc(step, 1)
                link.n += 1
            dve.wait_ge(step, link.n)
            for t in range(T):
                dve.max_index(ix[:, t, :], top[:, t, :], src[:, t, :]).then_inc(step, 1)
                link.n += 1
            dve.wait_ge(step, link.n)
            link(dve.tensor_copy(ixf[:], ix[:]))
            for c in range(2):
                link(dve.tensor_tensor(sel[:, c], iota[:].unsqueeze(1).to_broadcast([P, T, E]), along(ixf[:, :, c]),
                                       ALU.is_equal))
            dve.tensor_tensor(sel[:, 2], sel[:, 0], sel[:, 1], ALU.add).then_inc(sel_ready, 1)
            if capped:
                dve.tensor_tensor(z[:], top[:, :, 1], top[:, :, 0], ALU.subtract).then_inc(exp_in, 1)
                dve.wait_ge(exp_out, 1)
                link(dve.tensor_scalar(t1[:], z[:], 1.0, None, ALU.add))
                link(dve.reciprocal(weight[:, 0, :], t1[:]))
                link(dve.tensor_tensor(weight[:, 1, :], z[:], weight[:, 0, :], ALU.mult))
            else:
                link(dve.tensor_tensor(t1[:], top[:, :, 0], top[:, :, 1], ALU.add))
                link(dve.tensor_scalar(t2[:], t1[:], 1e-8, None, ALU.add))
                link(dve.reciprocal(t1[:], t2[:]))
                for c in range(2):
                    link(dve.tensor_tensor(weight[:, c, :], top[:, :, c], t1[:], ALU.mult))
            dve.wait_ge(rank_ready, 1)
            link(dve.tensor_copy(tot[:].rearrange("p e t -> p (e t)"), pb[:, 1, :]))
            link(dve.tensor_tensor_scan(out=incl[:].rearrange("p e t -> p (e t)"), data0=reset[:],
                                        data1=tot[:].rearrange("p e t -> p (e t)"), initial=0.0,
                                        op0=ALU.mult, op1=ALU.add))
            link(dve.tensor_tensor(rank[:], incl[:], tot[:], ALU.subtract))
            link(dve.tensor_tensor(rank[:].rearrange("p e t -> p (e t)"), pb[:, 0, :],
                                   rank[:].rearrange("p e t -> p (e t)"), ALU.add))
            base = first
            if capped:
                link(dve.tensor_scalar(keep[:], rank[:], float(CAP), None, ALU.is_lt))
            else:
                link(dve.tensor_tensor(keep[:], incl[:, :, T - 1:T].to_broadcast([P, E, T]),
                                       steps[:].unsqueeze(1).to_broadcast([P, E, T]), ALU.is_gt))
                link(dve.tensor_reduce(nt[:], keep[:], AXX, ALU.add))
                link(dve.tensor_tensor_scan(out=tb[:], data0=ones[:, 0:E], data1=nt[:], initial=0.0,
                                            op0=ALU.mult, op1=ALU.add))
                link(dve.tensor_tensor(tx[:], tb[:], nt[:], ALU.subtract))
                link(dve.tensor_scalar(tx[:], tx[:], float(P), None, ALU.mult))
                base = tx
                link(dve.tensor_tensor(ge[:], tiles[0:1, 0:J1].unsqueeze(2).to_broadcast([1, J1, E]),
                                       tb[0:1, :].unsqueeze(1).to_broadcast([1, J1, E]), ALU.is_ge))
                link(dve.tensor_reduce(tef[:], ge[:], AXX, ALU.add))
                link(dve.tensor_scalar(te[:], tef[:], float(E - 1), None, ALU.min))
            link(dve.tensor_tensor(rank[:], rank[:], base[:].unsqueeze(2).to_broadcast([P, E, T]), ALU.add))
            if capped:
                link(dve.tensor_scalar(rank[:], rank[:], -2.0 * N, None, ALU.add))
                link(dve.tensor_tensor(rank[:], rank[:], keep[:], ALU.mult))
                link(dve.tensor_scalar(rank[:], rank[:], 2.0 * N, None, ALU.add))
            for c in range(2):
                link(dve.tensor_tensor(v[:], sel[:, c], rank[:].rearrange("p e t -> p t e"), ALU.mult))
                link(dve.tensor_reduce(sf[:, c, :], v[:], AXX, ALU.add))
            slot = sf[:].rearrange("p c t -> p (c t)")
            link(dve.tensor_tensor(begun[:], slot.unsqueeze(2).to_broadcast([P, 2 * T, J + 1]),
                                   starts[:, 0:J + 1].unsqueeze(1).to_broadcast([P, 2 * T, J + 1]), ALU.is_ge))
            link(dve.tensor_reduce(count[:], begun[:], AXX, ALU.add))
            link(dve.scalar_tensor_tensor(out=low[:], in0=count[:], scalar=-float(P), in1=slot, op0=ALU.mult, op1=ALU.add))
            link(dve.tensor_tensor(in_tile[:], begun[:, :, 0:J], begun[:, :, 1:J + 1], ALU.subtract))
            link(dve.tensor_scalar(values[:, :, 0, :], in_tile[:], p1[:, 0:1], None, ALU.mult))
            dve.tensor_tensor(values[:, :, 1, :], in_tile[:], copies[:].unsqueeze(2).to_broadcast([P, 2 * T, J]),
                              ALU.mult).then_inc(values_ready, 1)
            for c in range(4):
                part = slice(T // 2 * c, T // 2 * c + T // 2)
                dve.tensor_tensor(at_slot[:, part], lows[:].unsqueeze(1).to_broadcast([P, T // 2, P]),
                                  low[:, part].unsqueeze(2).to_broadcast([P, T // 2, P]), ALU.is_equal).then_inc(at_ready, 1)
            dve.wait_ge(inv_ready, 1)
            link(dve.tensor_copy(second[:], inv[:, 1, :]))
            link(dve.scalar_tensor_tensor(out=row[:], in0=second[:], scalar=float(P), in1=inv[:, 0, :], op0=ALU.mult, op1=ALU.add))
            link(dve.tensor_scalar(empty[:], inv[:, 0, :], 0.0, EMPTY + 1.0, ALU.is_equal, ALU.mult))
            link(dve.scalar_tensor_tensor(out=empty[:], in0=row[:], scalar=-1.0, in1=empty[:], op0=ALU.add, op1=ALU.add))
            link(dve.tensor_copy(target[:], empty[:]))
            link(dve.tensor_scalar(second[:], second[:], float(T), -float(N), ALU.is_ge, ALU.mult))
            link(dve.scalar_tensor_tensor(out=row[:], in0=row[:], scalar=-1.0, in1=second[:], op0=ALU.add, op1=ALU.add))
            link(dve.tensor_scalar(row[:], row[:], 0.0, None, ALU.max))
            link(dve.tensor_copy(source[:], row[:]))


def gather_rows(pool, out, rows, index):
    return pool.indirect_dma_start(out=out, out_offset=None, in_=rows,
                                   in_offset=bass.IndirectOffsetOnAxis(ap=index, axis=0))


def scatter_rows(pool, out, index, rows):
    return pool.indirect_dma_start(out=out, out_offset=bass.IndirectOffsetOnAxis(ap=index, axis=0), in_=rows,
                                   in_offset=None, bounds_check=2 * N - 1, oob_is_err=False)


def first_experts_phase(nc, io, rows, yg, source, target, te, w13, w2, w_loaded, base, xs, base_loaded):
    with ExitStack() as st:
        p = Mem(nc, st)
        ident = p.sb("e1_ident", [P, P])
        gb = p.sb("e1_gb", [P, 2, 2])
        x = p.sb("e1_x", [P, 2, D])
        xT = p.sb("e1_xT", [P, 2, 2, P])
        s = p.sb("e1_s", [P, F1])
        h = p.sb("e1_h", [P, F1])
        hT = p.sb("e1_hT", [P, 4, P])
        y = p.sb("e1_y", [P, 2, D])
        tb = p.ps("e1_tb", [P, 2, P])
        ab = p.ps("e1_ab", [P, F1])
        bb = p.ps("e1_bb", [P, F1])
        hb = p.ps("e1_hb", [P, 4, P])
        yb = p.ps("e1_yb", [P, D])
        loaded = p.sem("e1_loaded")
        x_loaded = [p.sem(f"e1_x_loaded{i}") for i in range(2)]
        y_written = [p.sem(f"e1_y_written{i}") for i in range(2)]
        t_ready = p.sem("e1_t_ready")
        xT_ready = p.sem("e1_xT_ready")
        a_ready = p.sem("e1_a_ready")
        b_ready = p.sem("e1_b_ready")
        s_ready = p.sem("e1_s_ready")
        h_ready = p.sem("e1_h_ready")
        hb_ready = p.sem("e1_hb_ready")
        hT_ready = p.sem("e1_hT_ready")
        yb_ready = p.sem("e1_yb_ready")
        y_ready = p.sem("e1_y_ready")
        block = st.enter_context(nc.Block())

        def tiles(eng, step, lag=0):
            for j in range(4):
                step(j, j % 2)
            with eng.Fori(2, J1 // 2 - 1) as i:
                for j in range(2):
                    step(i * 2 + j, j)
            for j in range(2 * (J1 // 2 - 1), J1 + lag):
                step(j, j % 2)

        def there(j, back):
            return not isinstance(j, int) or 0 <= j - back < J1

        @block.sync
        def _(sp):
            sp.dma_start(ident[:], io["c_ident"]).then_inc(loaded, 16)
            sp.dma_start(gb[:, 0, :], io["g2"]).then_inc(loaded, 16)
            sp.dma_start(gb[:, 1, :], io["b2"]).then_inc(loaded, 16)
            sp.dma_start(xs[:], base).then_inc(base_loaded, 16)
            sp.wait_ge(base_loaded, 16)

        @block.gpsimd
        def _(pool):
            for j in range(2):
                gather_rows(pool, x[:, j, :], rows, source[:, j:j + 1]).then_inc(x_loaded[j], 16)
            for j in range(J1 + 1):
                if j + 2 < J1:
                    pool.wait_ge(t_ready, j + 1)
                    gather_rows(pool, x[:, j % 2, :], rows, source[:, j + 2:j + 3]).then_inc(x_loaded[j % 2], 16)
                if j >= 1:
                    pool.wait_ge(y_ready, j)
                    scatter_rows(pool, yg, target[:, j - 1:j], y[:, (j - 1) % 2, :]).then_inc(y_written[(j - 1) % 2], 16)
            pool.wait_ge(y_written[0], 16 * ((J1 + 1) // 2))
            pool.wait_ge(y_written[1], 16 * (J1 // 2))

        @block.tensor
        def _(pe):
            pe.wait_ge(loaded, 48)
            pe.wait_ge(*w_loaded)

            def loads_of(j, par):
                return 16 * (j // 2 + 1) if isinstance(j, int) else j * 8 + (16 if par == 0 else 8)

            def turn_x(j, par):
                pe.wait_ge(x_loaded[par], loads_of(j, par))
                pe.wait_ge(xT_ready, j * 2)
                for k in range(2):
                    mm = pe.transpose(tb[:, k, :], x[:, par, P * k:P * k + P], ident[:])
                mm.then_inc(t_ready, 1)

            def step(j, par):
                if there(j, 0):
                    e = pe.value_load(te[0:1, bass.ds(j, 1)], min_val=0, max_val=E - 1)
                    pe.wait_ge(xT_ready, j * 2 + 2)
                    pe.wait_ge(s_ready, j)
                    for k in range(2):
                        mm = pe.matmul(ab[:], xT[:, par, k, :], w13[:, bass.ds(e * 4 + k, 1), :].rearrange("p a f -> p (a f)"),
                                       start=(k == 0), stop=(k == 1))
                    mm.then_inc(a_ready, 1)
                if there(j, 1):
                    pe.wait_ge(h_ready, j)
                    pe.wait_ge(hT_ready, j - 1)
                    for f in range(4):
                        mm = pe.transpose(hb[:, f, :], h[:, P * f:P * f + P], ident[:])
                    mm.then_inc(hb_ready, 1)
                if there(j, 0):
                    pe.wait_ge(h_ready, j)
                    for k in range(2):
                        mm = pe.matmul(bb[:], xT[:, par, k, :], w13[:, bass.ds(e * 4 + (2 + k), 1), :].rearrange("p a f -> p (a f)"),
                                       start=(k == 0), stop=(k == 1))
                    mm.then_inc(b_ready, 1)
                if there(j, -1):
                    turn_x(j + 1, 1 - par)
                if there(j, 1):
                    d = pe.value_load(te[0:1, bass.ds(j - 1, 1)], min_val=0, max_val=E - 1)
                    pe.wait_ge(hT_ready, j)
                    pe.wait_ge(y_ready, j - 1)
                    for f in range(4):
                        mm = pe.matmul(yb[:], hT[:, f, :], w2[:, bass.ds(d * 4 + f, 1), :].rearrange("p a c -> p (a c)"),
                                       start=(f == 0), stop=(f == 3))
                    mm.then_inc(yb_ready, 1)

            turn_x(0, 0)
            tiles(pe, step, 1)

        @block.scalar
        def _(act):
            act.wait_ge(loaded, 48)

            def turn_x(j, par):
                act.wait_ge(t_ready, j + 1)
                if not isinstance(j, int) or j >= 2:
                    act.wait_ge(b_ready, j - 1)
                for k in range(2):
                    act.activation(xT[:, par, k, :], tb[:, k, :], ACT.Identity,
                                   bias=gb[:, 1, k:k + 1], scale=gb[:, 0, k:k + 1]).then_inc(xT_ready, 1)

            def step(j, par):
                if there(j, 0):
                    act.wait_ge(a_ready, j + 1)
                    act.wait_ge(h_ready, j)
                    act.activation(s[:], ab[:], ACT.Silu).then_inc(s_ready, 1)
                if there(j, -1):
                    turn_x(j + 1, 1 - par)
                if there(j, 1):
                    act.wait_ge(yb_ready, j)
                    if not isinstance(j, int) or j >= 3:
                        act.wait_ge(y_written[1 - par], (j - 1) // 2 * 16 if isinstance(j, int) else j * 8 - (16 if par == 0 else 8))
                    act.activation(y[:, 1 - par, :], yb[:], ACT.Copy).then_inc(y_ready, 1)

            turn_x(0, 0)
            tiles(act, step, 1)

        @block.vector
        def _(dve):
            def step(j, par):
                if there(j, 1):
                    dve.wait_ge(hb_ready, j)
                    dve.wait_ge(yb_ready, j - 1)
                    dve.tensor_copy(hT[:], hb[:]).then_inc(hT_ready, 1)
                if there(j, 0):
                    dve.wait_ge(s_ready, j + 1)
                    dve.wait_ge(b_ready, j + 1)
                    dve.wait_ge(hb_ready, j)
                    dve.tensor_tensor(h[:], bb[:], s[:], ALU.mult).then_inc(h_ready, 1)

            tiles(dve, step, 1)


def first_combine_phase(nc, io, yg, weight, r_all, xb, x2, stats):
    with ExitStack() as st:
        p = Mem(nc, st)
        ls2 = p.sb("c1_ls2", [P, D])
        sb_ = p.sb("c1_sb", [P, 3])
        y = p.sb("c1_y", [P, GA, 2, D])
        c1 = p.sb("c1_c1", [P, 2, D])
        c2 = p.sb("c1_c2", [P, 2, D])
        c3 = p.sb("c1_c3", [P, 2, D])
        c4 = p.sb("c1_c4", [P, 2, D])
        halt = p.sb("c1_halt", [P, 2, T])
        rem = p.sb("c1_rem", [P, 2, T])
        w1 = p.sb("c1_w1", [P, T])
        ws = p.sb("c1_ws", [P, 2, T])
        loaded = p.sem("c1_loaded")
        halt_ready = p.sem("c1_halt_ready")
        y_loaded = [p.sem(f"c1_y_loaded{i}") for i in range(GA)]
        c1_ready = p.sem("c1_c1_ready")
        c2_ready = p.sem("c1_c2_ready")
        c3_ready = p.sem("c1_c3_ready")
        c4_ready = p.sem("c1_c4_ready")
        x2_ready = p.sem("c1_x2_ready")
        stats_ready = p.sem("c1_stats_ready")
        step = p.sem("c1_step")
        block = st.enter_context(nc.Block())

        @block.sync
        def _(sp):
            sp.dma_start(ls2[:], io["ls2"].partition_broadcast(P)).then_inc(loaded, 16)
            sp.dma_start(sb_[:], io["step_bias"].partition_broadcast(P)).then_inc(loaded, 16)
            for t in range(T):
                if t >= GA:
                    sp.wait_ge(c2_ready, t - GA + 1)
                sp.dma_start(y[:, t % GA], yg.rearrange("(c t p) d -> p c t d", p=P, c=2)[:, :, t, :]
                             ).then_inc(y_loaded[t % GA], 16)

        @block.gpsimd
        def _(pool):
            pool.wait_ge(loaded, 32)
            for t in range(T):
                j = t % 2
                pool.wait_ge(c2_ready, t + 1)
                if t >= 2:
                    pool.wait_ge(c4_ready, t - 1)
                pool.tensor_tensor(c3[:, j, :], c2[:, j, :], ls2[:], ALU.mult).then_inc(c3_ready, 1)
                pool.wait_ge(c3_ready, t + 1)
                if t >= 2:
                    pool.wait_ge(x2_ready, t - 1)
                pool.tensor_tensor(c4[:, j, :], c3[:, j, :], xb[:, t, :], ALU.add).then_inc(c4_ready, 1)

        @block.scalar
        def _(act):
            act.wait_ge(loaded, 32)
            for s in range(2):
                act.activation(halt[:, s, :], r_all[:, :, 1], ACT.Sigmoid, bias=sb_[:, s:s + 1]).then_inc(halt_ready, 1)
            for t in range(T):
                act.wait_ge(y_loaded[t % GA], 16 * (t // GA + 1))
                if t >= 2:
                    act.wait_ge(c2_ready, t - 1)
                act.activation(c1[:, t % 2, :], y[:, t % GA, 0, :], ACT.Copy, scale=weight[:, 0, t:t + 1]).then_inc(c1_ready, 1)

        @block.vector
        def _(dve):
            link = Link(dve, step)
            dve.wait_ge(halt_ready, 2)
            link(dve.tensor_scalar(rem[:, 0, :], halt[:, 0, :], -1.0, 1.0, ALU.mult, ALU.add))
            link(dve.tensor_scalar(rem[:, 0, :], rem[:, 0, :], 0.0, None, ALU.max))
            link(dve.tensor_tensor(w1[:], halt[:, 1, :], rem[:, 0, :], ALU.mult))
            link(dve.tensor_tensor(rem[:, 1, :], rem[:, 0, :], w1[:], ALU.subtract))
            link(dve.tensor_scalar(rem[:, 1, :], rem[:, 1, :], 0.0, None, ALU.max))
            link(dve.tensor_tensor(ws[:, 0, :], halt[:, 0, :], w1[:], ALU.add))
            link(dve.tensor_tensor(ws[:, 1, :], ws[:, 0, :], rem[:, 1, :], ALU.add))

            def finish(t):
                dve.wait_ge(c4_ready, t + 1)
                dve.scalar_tensor_tensor(out=x2[:, t, :], in0=c4[:, t % 2, :], scalar=ws[:, 1, t:t + 1],
                                         in1=x2[:, t, :], op0=ALU.mult, op1=ALU.add).then_inc(x2_ready, 1)

            def measure(t):
                dve.wait_ge(x2_ready, t + 1)
                dve.bn_stats(stats[:, t, :], x2[:, t, :]).then_inc(stats_ready, 1)

            for t in range(T):
                dve.wait_ge(c1_ready, t + 1)
                if t >= 2:
                    dve.wait_ge(c3_ready, t - 1)
                dve.scalar_tensor_tensor(out=c2[:, t % 2, :], in0=y[:, t % GA, 1, :], scalar=weight[:, 1, t:t + 1],
                                         in1=c1[:, t % 2, :], op0=ALU.mult, op1=ALU.add).then_inc(c2_ready, 1)
                if t >= 1:
                    finish(t - 1)
                if t >= 2:
                    measure(t - 2)
            finish(T - 1)
            measure(T - 2)
            measure(T - 1)


def load_second_experts(sp, io, w, w_loaded, e, par):
    w1, w2 = w
    sp.dma_start(w1[:, par], io["F_W1"][bass.ds(e, 1), :, :].rearrange("a (k p) f -> p (a k) f", p=P)).then_inc(w_loaded[par], 16)
    sp.dma_start(w2[:, par], io["F_W2"][bass.ds(e, 1), :, :].rearrange("a (k p) d -> p (a k) d", p=P)).then_inc(w_loaded[par], 16)


def second_experts_phase(nc, io, rows, yg, zeroed, source, target, w, w_loaded):
    ST = CAP // P
    M = F2 // P
    w1, w2 = w
    with ExitStack() as st:
        p = Mem(nc, st)
        ident = p.sb("e2_ident", [P, P])
        b1 = p.sb("e2_b1", [P, E, M])
        b2 = p.sb("e2_b2", [P, 2, D])
        w1s = p.sb("e2_w1s", [P, 2, 2, F2], F32R)
        w2s = p.sb("e2_w2s", [P, 2, M, D], F32R)
        x = p.sb("e2_x", [P, 2, ST, D])
        xTs = p.sb("e2_xTs", [P, 2, 2, CAP], F32R)
        h = p.sb("e2_h", [P, 2, CAP])
        hTs = p.sb("e2_hTs", [P, 2, M, CAP], F32R)
        y = p.sb("e2_y", [P, 2, ST, D])
        tb = p.ps("e2_tb", [P, 2, CAP])
        hb = p.ps("e2_hb", [P, 2, CAP])
        yb = p.ps("e2_yb", [P, 2, 512])
        loaded = p.sem("e2_loaded")
        b_loaded = [p.sem(f"e2_b_loaded{i}") for i in range(2)]
        x_loaded = [p.sem(f"e2_x_loaded{i}") for i in range(2)]
        y_written = [p.sem(f"e2_y_written{i}") for i in range(2)]
        t_ready = p.sem("e2_t_ready")
        xh_ready = p.sem("e2_xh_ready")
        xl_ready = p.sem("e2_xl_ready")
        w1h_ready = p.sem("e2_w1h_ready")
        w1l_ready = p.sem("e2_w1l_ready")
        w2h_ready = p.sem("e2_w2h_ready")
        w2l_ready = p.sem("e2_w2l_ready")
        hb_ready = p.sem("e2_hb_ready")
        h_ready = p.sem("e2_h_ready")
        hh_ready = p.sem("e2_hh_ready")
        hl_ready = p.sem("e2_hl_ready")
        yb_ready = p.sem("e2_yb_ready")
        y_ready = p.sem("e2_y_ready")
        block = st.enter_context(nc.Block())

        def experts(eng, step):
            for e in range(2):
                step(e, e)
            with eng.Fori(1, E // 2 - 1) as i:
                for j in range(2):
                    step(i * 2 + j, j)
            for e in range(E - 2, E):
                step(e, e % 2)

        def static(e):
            return isinstance(e, int)

        def uses(e, par, each):
            return each * (e // 2 + 1) if static(e) else e * (each // 2) + (each if par == 0 else each // 2)

        @block.sync
        def _(sp):
            sp.dma_start(ident[:], io["c_ident"]).then_inc(loaded, 16)
            sp.dma_start(b1[:], io["F_b1"]).then_inc(loaded, 16)

            def load(e, par):
                sp.dma_start(b2[:, par, :], io["F_b2"][bass.ds(e, 1), :].partition_broadcast(P).rearrange("p a d -> p (a d)")).then_inc(b_loaded[par], 16)

            for e in range(2):
                load(e, e)

            def step(e, par):
                if not static(e) or e + 2 < E:
                    sp.wait_ge(w2l_ready, e * 2 + 2)
                    sp.wait_ge(w2h_ready, e * 2 + 2)
                    load_second_experts(sp, io, w, w_loaded, e + 2, par)
                if not static(e) or e + 2 < E:
                    sp.wait_ge(y_ready, e * ST + ST)
                    load(e + 2, par)

            experts(sp, step)

        PARTS = ((0, 0), (0, 1), (1, 0))

        @block.tensor
        def _(pe):
            pe.wait_ge(loaded, 32)

            def turn_x(e, par):
                pe.wait_ge(x_loaded[par], uses(e, par, 16 * ST))
                for k in range(2):
                    if not (static(e) and e == 0):
                        pe.wait_ge(xl_ready, e * 2)
                    for s in range(ST):
                        mm = pe.transpose(tb[:, k, P * s:P * s + P], x[:, par, s, P * k:P * k + P], ident[:])
                    mm.then_inc(t_ready, 1)

            def step(e, par):
                pe.wait_ge(xh_ready, e * 2 + 2)
                pe.wait_ge(xl_ready, e * 2 + 2)
                pe.wait_ge(w1h_ready, e * 2 + 2)
                pe.wait_ge(w1l_ready, e * 2 + 2)
                for f in range(M):
                    if f >= 2:
                        pe.wait_ge(h_ready, e * M + (f - 1))
                    elif not (static(e) and e == 0):
                        pe.wait_ge(h_ready, e * M)
                    n = 0
                    for k in range(2):
                        for a, b in PARTS:
                            mm = pe.matmul(hb[:, f % 2, :], w1s[:, a, k, P * f:P * f + P], xTs[:, b, k, :],
                                           start=(n == 0), stop=(n == 5))
                            n += 1
                    mm.then_inc(hb_ready, 1)
                if not static(e) or e + 1 < E:
                    turn_x(e + 1, 1 - par)
                pe.wait_ge(w2h_ready, e * 2 + 2)
                pe.wait_ge(w2l_ready, e * 2 + 2)
                for s in range(ST):
                    if not (static(e) and e == 0 and s < 2):
                        pe.wait_ge(y_ready, e * ST + (s - 1))
                    for f in range(M):
                        if s == 0:
                            pe.wait_ge(hh_ready, e * M + (f + 1))
                            pe.wait_ge(hl_ready, e * M + (f + 1))
                        for a, b in PARTS:
                            mm = pe.matmul(yb[:, s % 2, 0:D], hTs[:, a, f, P * s:P * s + P], w2s[:, b, f, :],
                                           start=(f == 0 and (a, b) == (0, 0)), stop=(f == M - 1 and a == 1))
                    mm.then_inc(yb_ready, 1)

            turn_x(0, 0)
            experts(pe, step)

        @block.scalar
        def _(act):
            act.wait_ge(loaded, 32)

            def high_w1(e, par):
                act.wait_ge(w_loaded[par], uses(e, par, 32))
                if not (static(e) and e == 0):
                    act.wait_ge(hb_ready, e * M)
                for k in range(2):
                    act.activation(w1s[:, 0, k, :], w1[:, par, k, :], ACT.Copy).then_inc(w1h_ready, 1)

            def step(e, par):
                for f in range(M):
                    act.wait_ge(hb_ready, e * M + (f + 1))
                    if not (static(e) and e == 0 and f < 2):
                        act.wait_ge(hh_ready, e * M + (f - 1))
                        act.wait_ge(hl_ready, e * M + (f - 1))
                    act.activation(h[:, f % 2, :], hb[:, f % 2, :], ACT.Gelu,
                                   bias=b1[:, bass.ds(e, 1), f:f + 1].rearrange("p a b -> p (a b)")).then_inc(h_ready, 1)
                    if f in (1, 3):
                        if not (static(e) and e == 0):
                            act.wait_ge(yb_ready, e * ST)
                        m = slice(M // 2 * (f // 2), M // 2 * (f // 2) + M // 2)
                        act.activation(w2s[:, 0, m, :], w2[:, par, m, :], ACT.Copy).then_inc(w2h_ready, 1)
                if not static(e) or e + 1 < E:
                    high_w1(e + 1, 1 - par)

            high_w1(0, 0)
            experts(act, step)

        @block.gpsimd
        def _(pool):
            def gather(e, par):
                for s in range(ST):
                    i = e * ST + s
                    gather_rows(pool, x[:, par, s, :], rows, source[:, i:i + 1]).then_inc(x_loaded[par], 16)

            def scatter(e, par):
                for s in range(ST):
                    i = e * ST + s
                    pool.wait_ge(y_ready, i + 1)
                    scatter_rows(pool, yg, target[:, i:i + 1], y[:, par, s, :]).then_inc(y_written[par], 16)

            def rest_w1(e, par):
                for k in range(2):
                    pool.wait_ge(w1h_ready, e * 2 + (k + 1))
                    pool.tensor_tensor(w1s[:, 1, k, :], w1[:, par, k, :], w1s[:, 0, k, :], ALU.subtract).then_inc(w1l_ready, 1)

            def step(e, par):
                for c in range(2):
                    m = slice(M // 2 * c, M // 2 * c + M // 2)
                    pool.wait_ge(w2h_ready, e * 2 + (c + 1))
                    pool.tensor_tensor(w2s[:, 1, m, :], w2[:, par, m, :], w2s[:, 0, m, :], ALU.subtract).then_inc(w2l_ready, 1)
                if e >= 1:
                    scatter(e - 1, 1 - par)
                if e + 1 < E:
                    rest_w1(e + 1, 1 - par)
                if e + 2 < E:
                    pool.wait_ge(t_ready, e * 2 + 2)
                    gather(e + 2, par)

            for e in range(2):
                gather(e, e)
            rest_w1(0, 0)
            pool.wait_ge(*zeroed)
            for e in range(E):
                step(e, e % 2)
            scatter(E - 1, 1)
            for c in range(2):
                pool.wait_ge(y_written[c], 16 * ST * E // 2)

        @block.vector
        def _(dve):
            def split_x(e, par):
                if not (static(e) and e == 0):
                    dve.wait_ge(hb_ready, e * M)
                for k in range(2):
                    dve.wait_ge(t_ready, e * 2 + (k + 1))
                    dve.tensor_copy(xTs[:, 0, k, :], tb[:, k, :]).then_inc(xh_ready, 1)
                for k in range(2):
                    dve.wait_ge(xh_ready, e * 2 + (k + 1))
                    dve.tensor_tensor(xTs[:, 1, k, :], tb[:, k, :], xTs[:, 0, k, :], ALU.subtract).then_inc(xl_ready, 1)

            def step(e, par):
                if not (static(e) and e == 0):
                    dve.wait_ge(yb_ready, e * ST)
                for f in range(M):
                    dve.wait_ge(h_ready, e * M + (f + 1))
                    dve.tensor_copy(hTs[:, 0, f, :], h[:, f % 2, :]).then_inc(hh_ready, 1)
                    dve.wait_ge(hh_ready, e * M + (f + 1))
                    dve.tensor_tensor(hTs[:, 1, f, :], h[:, f % 2, :], hTs[:, 0, f, :], ALU.subtract).then_inc(hl_ready, 1)
                if not static(e) or e + 1 < E:
                    split_x(e + 1, 1 - par)
                dve.wait_ge(b_loaded[par], uses(e, par, 16))
                if not (static(e) and e < 2):
                    dve.wait_ge(y_written[par], uses(e, par, 16 * ST) - 16 * ST)
                for s in range(ST):
                    dve.wait_ge(yb_ready, e * ST + (s + 1))
                    dve.tensor_tensor(y[:, par, s, :], yb[:, s % 2, 0:D], b2[:, par, :], ALU.add).then_inc(y_ready, 1)

            split_x(0, 0)
            experts(dve, step)


def output_phase(nc, io, yg, weight, x2):
    with ExitStack() as st:
        p = Mem(nc, st)
        y = p.sb("o_y", [P, GA, 2, D])
        c1 = p.sb("o_c1", [P, GA, D])
        res = p.sb("o_res", [P, GA, D])
        loaded = [p.sem(f"o_loaded{i}") for i in range(GA)]
        written = [p.sem(f"o_written{i}") for i in range(GA)]
        c1_ready = p.sem("o_c1_ready")
        res_ready = p.sem("o_res_ready")
        block = st.enter_context(nc.Block())
        out = io["out"].rearrange("(t p) d -> p t d", p=P)

        @block.scalar
        def _(act):
            for t in range(T):
                if t >= GA:
                    act.wait_ge(res_ready, t - GA + 1)
                act.dma_start(y[:, t % GA], yg.rearrange("(c t p) d -> p c t d", p=P, c=2)[:, :, t, :]
                              ).then_inc(loaded[t % GA], 16)

        @block.vector
        def _(dve):
            for t in range(T):
                g = t % GA
                dve.wait_ge(loaded[g], 16 * (t // GA + 1))
                dve.scalar_tensor_tensor(out=c1[:, g, :], in0=y[:, g, 0, :], scalar=weight[:, 0, t:t + 1],
                                         in1=x2[:, t, :], op0=ALU.mult, op1=ALU.add).then_inc(c1_ready, 1)
                dve.wait_ge(c1_ready, t + 1)
                if t >= GA:
                    dve.wait_ge(written[g], 16 * (t // GA))
                dve.scalar_tensor_tensor(out=res[:, g, :], in0=y[:, g, 1, :], scalar=weight[:, 1, t:t + 1],
                                         in1=c1[:, g, :], op0=ALU.mult, op1=ALU.add).then_inc(res_ready, 1)

        @block.sync
        def _(sp):
            for t in range(T):
                sp.wait_ge(res_ready, t + 1)
                sp.dma_start(out[:, t, :], res[:, t % GA, :]).then_inc(written[t % GA], 16)
            for g in range(GA):
                sp.wait_ge(written[g], 16 * (T // GA))


def build_program(nc, io):
    with ExitStack() as st:
        m = Mem(nc, st)
        rows1 = nc.dram_tensor("rows1", (N, D), F32, kind="Internal").ap()
        rows2 = nc.dram_tensor("rows2", (N, D), F32, kind="Internal").ap()
        yg1 = nc.dram_tensor("yg1", (2 * N, D), F32, kind="Internal").ap()
        yg2 = nc.dram_tensor("yg2", (2 * N, D), F32, kind="Internal").ap()
        base = nc.dram_tensor("base", (P, T, D), F32, kind="Internal").ap()
        zeroed = m.sem("zeroed")
        w_loaded = m.sem("w_loaded")
        base_written = m.sem("base_written")
        rows_written = [[m.sem(f"rows{k}_written{i}") for i in range(4)] for k in range(2)]
        base_loaded = m.sem("base_loaded")
        weight1 = m.sb("weight1", [P, 2, T])
        weight2 = m.sb("weight2", [P, 2, T])
        te = m.sb("te", [1, J1], I32)
        r_all = m.sb("r_all", [P, T, 2])
        alpha = m.sb("alpha", [P, T])
        stats = m.sb("stats", [P, T, 6])

        def zero_slots(sp, zero):
            z8 = zero[:].to_broadcast([P, 8, D])
            for i in range(J2 // 8):
                sp.dma_start(yg2[8 * P * i:8 * P * i + 8 * P, :].rearrange("(t p) d -> p t d", p=P),
                             z8).then_inc(zeroed, 16)

        NZ = 16 * (J2 // 8)
        xs = m.sb("xs", [P, T, D])
        with ExitStack() as s0:
            m0 = Mem(nc, s0)
            oT = m0.sb("oT", [P, 2, N])
            rawsum = m0.sb("rawsum", [P, B * G])
            csum = m0.sb("csum", [P, 2, B])
            with ExitStack() as s1:
                m1 = Mem(nc, s1)
                qs = m1.sb("qs", [P, 2, 2, N], F32R)
                xw = cross_attention_weights(io, m1)
                query_phase(nc, io, xs, qs, xw.load)
                cross_attention_phase(nc, io, xw, xs, qs, oT, rawsum, csum, zero_slots, (zeroed, NZ))
            nT = m0.sb("nT", [P, 2, N])
            xb = m0.sb("xb", [P, T, D])
            w13 = m0.sb("w13", [P, E * 4, F1])
            w2 = m0.sb("w2", [P, E * 4, D])

            def load_experts(sp):
                for e in range(E):
                    for c, name in enumerate(("W1", "W3")):
                        sp.dma_start(w13[:, 4 * e + 2 * c:4 * e + 2 * c + 2, :],
                                     io[name][e].rearrange("(k p) f -> p k f", p=P)).then_inc(w_loaded, 16)
                    sp.dma_start(w2[:, 4 * e:4 * e + 4, :],
                                 io["W2"][e].rearrange("(k p) d -> p k d", p=P)).then_inc(w_loaded, 16)

            ssm, sg = xs, oT[:].rearrange("p k (t c) -> p (k t) c", c=D)
            with ExitStack() as s2:
                m2 = Mem(nc, s2)
                aw = self_attention_weights(io, m2)
                with ExitStack() as s3:
                    sw = state_space_weights(io, Mem(nc, s3))
                    merge_phase(nc, io, oT, rawsum, csum, xs, xb, nT, base, base_written, sw.load)
                    state_space_phase(nc, sw, nT, ssm, sg, r_all, lambda sp: (aw.load(sp), load_experts(sp)))
                self_attention_phase(nc, aw, nT, ssm, sg, r_all, alpha, xb, stats)
            rw = route_constants(io, m0, "rw1_")
            lg = m0.sb("lg1", [P, T, E])
            source1, target1 = m0.sb("source1", [P, J1], I32), m0.sb("target1", [P, J1], I32)
            normed_router_phase(nc, io, "n1_", xb, rows1, rows_written[0], lg, "Wg", "g2", "b2", "zero8", rw.load,
                                lambda sp: None, stats)
            route_phase(nc, "r1_", rw, lg, weight1, te, source1, target1, False)
            first_experts_phase(nc, io, rows1, yg1, source1, target1, te, w13, w2, (w_loaded, 16 * 3 * E),
                                base, xs, base_loaded)
            first_combine_phase(nc, io, yg1, weight1, r_all, xb, xs, stats)
        x2 = xs
        lg = m.sb("lg2", [P, T, E])
        source2, target2 = m.sb("source2", [P, J2], I32), m.sb("target2", [P, J2], I32)
        e2w = m.sb("e2_w1", [P, 2, 2, F2]), m.sb("e2_w2", [P, 2, F2 // P, D])
        e2w_loaded = [m.sem(f"e2_w_loaded{i}") for i in range(2)]
        rw = route_constants(io, m, "rw2_")
        normed_router_phase(nc, io, "n2_", x2, rows2, rows_written[1], lg, "F_Wr", "one2", "zero2", "F_br", rw.load,
                            lambda sp: [load_second_experts(sp, io, e2w, e2w_loaded, e, e) for e in range(2)],
                            stats)
        route_phase(nc, "r2_", rw, lg, weight2, None, source2, target2, True)
        second_experts_phase(nc, io, rows2, yg2, (zeroed, NZ), source2, target2, e2w, e2w_loaded)
        output_phase(nc, io, yg2, weight2, x2)


def kernel(**inputs):
    import concourse.bacc as bacc
    from concourse.bass_utils import run_bass_kernel_spmd

    a = {k: np.ascontiguousarray(v) for k, v in inputs.items()}
    X, A, Fn = "L0_xattn_", "L0_attn_", "L0_ffn_"

    def by_partition(v):
        return np.ascontiguousarray(v.reshape(2, P).T)

    ctxT = np.ascontiguousarray(a["ctx_768"].transpose(2, 0, 1))
    arrays = {"x": a["x"].reshape(N, D), "ctxT": ctxT, "ctx_last": np.ascontiguousarray(ctxT[:, :, -1])}
    for k in ("Wq", "Wk", "Wv", "Wo", "bo"):
        arrays[k] = a[X + k]
    for k in ("bq", "bk", "bv"):
        arrays[k] = by_partition(a[X + k])
    for k, name in (("g1", "ln1_g"), ("b1", "ln1_b"), ("g2", "ln2_g"), ("b2", "ln2_b"), ("cb", "conv_b")):
        arrays[k] = by_partition(a[A + name])
    for k, name in (("Wzx", "Win_ssm"), ("Wgate", "Wgate"), ("Wr", "Wr"), ("br", "br"), ("Wos", "Wout_ssm"),
                    ("Wout2", "Wout"), ("ls1", "ls1"), ("ls2", "ls2"), ("step_bias", "step_bias"), ("Wg", "Wg"),
                    ("W1", "W1"), ("W2", "W2"), ("W3", "W3")):
        arrays[k] = a[A + name]
    arrays["cw"] = np.ascontiguousarray(a[A + "conv_w"].reshape(2, P, 4).transpose(1, 0, 2))
    arrays["Wqk2"] = np.ascontiguousarray(a[A + "Wqkv"][:, :2 * D])
    arrays["Wv2"] = np.ascontiguousarray(a[A + "Wqkv"][:, 2 * D:])
    for k, name in (("F_Wr", "Wr"), ("F_br", "br"), ("F_W1", "W1"), ("F_W2", "W2"), ("F_b2", "b2")):
        arrays[k] = a[Fn + name]
    arrays["F_b1"] = np.ascontiguousarray(a[Fn + "b1"].reshape(E, F2 // P, P).transpose(2, 0, 1))
    arrays.update(constants())

    nc = bacc.Bacc("TRN2", target_bir_lowering=False, num_devices=1)
    io = {}
    ins = {}
    for name, v in arrays.items():
        ins["in_" + name] = v
        io[name] = nc.dram_tensor("in_" + name, v.shape, mybir.dt.from_np(v.dtype), kind="ExternalInput").ap()
    io["out"] = nc.dram_tensor("out_x", (N, D), F32, kind="ExternalOutput").ap()
    build_program(nc, io)
    r = run_bass_kernel_spmd(nc, [ins], core_ids=[0])
    return r.results[0]["out_x"].reshape(B, L, D)
```
